# Optimizing a Trainium2 kernel written in Bass

```python
import numpy as np
import jax
import jax.numpy as jnp

def _softmax(x, axis=-1):
    return jax.nn.softmax(x, axis=axis)

def _gelu(x):
    return jax.nn.gelu(x, approximate=True)

def _silu(x):
    return jax.nn.silu(x)

def _sigmoid(x):
    return jax.nn.sigmoid(x)

def _layernorm(x, axis=-1, eps=1e-05):
    m = jnp.mean(x, axis=axis, keepdims=True)
    v = jnp.var(x, axis=axis, keepdims=True)
    return (x - m) / jnp.sqrt(v + eps)

def _scatter_add(tgt, idx, src, axis=0):
    return tgt.at[idx].add(src)

def _segment_sum(src, seg, n):
    return jax.ops.segment_sum(src, seg, n)
kernel_name = 'mk_gps_d2_gnn_r16_8a53b7'

def setup_inputs(seed: int=0):
    np.random.seed(seed)
    _w = jnp.asarray

    def _rec_inputs():
        import jax
        import jax.numpy as jnp
        _gk = jax.random.key(seed)
        x = -0.0001126 + 1 * jax.random.normal(jax.random.fold_in(_gk, 1), (625, 768), jnp.float32)
        src = jax.random.randint(jax.random.fold_in(_gk, 2), (20000,), 0, 625, jnp.int32)
        dst = jax.random.randint(jax.random.fold_in(_gk, 3), (20000,), 0, 625, jnp.int32)
        _o = jnp.argsort(dst, stable=True)
        src = src[_o]
        dst = dst[_o]
        return (x, src, dst)
    x, src, dst = _rec_inputs()

    def _L0_gnn_setup():
        import jax, jax.numpy as jnp
        import numpy as np
        N_NODES = 625
        D = 768
        N_EDGES = 10000

        def gcn_conv(x, W, b, src, dst, n_nodes):
            h = x @ W
            deg = jax.ops.segment_sum(jnp.ones_like(dst, dtype=h.dtype), dst, num_segments=n_nodes)
            dinv = jnp.where(deg > 0, jax.lax.rsqrt(deg), 0.0)
            norm = dinv[src] * dinv[dst]
            msgs = h[src] * norm[:, None]
            out = jax.ops.segment_sum(msgs, dst, num_segments=n_nodes)
            return out + b

        def add_self_loops(edge_index, n_nodes):
            loop = jnp.arange(n_nodes, dtype=edge_index.dtype)
            src = jnp.concatenate([edge_index[0], loop])
            dst = jnp.concatenate([edge_index[1], loop])
            return (src, dst)
        key = jax.random.key(seed)
        k1, k2, k3, k4 = jax.random.split(key, 4)
        x = jax.random.normal(k1, (N_NODES, D), dtype=jnp.float32)
        edge_index = jax.random.randint(k2, (2, N_EDGES), 0, N_NODES, dtype=jnp.int32)
        glorot = float(np.sqrt(6.0 / (D + D)))
        W1 = jax.random.uniform(k3, (D, D), jnp.float32, -glorot, glorot)
        W2 = jax.random.uniform(k4, (D, D), jnp.float32, -glorot, glorot)
        b1 = jnp.zeros((D,), jnp.float32)
        b2 = jnp.zeros((D,), jnp.float32)
        return {'x': x, 'W1': W1, 'b1': b1, 'W2': W2, 'b2': b2, 'edge_index': edge_index}
    _L0_gnn_all = _L0_gnn_setup()
    _L0_gnn_in = {k: v for k, v in _L0_gnn_all.items() if k in ('W1', 'b1', 'W2', 'b2')}
    del _L0_gnn_all

    def _L0_mix_setup():
        import jax, jax.numpy as jnp
        import numpy as np
        DIM = 768
        HEADS = 12
        DIM_HEAD = 64
        INNER = HEADS * DIM_HEAD
        EPS = 1e-05

        def _layernorm(t, gamma, beta):
            mu = jnp.mean(t, axis=-1, keepdims=True)
            var = jnp.var(t, axis=-1, keepdims=True)
            return (t - mu) * jax.lax.rsqrt(var + EPS) * gamma + beta
        key = jax.random.key(seed)
        ks = jax.random.split(key, 5)
        x = jax.random.normal(ks[0], (8, 256, DIM), dtype=jnp.float32)
        w_map = jax.random.normal(ks[1], (3 * INNER, DIM), dtype=jnp.float32) * (1.0 / np.sqrt(DIM))
        g_k = jnp.ones((DIM_HEAD,), dtype=jnp.float32)
        b_k = jnp.zeros((DIM_HEAD,), dtype=jnp.float32)
        g_v = jnp.ones((DIM_HEAD,), dtype=jnp.float32)
        b_v = jnp.zeros((DIM_HEAD,), dtype=jnp.float32)
        w_out = jax.random.normal(ks[2], (DIM, INNER), dtype=jnp.float32) * (1.0 / np.sqrt(INNER))
        b_out = jax.random.normal(ks[3], (DIM,), dtype=jnp.float32) * 0.01
        return {'x': x, 'w_map': w_map, 'g_k': g_k, 'b_k': b_k, 'g_v': g_v, 'b_v': b_v, 'w_out': w_out, 'b_out': b_out}
    _L0_mix_all = _L0_mix_setup()
    _L0_mix_in = {k: v for k, v in _L0_mix_all.items() if k in ('w_map', 'g_k', 'b_k', 'g_v', 'b_v', 'w_out', 'b_out')}
    del _L0_mix_all

    def _L0_ffn_setup():
        import jax, jax.numpy as jnp
        import numpy as np
        TOP_K = 2
        key = jax.random.key(seed)
        ks = jax.random.split(key, 5)
        B, S, D, H, E = (1, 128, 768, 192, 8)
        x = jax.random.normal(ks[0], (B, S, D), dtype=jnp.float32)
        gate_w = jax.random.normal(ks[1], (E, D), dtype=jnp.float32) * 0.02
        w1 = jax.random.normal(ks[2], (E, D, H), dtype=jnp.float32) * 0.02
        b1 = jnp.zeros((E, H), dtype=jnp.float32)
        w2 = jax.random.normal(ks[3], (E, H, D), dtype=jnp.float32) * 0.02
        b2 = jnp.zeros((E, D), dtype=jnp.float32)
        return {'x': x, 'gate_w': gate_w, 'w1': w1, 'b1': b1, 'w2': w2, 'b2': b2}
    _L0_ffn_all = _L0_ffn_setup()
    _L0_ffn_in = {k: v for k, v in _L0_ffn_all.items() if k in ('gate_w', 'w1', 'b1', 'w2', 'b2')}
    del _L0_ffn_all

    def _L1_gnn_setup():
        import jax, jax.numpy as jnp
        import numpy as np
        N_NODES = 625
        NEG_SLOPE = 0.2
        EPS = 1e-16

        def gat_layer(x, W, att_src, att_dst, bias, src, dst, heads, out_ch, concat):
            n = x.shape[0]
            h = (x @ W.T).reshape(n, heads, out_ch)
            a_src = jnp.einsum('nhc,hc->nh', h, att_src)
            a_dst = jnp.einsum('nhc,hc->nh', h, att_dst)
            e = a_src[src] + a_dst[dst]
            e = jax.nn.leaky_relu(e, NEG_SLOPE)
            m = jax.ops.segment_max(e, dst, num_segments=n)
            ex = jnp.exp(e - m[dst])
            denom = jax.ops.segment_sum(ex, dst, num_segments=n)
            alpha = ex / (denom[dst] + EPS)
            msg = alpha[:, :, None] * h[src]
            out = jax.ops.segment_sum(msg, dst, num_segments=n)
            if concat:
                out = out.reshape(n, heads * out_ch)
            else:
                out = out.mean(axis=1)
            return out + bias
        key = jax.random.key(seed)
        ks = jax.random.split(key, 12)
        x = jax.random.normal(ks[0], (N_NODES, 768), dtype=jnp.float32)
        edge_index = jax.random.randint(ks[1], (2, 10000), 0, N_NODES, dtype=jnp.int64)
        s1 = 1.0 / np.sqrt(768.0)
        W1 = jax.random.normal(ks[2], (8 * 128, 768), dtype=jnp.float32) * s1
        att_src1 = jax.random.normal(ks[3], (8, 128), dtype=jnp.float32) * (1.0 / np.sqrt(128.0))
        att_dst1 = jax.random.normal(ks[4], (8, 128), dtype=jnp.float32) * (1.0 / np.sqrt(128.0))
        b1 = jnp.zeros((8 * 128,), dtype=jnp.float32)
        s2 = 1.0 / np.sqrt(1024.0)
        W2 = jax.random.normal(ks[5], (1 * 768, 1024), dtype=jnp.float32) * s2
        att_src2 = jax.random.normal(ks[6], (1, 768), dtype=jnp.float32) * (1.0 / np.sqrt(768.0))
        att_dst2 = jax.random.normal(ks[7], (1, 768), dtype=jnp.float32) * (1.0 / np.sqrt(768.0))
        b2 = jnp.zeros((768,), dtype=jnp.float32)
        return {'x': x, 'edge_index': edge_index, 'W1': W1, 'att_src1': att_src1, 'att_dst1': att_dst1, 'b1': b1, 'W2': W2, 'att_src2': att_src2, 'att_dst2': att_dst2, 'b2': b2}
    _L1_gnn_all = _L1_gnn_setup()
    _L1_gnn_in = {k: v for k, v in _L1_gnn_all.items() if k in ('W1', 'att_src1', 'att_dst1', 'b1', 'W2', 'att_src2', 'att_dst2', 'b2')}
    del _L1_gnn_all

    def _L1_mix_setup():
        import jax, jax.numpy as jnp
        import numpy as np
        NUM_HEADS = 12

        def _reference_tuple_inner(x, w_qkv, w_proj, b_proj):
            B, N, C = x.shape
            H = NUM_HEADS
            D = C // H
            qkv = (x @ w_qkv).reshape(B, N, 3, H, D)
            q = jnp.transpose(qkv[:, :, 0], (0, 2, 1, 3))
            k = jnp.transpose(qkv[:, :, 1], (0, 2, 1, 3))
            v = jnp.transpose(qkv[:, :, 2], (0, 2, 1, 3))
            q = jax.nn.elu(q) + 1.0
            k = jax.nn.elu(k) + 1.0
            attn = jnp.einsum('bhnd,bhmd->bhnm', q, k)
            attn = attn / jnp.sum(attn, axis=-1, keepdims=True)
            out = jnp.einsum('bhnm,bhmd->bhnd', attn, v)
            out = jnp.transpose(out, (0, 2, 1, 3)).reshape(B, N, C)
            out = out @ w_proj + b_proj
            return (out, attn)
        key = jax.random.key(seed)
        k1, k2, k3 = jax.random.split(key, 3)
        B, N, C = (2, 128, 768)
        x = jax.random.normal(k1, (B, N, C), dtype=jnp.float32)
        w_qkv = jax.random.normal(k2, (C, 3 * C), dtype=jnp.float32) * 0.02
        w_proj = jax.random.normal(k3, (C, C), dtype=jnp.float32) * 0.02
        b_proj = jnp.zeros((C,), dtype=jnp.float32)
        return {'x': x, 'w_qkv': w_qkv, 'w_proj': w_proj, 'b_proj': b_proj}
    _L1_mix_all = _L1_mix_setup()
    _L1_mix_in = {k: v for k, v in _L1_mix_all.items() if k in ('w_qkv', 'w_proj', 'b_proj')}
    del _L1_mix_all

    def _L1_ffn_setup():
        import jax, jax.numpy as jnp
        import numpy as np
        B, S, D, E, K = (1, 1024, 768, 8, 2)
        H = 4 * D
        key = jax.random.key(seed)
        ks = jax.random.split(key, 6)
        s = jnp.float32(0.02)
        return {'x': jax.random.normal(ks[0], (B, S, D), jnp.float32), 'Wr': jax.random.normal(ks[1], (E, D), jnp.float32) * s, 'W1': jax.random.normal(ks[2], (E, H, D), jnp.float32) * s, 'b1': jnp.zeros((E, H), jnp.float32), 'W2': jax.random.normal(ks[3], (E, D, H), jnp.float32) * s, 'b2': jnp.zeros((E, D), jnp.float32), 'sW1': jax.random.normal(ks[4], (H, D), jnp.float32) * s, 'sb1': jnp.zeros((H,), jnp.float32), 'sW2': jax.random.normal(ks[5], (D, H), jnp.float32) * s, 'sb2': jnp.zeros((D,), jnp.float32)}
    _L1_ffn_all = _L1_ffn_setup()
    _L1_ffn_in = {k: v for k, v in _L1_ffn_all.items() if k in ('Wr', 'W1', 'b1', 'W2', 'b2', 'sW1', 'sb1', 'sW2', 'sb2')}
    del _L1_ffn_all
    return {'x': x, 'src': src, 'dst': dst, 'L0_gnn_W1': _L0_gnn_in['W1'], 'L0_gnn_b1': _L0_gnn_in['b1'], 'L0_gnn_W2': _L0_gnn_in['W2'], 'L0_gnn_b2': _L0_gnn_in['b2'], 'L0_mix_w_map': _L0_mix_in['w_map'], 'L0_mix_g_k': _L0_mix_in['g_k'], 'L0_mix_b_k': _L0_mix_in['b_k'], 'L0_mix_g_v': _L0_mix_in['g_v'], 'L0_mix_b_v': _L0_mix_in['b_v'], 'L0_mix_w_out': _L0_mix_in['w_out'], 'L0_mix_b_out': _L0_mix_in['b_out'], 'L0_ffn_gate_w': _L0_ffn_in['gate_w'], 'L0_ffn_w1': _L0_ffn_in['w1'], 'L0_ffn_b1': _L0_ffn_in['b1'], 'L0_ffn_w2': _L0_ffn_in['w2'], 'L0_ffn_b2': _L0_ffn_in['b2'], 'L1_gnn_W1': _L1_gnn_in['W1'], 'L1_gnn_att_src1': _L1_gnn_in['att_src1'], 'L1_gnn_att_dst1': _L1_gnn_in['att_dst1'], 'L1_gnn_b1': _L1_gnn_in['b1'], 'L1_gnn_W2': _L1_gnn_in['W2'], 'L1_gnn_att_src2': _L1_gnn_in['att_src2'], 'L1_gnn_att_dst2': _L1_gnn_in['att_dst2'], 'L1_gnn_b2': _L1_gnn_in['b2'], 'L1_mix_w_qkv': _L1_mix_in['w_qkv'], 'L1_mix_w_proj': _L1_mix_in['w_proj'], 'L1_mix_b_proj': _L1_mix_in['b_proj'], 'L1_ffn_Wr': _L1_ffn_in['Wr'], 'L1_ffn_W1': _L1_ffn_in['W1'], 'L1_ffn_b1': _L1_ffn_in['b1'], 'L1_ffn_W2': _L1_ffn_in['W2'], 'L1_ffn_b2': _L1_ffn_in['b2'], 'L1_ffn_sW1': _L1_ffn_in['sW1'], 'L1_ffn_sb1': _L1_ffn_in['sb1'], 'L1_ffn_sW2': _L1_ffn_in['sW2'], 'L1_ffn_sb2': _L1_ffn_in['sb2']}

def reference(x, src, dst, L0_gnn_W1, L0_gnn_b1, L0_gnn_W2, L0_gnn_b2, L0_mix_w_map, L0_mix_g_k, L0_mix_b_k, L0_mix_g_v, L0_mix_b_v, L0_mix_w_out, L0_mix_b_out, L0_ffn_gate_w, L0_ffn_w1, L0_ffn_b1, L0_ffn_w2, L0_ffn_b2, L1_gnn_W1, L1_gnn_att_src1, L1_gnn_att_dst1, L1_gnn_b1, L1_gnn_W2, L1_gnn_att_src2, L1_gnn_att_dst2, L1_gnn_b2, L1_mix_w_qkv, L1_mix_w_proj, L1_mix_b_proj, L1_ffn_Wr, L1_ffn_W1, L1_ffn_b1, L1_ffn_W2, L1_ffn_b2, L1_ffn_sW1, L1_ffn_sb1, L1_ffn_sW2, L1_ffn_sb2):
    import jax
    import jax.numpy as jnp

    def _L0_gnn_ref(x, W1, b1, W2, b2, edge_index):
        import jax, jax.numpy as jnp
        import numpy as np
        N_NODES = 625
        D = 768
        N_EDGES = 10000

        def gcn_conv(x, W, b, src, dst, n_nodes):
            h = x @ W
            deg = jax.ops.segment_sum(jnp.ones_like(dst, dtype=h.dtype), dst, num_segments=n_nodes)
            dinv = jnp.where(deg > 0, jax.lax.rsqrt(deg), 0.0)
            norm = dinv[src] * dinv[dst]
            msgs = h[src] * norm[:, None]
            out = jax.ops.segment_sum(msgs, dst, num_segments=n_nodes)
            return out + b

        def add_self_loops(edge_index, n_nodes):
            loop = jnp.arange(n_nodes, dtype=edge_index.dtype)
            src = jnp.concatenate([edge_index[0], loop])
            dst = jnp.concatenate([edge_index[1], loop])
            return (src, dst)
        n = x.shape[0]
        src, dst = add_self_loops(edge_index, n)
        h = gcn_conv(x, W1, b1, src, dst, n)
        h = jax.nn.relu(h)
        out = gcn_conv(h, W2, b2, src, dst, n)
        return out

    def _L0_mix_ref(x, w_map, g_k, b_k, g_v, b_v, w_out, b_out):
        import jax, jax.numpy as jnp
        import numpy as np
        DIM = 768
        HEADS = 12
        DIM_HEAD = 64
        INNER = HEADS * DIM_HEAD
        EPS = 1e-05

        def _layernorm(t, gamma, beta):
            mu = jnp.mean(t, axis=-1, keepdims=True)
            var = jnp.var(t, axis=-1, keepdims=True)
            return (t - mu) * jax.lax.rsqrt(var + EPS) * gamma + beta
        b, n, _ = x.shape
        qkv = x @ w_map.T
        q, k, v = jnp.split(qkv, 3, axis=-1)

        def to_heads(t):
            return t.reshape(b, n, HEADS, DIM_HEAD).transpose(0, 2, 1, 3)
        q, k, v = (to_heads(q), to_heads(k), to_heads(v))
        k = _layernorm(k, g_k, b_k)
        v = _layernorm(v, g_v, b_v)
        attn = jnp.einsum('bhnd,bhne->bhde', k, v) / n
        out = jnp.einsum('bhnd,bhde->bhne', q, attn)
        out = out.transpose(0, 2, 1, 3).reshape(b, n, INNER)
        return out @ w_out.T + b_out

    def _L0_ffn_ref(x, gate_w, w1, b1, w2, b2):
        import jax, jax.numpy as jnp
        import numpy as np
        TOP_K = 2
        B, S, D = x.shape
        E, _, H = w1.shape
        T = B * S
        K = TOP_K
        xf = x.reshape(T, D)
        logits = xf @ gate_w.T
        probs = jax.nn.softmax(logits, axis=-1)
        top_w, top_i = jax.lax.top_k(probs, K)
        top_w = top_w / (jnp.sum(top_w, axis=-1, keepdims=True) + 1e-09)
        flat_e = top_i.reshape(-1)
        flat_w = top_w.reshape(-1)
        tok_idx = jnp.repeat(jnp.arange(T), K)
        order = jnp.argsort(flat_e)
        se = flat_e[order]
        pt = tok_idx[order]
        pw = flat_w[order]
        counts = jax.ops.segment_sum(jnp.ones(T * K, jnp.int32), se, num_segments=E)
        starts = jnp.concatenate([jnp.zeros((1,), jnp.int32), jnp.cumsum(counts)[:-1]])
        pos = jnp.arange(T * K) - starts[se]
        cap = T * K
        padded = jnp.zeros((E, cap, D), x.dtype).at[se, pos].set(xf[pt])
        hidden = jax.nn.gelu(jnp.einsum('ecd,edh->ech', padded, w1) + b1[:, None, :], approximate=False)
        out = jnp.einsum('ech,ehd->ecd', hidden, w2) + b2[:, None, :]
        expert_out = out[se, pos] * pw[:, None]
        final = jnp.zeros((T, D), x.dtype).at[pt].add(expert_out)
        return final.reshape(B, S, D)

    def _L1_gnn_ref(x, edge_index, W1, att_src1, att_dst1, b1, W2, att_src2, att_dst2, b2):
        import jax, jax.numpy as jnp
        import numpy as np
        N_NODES = 625
        NEG_SLOPE = 0.2
        EPS = 1e-16

        def gat_layer(x, W, att_src, att_dst, bias, src, dst, heads, out_ch, concat):
            n = x.shape[0]
            h = (x @ W.T).reshape(n, heads, out_ch)
            a_src = jnp.einsum('nhc,hc->nh', h, att_src)
            a_dst = jnp.einsum('nhc,hc->nh', h, att_dst)
            e = a_src[src] + a_dst[dst]
            e = jax.nn.leaky_relu(e, NEG_SLOPE)
            m = jax.ops.segment_max(e, dst, num_segments=n)
            ex = jnp.exp(e - m[dst])
            denom = jax.ops.segment_sum(ex, dst, num_segments=n)
            alpha = ex / (denom[dst] + EPS)
            msg = alpha[:, :, None] * h[src]
            out = jax.ops.segment_sum(msg, dst, num_segments=n)
            if concat:
                out = out.reshape(n, heads * out_ch)
            else:
                out = out.mean(axis=1)
            return out + bias
        src, dst = (edge_index[0], edge_index[1])
        h = gat_layer(x, W1, att_src1, att_dst1, b1, src, dst, heads=8, out_ch=128, concat=True)
        h = jax.nn.relu(h)
        out = gat_layer(h, W2, att_src2, att_dst2, b2, src, dst, heads=1, out_ch=768, concat=True)
        return out

    def _L1_mix_ref(x, w_qkv, w_proj, b_proj):
        import jax, jax.numpy as jnp
        import numpy as np
        NUM_HEADS = 12

        def _reference_tuple_inner(x, w_qkv, w_proj, b_proj):
            B, N, C = x.shape
            H = NUM_HEADS
            D = C // H
            qkv = (x @ w_qkv).reshape(B, N, 3, H, D)
            q = jnp.transpose(qkv[:, :, 0], (0, 2, 1, 3))
            k = jnp.transpose(qkv[:, :, 1], (0, 2, 1, 3))
            v = jnp.transpose(qkv[:, :, 2], (0, 2, 1, 3))
            q = jax.nn.elu(q) + 1.0
            k = jax.nn.elu(k) + 1.0
            attn = jnp.einsum('bhnd,bhmd->bhnm', q, k)
            attn = attn / jnp.sum(attn, axis=-1, keepdims=True)
            out = jnp.einsum('bhnm,bhmd->bhnd', attn, v)
            out = jnp.transpose(out, (0, 2, 1, 3)).reshape(B, N, C)
            out = out @ w_proj + b_proj
            return (out, attn)
        return _reference_tuple_inner(x, w_qkv, w_proj, b_proj)[0]

    def _L1_ffn_ref(x, Wr, W1, b1, W2, b2, sW1, sb1, sW2, sb2):
        import jax, jax.numpy as jnp
        import numpy as np
        B, S, D, E, K = (1, 1024, 768, 8, 2)
        H = 4 * D
        Bx, Sx, Dx = x.shape
        xf = x.reshape(-1, Dx)
        T = xf.shape[0]
        logits = xf @ Wr.T
        topv, idx = jax.lax.top_k(logits, K)
        gate_k = jax.nn.softmax(topv, axis=-1)
        gates = jnp.zeros((T, logits.shape[-1]), x.dtype).at[jnp.arange(T)[:, None], idx].add(gate_k)
        h = jax.nn.relu(jnp.einsum('td,ehd->teh', xf, W1) + b1)
        y = jnp.einsum('teh,edh->ted', h, W2) + b2
        moe = jnp.einsum('te,ted->td', gates, y)
        sh = jax.nn.relu(xf @ sW1.T + sb1) @ sW2.T + sb2
        out = moe + 0.1 * K * sh
        return out.reshape(Bx, Sx, Dx)
    edge_index = jnp.stack([src, dst])
    xn = _layernorm(x, axis=-1)
    x = x + _L0_gnn_ref(xn, L0_gnn_W1, L0_gnn_b1, L0_gnn_W2, L0_gnn_b2, edge_index) + _L0_mix_ref(xn[None], L0_mix_w_map, L0_mix_g_k, L0_mix_b_k, L0_mix_g_v, L0_mix_b_v, L0_mix_w_out, L0_mix_b_out)[0]
    x = x + _L0_ffn_ref(_layernorm(x, axis=-1)[None], L0_ffn_gate_w, L0_ffn_w1, L0_ffn_b1, L0_ffn_w2, L0_ffn_b2)[0]
    xn = _layernorm(x, axis=-1)
    x = x + _L1_gnn_ref(xn, edge_index, L1_gnn_W1, L1_gnn_att_src1, L1_gnn_att_dst1, L1_gnn_b1, L1_gnn_W2, L1_gnn_att_src2, L1_gnn_att_dst2, L1_gnn_b2) + _L1_mix_ref(xn[None], L1_mix_w_qkv, L1_mix_w_proj, L1_mix_b_proj)[0]
    x = x + _L1_ffn_ref(_layernorm(x, axis=-1)[None], L1_ffn_Wr, L1_ffn_W1, L1_ffn_b1, L1_ffn_W2, L1_ffn_b2, L1_ffn_sW1, L1_ffn_sb1, L1_ffn_sW2, L1_ffn_sb2)[0]
    return x

_drawn_inputs = setup_inputs


def setup_inputs(seed=0):
    import zlib

    import numpy as np

    out = dict(_drawn_inputs(seed))
    spreads = {'L0_gnn_b1': (0.0, 0.1),
     'L0_gnn_b2': (0.0, 0.1),
     'L0_mix_g_k': (1.0, 0.2),
     'L0_mix_b_k': (0.0, 0.1),
     'L0_mix_g_v': (1.0, 0.2),
     'L0_mix_b_v': (0.0, 0.1),
     'L0_ffn_b1': (0.0, 0.36),
     'L0_ffn_b2': (0.0, 0.1),
     'L1_gnn_b1': (0.0, 0.1),
     'L1_gnn_b2': (0.0, 0.1),
     'L1_mix_b_proj': (0.0, 0.1),
     'L1_ffn_b1': (0.0, 0.1),
     'L1_ffn_b2': (0.0, 0.1),
     'L1_ffn_sb1': (0.0, 0.669),
     'L1_ffn_sb2': (0.0, 0.514)}
    factors = {'L0_mix_b_out': 3.028,
     'L1_gnn_att_dst1': 6.755,
     'L1_gnn_att_src2': 5.46,
     'L1_gnn_att_dst2': 7.334}
    for name, (base, spread) in spreads.items():
        noise = np.random.default_rng([zlib.crc32(name.encode()), seed]).standard_normal(out[name].shape)
        drawn = base * np.exp(spread * noise) if base else spread * noise
        out[name] = jnp.asarray(drawn.astype(out[name].dtype))
    for name, factor in factors.items():
        out[name] = (out[name] * factor).astype(out[name].dtype)
    return out
```

```python
from contextlib import ExitStack

import concourse.bass as bass
from concourse import mybir

F32 = mybir.dt.float32
F32R = mybir.dt.float32r
F16 = mybir.dt.float16
I32 = mybir.dt.int32
U32 = mybir.dt.uint32
ACT = mybir.ActivationFunctionType
ALU = mybir.AluOpType
AX_X = mybir.AxisListType.X

P = 128
T = 625
TT = (T + P - 1) // P
TP = TT * P
LAST = T - (TT - 1) * P
D = 768
KD = D // P
HALF = D // 2
NE = 20000
EP = 125
EC = NE // EP
TM = T // 2 + 1
PACK = 4096
CHUNK_E = 32
assert CHUNK_E * EP < PACK and EC % CHUNK_E == 0 and PACK * CHUNK_E * EP < 2 ** 24
HEADS = 12
DH = 64
PAIRS = HEADS // 2
E = 8
H0 = 192
KH0 = E * H0 // P
G1 = 8
C1 = G1 * P
H1 = 3072
WC = KD * HALF
NCH = H1 // HALF
MAIN = 2
CAP = MAIN * P
EXTRA = TT - MAIN
NEG = -1.0e30
LN_EPS = 1e-5
SLOPE = 0.2
TOKEN_SPANS = [(0, 320), (320, 306)]


class Queue:

    def __init__(self, engine, semaphore):
        self.engine, self.semaphore, self.count, self.seen = engine, semaphore, 0, {}

    def wait(self, *tokens):
        for token in tokens:
            if token is None:
                continue
            semaphore, value = token
            if self.seen.get(semaphore.name, 0) < value:
                self.engine.wait_ge(semaphore, value)
                self.seen[semaphore.name] = value

    def done(self, instruction):
        self.count += 1
        instruction.then_inc(self.semaphore, 1)
        return (self.semaphore, self.count)

    def last(self):
        return (self.semaphore, self.count) if self.count else None


class Banks:

    def __init__(self, banks):
        self.banks, self.free, self.at = banks, [None] * len(banks), 0

    def take(self):
        i = self.at % len(self.banks)
        self.at += 1
        return i, self.banks[i], self.free[i]

    def release(self, i, token):
        self.free[i] = token


def build(nc, ins, out, slots_dram, result_dram):
    with ExitStack() as ctx:
        def sb(name, shape, dt=F32, scope=None):
            return (scope or ctx).enter_context(nc.sbuf_tensor(name, shape, dt))

        def sem(name):
            return ctx.enter_context(nc.semaphore(name))

        pe = Queue(nc.tensor, sem("pe_done"))
        act = Queue(nc.scalar, sem("act_done"))
        dve = Queue(nc.vector, sem("dve_done"))
        pool = Queue(nc.gpsimd, sem("pool_done"))
        sp = Queue(nc.sync, sem("sp_done"))
        engines = (pe, act, dve, pool)
        stores = []

        def phase_end():
            ends = [q.last() for q in engines]
            for q in engines + (sp,):
                q.wait(*ends, *stores)

        def load(name, dst, src, *after, queue=sp):
            s = sem("in_" + name)
            queue.wait(*after)
            queue.engine.dma_start(dst, src).then_inc(s, 16)
            return (s, 16)

        psum = [ctx.enter_context(nc.psum_tensor(f"bank{i}", [P, 512], F32)) for i in range(8)]
        banks = Banks(psum)

        order = []
        for name, n in (("mix0_kv", 4), ("mix0_q", 2), ("mix0_out", 2), ("gnn0_w1", 2), ("gnn0_w2", 2)):
            if name == "mix0_q":
                for g in range(2):
                    order += [("mix0_q", g), ("mix0_out", g)]
            elif name != "mix0_out":
                order += [(name, i) for i in range(n)]
        for half in range(2):
            order += [(f"ffn0_w{n}", 2 * half + i) for n in (1, 2) for i in range(2)]
        order += [("mix1_kv", i) for i in range(4)]
        for g in range(2):
            order += [("mix1_q", g), ("mix1_out", g)]
        for g in range(4):
            order += [("gat_w1", g), ("gat_w2", g)]
        passes = [("shared", g) for g in range(3)] + [(e, 0) for e in range(E)]
        for who, g in passes:
            for c in range(NCH + 1):
                if c < NCH:
                    order.append(("ffn1_w1", who, c))
                if c > 0:
                    order.append(("ffn1_w2", who, c - 1))

        def weight_source(key):
            if key[0] in ("ffn1_w1", "ffn1_w2"):
                if key[1] == "shared":
                    return ins["shared" + key[0][4:]][key[2]]
                return ins[key[0]][key[1] * NCH + key[2]]
            return ins[key[0]][key[1]]

        RAW, PAIR = 2, 3
        raw = sb("weight_raw", [P, RAW, WC])
        whi = sb("weight_hi", [P, PAIR, WC], F32R)
        wlo = sb("weight_lo", [P, PAIR, WC], F32R)
        raw_sem = [sem(f"weight_landed{i}") for i in range(RAW)]
        stream = {"loaded": 0, "split": 0, "used": 0}
        raw_free, pair_free, landed, pair_ready = {}, {}, {}, {}

        def stream_load():
            i = stream["loaded"]
            if i >= len(order):
                return
            src = weight_source(order[i])
            sp.wait(raw_free.get(i - RAW))
            sp.engine.dma_start(raw[:, i % RAW, 0:src.shape[1]], src).then_inc(raw_sem[i % RAW], 16)
            landed[i] = (raw_sem[i % RAW], 16 * (i // RAW + 1))
            stream["loaded"] += 1

        def stream_split():
            while stream["split"] < len(order):
                i = stream["split"]
                if i >= PAIR and i - PAIR not in pair_free:
                    return
                w = weight_source(order[i]).shape[1]
                r, h = i % RAW, i % PAIR
                act.wait(landed[i], pair_free.get(i - PAIR))
                hi_done = act.done(nc.scalar.activation(whi[:, h, 0:w], raw[:, r, 0:w], ACT.Copy))
                dve.wait(landed[i], hi_done, pair_free.get(i - PAIR))
                lo_done = dve.done(nc.vector.tensor_tensor(wlo[:, h, 0:w], raw[:, r, 0:w],
                                                           whi[:, h, 0:w].bitcast(F32), ALU.subtract))
                pair_ready[i] = lo_done
                raw_free[i] = lo_done
                stream["split"] += 1
                stream_load()

        def take_weight(*key):
            i = stream["used"]
            assert order[i] == key, (order[i], key)
            stream["used"] += 1
            stream_split()
            w = weight_source(key).shape[1]
            kt = {"mix0_out": 3, "mix1_out": 3, "ffn1_w2": 3, "gat_w2": 2}.get(key[0], KD)
            hi = whi[:, i % PAIR, 0:w].rearrange("p (k n) -> p k n", k=kt)
            lo = wlo[:, i % PAIR, 0:w].rearrange("p (k n) -> p k n", k=kt)
            return (hi, lo), i, pair_ready[i]

        def drop_weight(i):
            pair_free[i] = pe.last()
            stream_split()

        stream_load()
        stream_load()

        def mm3(dst, a, b, first, last):
            nc.tensor.matmul(dst, a[0], b[0], start=first, stop=False)
            nc.tensor.matmul(dst, a[0], b[1], start=False, stop=False)
            return nc.tensor.matmul(dst, a[1], b[0], start=False, stop=last)

        def product(dst, terms, first=True, last=True):
            terms = list(terms)
            for n, (a, b) in enumerate(terms):
                end = mm3(dst, a, b, first and n == 0, last and n == len(terms) - 1)
            return pe.done(end)

        def product_exact_a(dst, terms):
            terms = list(terms)
            for n, (a, b) in enumerate(terms):
                nc.tensor.matmul(dst, a, b[0], start=(n == 0), stop=False)
                end = nc.tensor.matmul(dst, a, b[1], start=False, stop=(n == len(terms) - 1))
            return pe.done(end)

        def split(pair, src, *after):
            act.wait(*after)
            hi_done = act.done(nc.scalar.activation(pair[0], src, ACT.Copy))
            dve.wait(hi_done, *after)
            return dve.done(nc.vector.tensor_tensor(pair[1], src, pair[0].bitcast(F32), ALU.subtract))

        def at(pair, *index):
            return (pair[0].__getitem__(index), pair[1].__getitem__(index))

        def v(instruction, *after):
            dve.wait(*after)
            return dve.done(instruction())

        def a(instruction, *after):
            act.wait(*after)
            return act.done(instruction())

        def g(instruction, *after):
            pool.wait(*after)
            return pool.done(instruction())

        ident = sb("identity", [P, P])
        ones = sb("ones", [P, P], F32R)
        iota_h = sb("iota_half", [P, TP], F16)
        ones_f = sb("ones_f", [P, P])
        c1 = g(lambda: nc.gpsimd.memset(ident[:, :], 0.0))
        c2 = g(lambda: nc.gpsimd.affine_select(out=ident[:, :], in_=ident[:, :], compare_op=ALU.not_equal, fill=1.0,
                                               base=0, pattern=[[-1, P]], channel_multiplier=1), c1)
        c3 = g(lambda: nc.gpsimd.memset(ones_f[:, :], 1.0))
        ones_ready = a(lambda: nc.scalar.activation(ones[:, :], ones_f[:, :], ACT.Copy), c3)

        x = sb("x", [P, TT, D])
        xT = (sb("xT_hi", [P, KD, TP], F32R), sb("xT_lo", [P, KD, TP], F32R))
        count = sb("edge_count", [P, TT, TP], mybir.dt.uint16)
        bias0 = sb("bias_row", [P, D])
        stats = sb("ln_stats", [P, TT, 2, 6])
        moments = sb("ln_moments", [P, TT, 2])
        rstd = sb("ln_rstd", [P, TT])
        start = ExitStack()
        iota_i = sb("iota_int", [P, TP], I32, start)
        edges_i = sb("edges_int", [EP, 2, EC], I32, start)
        c4 = g(lambda: nc.gpsimd.iota(iota_i[:, :], [[1, TP]], base=0, channel_multiplier=0))
        c5 = g(lambda: nc.gpsimd.tensor_copy(iota_h[:, :], iota_i[:, :]), c4)
        const_ready = c5
        zero_x = v(lambda: nc.vector.memset(x[96:P, TT - 1, :], 0.0))
        x_sem = sem("in_x")
        sp.wait(zero_x)
        sp.engine.dma_start(x[:, 0:TT - 1, :], ins["x"][0:(TT - 1) * P, :].rearrange("(t p) d -> p t d", p=P)).then_inc(x_sem, 16)
        sp.engine.dma_start(x[0:LAST, TT - 1, :], ins["x"][(TT - 1) * P:T, :]).then_inc(x_sem, 16)
        x_ready = (x_sem, 32)
        edge_sem = sem("in_edges")
        sp.engine.dma_start(edges_i[:, 0, :], ins["src"]).then_inc(edge_sem, 16)
        sp.engine.dma_start(edges_i[:, 1, :], ins["dst"]).then_inc(edge_sem, 16)
        edges_ready = (edge_sem, 32)
        zeros = v(lambda: nc.vector.memset(bias0[:, :], 0.0))
        zeroed = (sem("overflow_zeroed"), 16)
        act.wait(zeros, x_ready, edges_ready)
        act.engine.dma_start(result_dram[E * CAP:E * TP, :].rearrange("(n p) d -> p n d", p=P),
                             bias0[:, :].unsqueeze(1).broadcast_to([P, E * EXTRA, D])).then_inc(zeroed[0], 16)
        stores.append(zeroed)


        def layer_norm(xn, *after):
            for t in range(TT):
                for h in range(2):
                    s = v(lambda: nc.vector.bn_stats(stats[:, t, h, :], x[:, t, h * HALF:(h + 1) * HALF]), *after)
            dve.wait(s)
            for t in range(TT):
                s = v(lambda: nc.vector.bn_aggr(moments[:, t, :], stats[:, t, :, :].rearrange("p a b -> p (a b)")))
            s = v(lambda: nc.vector.tensor_scalar(rstd[:, :], moments[:, :, 1], LN_EPS, None, ALU.add), s)
            s = a(lambda: nc.scalar.activation(rstd[:, :], rstd[:, :], ACT.Sqrt), s)
            s = v(lambda: nc.vector.reciprocal(rstd[:, :], rstd[:, :]), s)
            dve.wait(s)
            return [v(lambda: nc.vector.tensor_scalar(xn[:, t, :], x[:, t, :], moments[:, t, 0:1], rstd[:, t:t + 1],
                                                      ALU.subtract, ALU.mult)) for t in range(TT)]

        def transpose_in(xn, ready, *after):
            done = []
            for t in range(TT):
                for c in range(2):
                    i, bank, free = banks.take()
                    pe.wait(ready[t], free, *after)
                    for k in range(3):
                        end = nc.tensor.transpose(bank[:, k * P:(k + 1) * P],
                                                  xn[:, t, (3 * c + k) * P:(3 * c + k + 1) * P], ident[:, :])
                    moved = pe.done(end)
                    part = at(xT, slice(None), slice(3 * c, 3 * c + 3), slice(t * P, (t + 1) * P))
                    s = split(part, bank[:, 0:3 * P].rearrange("p (k n) -> p k n", k=3), moved)
                    banks.release(i, s)
                done.append(s)
            return done

        def tok(t):
            return slice(t * P, (t + 1) * P)


        def row_load(name, dst, src, n, *after):
            return load(name, dst, src.rearrange("(a n) -> a n", a=1).broadcast_to([P, n]), *after)

        with ExitStack() as scope:
            xn = sb("xn0", [P, TT, D], scope=scope)
            pe.wait(c2)
            xT_ready = transpose_in(xn, layer_norm(xn, x_ready))

            edge = sb("edges", [EP, 4, EC], scope=scope)
            s = v(lambda: nc.vector.tensor_copy(edge[:, 0:2, :], edges_i[:, :, :]), edges_ready)
            s = v(lambda: nc.vector.tensor_scalar(edge[:, 3, :], edge[:, 1, :], float(TM), None, ALU.is_ge), s)
            s = v(lambda: nc.vector.tensor_scalar(edge[:, 2, :], edge[:, 3, :], float(PACK - 1), 1.0, ALU.mult, ALU.add), s)
            s = v(lambda: nc.vector.scalar_tensor_tensor(edge[:, 1, :], edge[:, 3, :], -float(TM), edge[:, 1, :],
                                                         ALU.mult, ALU.add), s)
            fold_ready = s
            RING = 4
            hot_src = sb("one_hot_src", [EP, RING, TP], F16, scope)
            hot_dst = sb("one_hot_dst", [EP, RING, 320], F16, scope)
            whole = sb("packed_counts", [P, TT, TM], I32, scope)
            low = sb("low_counts", [P, TT, TM], I32, scope)
            high = sb("high_counts", [P, TT, TM], I32, scope)
            cnt = sb("counts", [P, TT, TP], I32, scope)
            counted = g(lambda: nc.gpsimd.memset(cnt[:, :, :], 0))
            hot_free = [None] * RING
            dve.wait(const_ready, fold_ready)
            unpacked = None
            whole_free = None
            for chunk in range(EC // CHUNK_E):
                taken = [banks.take() for _ in range(TT)]
                for n in range(CHUNK_E):
                    j = chunk * CHUNK_E + n
                    r = j % RING
                    dve.wait(hot_free[r])
                    v(lambda: nc.vector.tensor_scalar(hot_src[:, r, :], iota_h[0:EP, :], edge[:, 0, j:j + 1], None, ALU.is_equal))
                    hot = v(lambda: nc.vector.tensor_scalar(hot_dst[:, r, :], iota_h[0:EP, 0:320], edge[:, 1, j:j + 1],
                                                            edge[:, 2, j:j + 1], ALU.is_equal, ALU.mult))
                    pe.wait(hot)
                    for t in range(TT):
                        if n == 0:
                            pe.wait(taken[t][2])
                        end = nc.tensor.matmul(taken[t][1][:, 0:TM], hot_src[:, r, tok(t)], hot_dst[:, r, 0:TM],
                                               start=(n == 0), stop=(n == CHUNK_E - 1))
                    hot_free[r] = pe.done(end)
                for t in range(TT):
                    got = a(lambda: nc.scalar.activation(whole[:, t, :], taken[t][1][:, 0:TM], ACT.Copy),
                            hot_free[r], whole_free)
                    banks.release(taken[t][0], got)
                v(lambda: nc.vector.tensor_scalar(low[:, :, :], whole[:, :, :], PACK - 1, None, ALU.bitwise_and), got, unpacked)
                cut = v(lambda: nc.vector.tensor_scalar(high[:, :, :], whole[:, :, :], 12, None, ALU.logical_shift_right))
                whole_free = cut
                counted = g(lambda: nc.gpsimd.tensor_tensor(cnt[:, :, 0:TM], cnt[:, :, 0:TM], low[:, :, :], ALU.add), cut, counted)
                counted = g(lambda: nc.gpsimd.tensor_tensor(cnt[:, :, TM:T], cnt[:, :, TM:T], high[:, :, 0:T - TM], ALU.add), counted)
                unpacked = counted
            counts_kept = v(lambda: nc.vector.tensor_copy(count[:, :, :], cnt[:, :, :]), counted)
            phase_end()
        start.close()

        def add_bias(names, scale=None):
            for name in names:
                s = row_load(name, bias0[:, :], ins[name], D, dve.last())
                if scale is not None:
                    s = v(lambda: nc.vector.tensor_scalar(bias0[:, :], bias0[:, :], scale, None, ALU.mult), s)
                dve.wait(s)
                for t in range(TT):
                    s = v(lambda: nc.vector.tensor_tensor(x[:, t, :], x[:, t, :], bias0[:, :], ALU.add), dve.last())
            return s

        def add_tokens(pairs_of, n_terms, weight, cols, c0, ready):
            for t in range(TT):
                i, bank, free = banks.take()
                pe.wait(free, *ready)
                got = product(bank[:, 0:cols], [(pairs_of(k, t), at(weight, slice(None), k, slice(0, cols))) for k in range(n_terms)])
                s = v(lambda: nc.vector.tensor_tensor(x[:, t, c0:c0 + cols], x[:, t, c0:c0 + cols], bank[:, 0:cols], ALU.add), got)
                banks.release(i, s)
            return s

        def linear_attention(kind, finish_kv, finish_q, normalised):
            with ExitStack() as scope:
                kv = sb(kind + "_kv", [P, TT, 2, HALF], F32, scope)
                kvp = (sb(kind + "_kv_hi", [P, TT, 2, HALF], F32R, scope), sb(kind + "_kv_lo", [P, TT, 2, HALF], F32R, scope))
                att = (sb(kind + "_att_hi", [P, PAIRS, P], F32R, scope), sb(kind + "_att_lo", [P, PAIRS, P], F32R, scope))
                attf = sb(kind + "_att", [P, PAIRS, P], F32, scope)
                s0 = v(lambda: nc.vector.memset(attf[:, :, :], 0.0))
                if normalised:
                    den = (sb(kind + "_den_hi", [P, PAIRS, P], F32R, scope), sb(kind + "_den_lo", [P, PAIRS, P], F32R, scope))
                    denf = sb(kind + "_den", [P, PAIRS, P], F32, scope)
                    s0 = v(lambda: nc.vector.memset(denf[:, :, :], 0.0))
                rows = finish_kv(None, kv, scope)
                kv_read = None
                for grp in range(2):
                    for which in range(2):
                        w, i, ready = take_weight(kind + "_kv", 2 * grp + which)
                        pe.wait(ready, *xT_ready)
                        for t in range(TT):
                            b, bank, free = banks.take()
                            pe.wait(free)
                            got = product(bank[:, 0:HALF], [(at(xT, slice(None), k, tok(t)), at(w, slice(None), k, slice(None))) for k in range(KD)])
                            s = a(lambda: nc.scalar.activation(kv[:, t, which, :], bank[:, 0:HALF], ACT.Copy), got, dve.last())
                            banks.release(b, s)
                        drop_weight(i)
                        s = finish_kv(which, kv, rows, s)
                    s = split(at(kvp, slice(None), slice(None), slice(None), slice(None)), kv[:, :, :, :], s, kv_read)
                    pe.wait(s)
                    for pr in range(3):
                        b, bank, free = banks.take()
                        pe.wait(free)
                        cols = slice(pr * P, (pr + 1) * P)
                        sizes = [P] * (TT - 1) + [LAST]
                        kv_read = product(bank[:, 0:P], [(at(kvp, slice(0, n), t, 0, cols), at(kvp, slice(0, n), t, 1, cols))
                                                         for t, n in enumerate(sizes)])
                        for h in range(2):
                            blk = slice(h * DH, (h + 1) * DH)
                            s = v(lambda: nc.vector.tensor_scalar(attf[blk, 3 * grp + pr, blk], bank[blk, h * DH:(h + 1) * DH],
                                                                  1.0 if normalised else 1.0 / T, None, ALU.mult), kv_read, s0)
                        banks.release(b, s)
                        if normalised:
                            b, bank, free = banks.take()
                            pe.wait(free)
                            for t, n in enumerate(sizes):
                                nc.tensor.matmul(bank[:, 0:P], kvp[0][0:n, t, 0, cols], ones[0:n, :], start=(t == 0), stop=False)
                                end = nc.tensor.matmul(bank[:, 0:P], kvp[1][0:n, t, 0, cols], ones[0:n, :], start=False, stop=(t == TT - 1))
                            kv_read = pe.done(end)
                            for h in range(2):
                                blk = slice(h * DH, (h + 1) * DH)
                                s = v(lambda: nc.vector.tensor_copy(denf[blk, 3 * grp + pr, blk], bank[blk, h * DH:(h + 1) * DH]), kv_read)
                            banks.release(b, s)
                att_ready = split(at(att, slice(None), slice(None), slice(None)), attf[:, :, :], s)
                if normalised:
                    att_ready = split(at(den, slice(None), slice(None), slice(None)), denf[:, :, :], s)
                phase_end()
                flat = [b[:, :, :, :].rearrange("p a b c -> p (a b c)") for b in kvp]
                qp = tuple(f[:, 0:TP].rearrange("p (a n) -> p a n", a=1) for f in flat)
                outT = tuple(f[:, TP:TP + 3 * TP].rearrange("p (a n) -> p a n", a=3) for f in flat)
                work = kv[:, :, :, :].rearrange("p a b c -> p (a b c)")
                q_tmp, q_tmp2, d_tmp = work[:, 0:TP], work[:, TP:2 * TP], work[:, 2 * TP:3 * TP]
                q_read = None
                out_read = None
                zero = v(lambda: nc.vector.memset(work[:, 0:4 * TP], 0.0))
                for part in (qp, outT):
                    zero = split(part, work[:, 0:part[0].shape[1] * TP].rearrange("p (a n) -> p a n", n=TP), zero)
                for grp in range(2):
                    w, i, ready = take_weight(kind + "_q", grp)
                    for pr in range(3):
                        got = {}
                        for c0, n in TOKEN_SPANS:
                            b, bank, free = banks.take()
                            pe.wait(free, ready)
                            tk = product(bank[:, 0:n], [(at(w, slice(None), k, slice(pr * P, (pr + 1) * P)),
                                                         at(xT, slice(None), k, slice(c0, c0 + n))) for k in range(KD)])
                            s = finish_q(q_tmp[:, c0:c0 + n], q_tmp2[:, c0:c0 + n], bank[:, 0:n], tk, b)
                        s = split(at(qp, slice(None), 0, slice(0, T + 1)), q_tmp[:, 0:T + 1], s, q_read)
                        pe.wait(s, att_ready)
                        for c0, n in TOKEN_SPANS:
                            b, bank, free = banks.take()
                            pe.wait(free)
                            q = at(qp, slice(None), 0, slice(c0, c0 + n))
                            tk = product(bank[:, 0:n], [(at(att, slice(None), 3 * grp + pr, slice(None)), q)])
                            o = at(outT, slice(None), pr, slice(c0, c0 + n))
                            if normalised:
                                b2, bank2, free = banks.take()
                                pe.wait(free)
                                tk2 = product(bank2[:, 0:n], [(at(den, slice(None), 3 * grp + pr, slice(None)), q)])
                                s = v(lambda: nc.vector.reciprocal(d_tmp[:, c0:c0 + n], bank2[:, 0:n]), tk2, dve.last())
                                banks.release(b2, s)
                                s = v(lambda: nc.vector.tensor_tensor(d_tmp[:, c0:c0 + n], bank[:, 0:n], d_tmp[:, c0:c0 + n], ALU.mult), tk, s)
                                banks.release(b, s)
                                s = split(o, d_tmp[:, c0:c0 + n], s, out_read)
                                tk = tk2
                            else:
                                s = split(o, bank[:, 0:n], tk, out_read)
                                banks.release(b, s)
                            q_read = tk
                    drop_weight(i)
                    w, i, ready = take_weight(kind + "_out", grp)
                    for c in range(2):
                        part = at(w, slice(None), slice(None), slice(c * HALF, (c + 1) * HALF))
                        add_tokens(lambda k, t: at(outT, slice(None), k, tok(t)), 3, part, HALF, c * HALF, (ready, s))
                    out_read = pe.last()
                    drop_weight(i)
                phase_end()

        x_based = add_bias(("gnn0_b2", "mix0_b"))

        def kv0(which, kv, rows, after=None):
            if which is None:
                scope = rows
                gb = sb("gain_shift_rows", [P, 4, DH], F32, scope)
                for n, name in enumerate(("mix0_gk", "mix0_bk", "mix0_gv", "mix0_bv")):
                    got = row_load(name, gb[:, n, :], ins[name], DH)
                    dve.wait(got)
                return gb, sb("kv_square", [P, TT * 6, DH], F32, scope), sb("kv_stats", [P, 3, TT * 6], F32, scope)
            gb, sq, st = rows
            z = [kv[:, t, which, :].rearrange("p (h d) -> p h d", d=DH) for t in range(TT)]
            n6 = lambda i, t: st[:, i, 6 * t:6 * t + 6]
            wide = lambda ap: ap.unsqueeze(2).broadcast_to([P, 6, DH])
            gain = lambda i: gb[:, i, :].unsqueeze(1).broadcast_to([P, 6, DH])
            sqt = lambda t: sq[:, 6 * t:6 * t + 6, :]
            every = range(TT)
            for t in every:
                s = v(lambda: nc.vector.tensor_reduce(n6(0, t), z[t], AX_X, ALU.add), after)
            s = v(lambda: nc.vector.tensor_scalar(st[:, 0, :], st[:, 0, :], 1.0 / DH, None, ALU.mult), s)
            dve.wait(s)
            for t in every:
                s = v(lambda: nc.vector.tensor_tensor(z[t], z[t], wide(n6(0, t)), ALU.subtract))
            act.wait(s)
            for t in every:
                s = a(lambda: nc.scalar.activation(sqt(t), z[t], ACT.Square))
            s = v(lambda: nc.vector.tensor_reduce(st[:, 1, :], sq[:, :, :], AX_X, ALU.add), s)
            s = v(lambda: nc.vector.tensor_scalar(st[:, 1, :], st[:, 1, :], 1.0 / DH, LN_EPS, ALU.mult, ALU.add), s)
            s = a(lambda: nc.scalar.activation(st[:, 1, :], st[:, 1, :], ACT.Sqrt), s)
            s = v(lambda: nc.vector.reciprocal(st[:, 2, :], st[:, 1, :]), s)
            for step in range(3):
                dve.wait(s)
                for t in every:
                    o = (wide(n6(2, t)), gain(2 * which), gain(2 * which + 1))[step]
                    s = v(lambda: nc.vector.tensor_tensor(z[t], z[t], o, ALU.add if step == 2 else ALU.mult))
            return s

        def q0(q, tmp, bank, got, b):
            s = a(lambda: nc.scalar.activation(q, bank, ACT.Copy), got, dve.last())
            banks.release(b, s)
            return s

        linear_attention("mix0", kv0, q0, False)

        gcn = ExitStack()
        adj = (sb("adj_hi", [P, TT, TP], F32R, gcn), sb("adj_lo", [P, TT, TP], F32R, gcn))
        with ExitStack() as scope:
            loops = sb("counts_with_loops", [P, TT, TP], F32, scope)
            deg_row = sb("deg_row", [P, TP], F32, scope)
            deg_col = sb("deg_col", [P, TT], F32, scope)
            s = v(lambda: nc.vector.tensor_copy(loops[:, :, :], count[:, :, :]))
            dve.wait(s)
            for t in range(TT):
                s = v(lambda: nc.vector.tensor_tensor(loops[:, t, tok(t)], loops[:, t, tok(t)], ident[:, :], ALU.add))
            s = split(at(adj, slice(None), slice(None), slice(None)), loops[:, :, :], s)
            pe.wait(s, ones_ready)
            for c0, n in ((0, 320), (320, 320)):
                i, bank, free = banks.take()
                pe.wait(free)
                got = product_exact_a(bank[:, 0:n], [(ones[:, :], at(adj, slice(None), k, slice(c0, c0 + n))) for k in range(TT)])
                s = a(lambda: nc.scalar.activation(deg_row[:, c0:c0 + n], bank[:, 0:n], ACT.Sqrt), got)
                banks.release(i, s)
            row_done = v(lambda: nc.vector.reciprocal(deg_row[:, :], deg_row[:, :]), s)
            for t in range(TT):
                i, bank, free = banks.take()
                pe.wait(free)
                for k in range(TT):
                    nc.tensor.matmul(bank[:, 0:2], adj[0][:, k, tok(t)], ones[:, 0:2], start=(k == 0), stop=False)
                    end = nc.tensor.matmul(bank[:, 0:2], adj[1][:, k, tok(t)], ones[:, 0:2], start=False, stop=(k == TT - 1))
                s = a(lambda: nc.scalar.activation(deg_col[:, t:t + 1], bank[:, 0:1], ACT.Sqrt), pe.done(end))
                banks.release(i, s)
            s = v(lambda: nc.vector.reciprocal(deg_col[:, :], deg_col[:, :]), s)
            dve.wait(s, row_done)
            for t in range(TT):
                s = v(lambda: nc.vector.scalar_tensor_tensor(loops[:, t, :], loops[:, t, :], deg_col[:, t:t + 1],
                                                             deg_row[:, :], ALU.mult, ALU.mult))
            adj_ready = split(at(adj, slice(None), slice(None), slice(None)), loops[:, :, :], s)
            phase_end()

        with ExitStack() as scope:
            h = (sb("gcn_h_hi", [P, TT, D], F32R, scope), sb("gcn_h_lo", [P, TT, D], F32R, scope))
            bcol = sb("gcn_b1", [P, KD], F32, scope)
            b1_ready = load("gcn_b1", bcol[:, :], ins["gnn0_b1"])
            z_tmp = sb("gcn_tmp", [P, 2, 320], F32, scope)

            def node_product(key, src, ready):
                for c in range(2):
                    w, i, w_ready = take_weight(key, c)
                    for t in range(TT):
                        b, bank, free = banks.take()
                        pe.wait(free, w_ready, *ready)
                        got = product(bank[:, 0:HALF], [(at(src, slice(None), k, tok(t)), at(w, slice(None), k, slice(None))) for k in range(KD)])
                        s = split(at(h, slice(None), t, slice(c * HALF, (c + 1) * HALF)), bank[:, 0:HALF], got)
                        banks.release(b, s)
                    drop_weight(i)
                return s

            s = node_product("gnn0_w1", xT, xT_ready)
            pe.wait(s)
            hT_start = pe.last()
            tmp_free = [None, None]
            n_tmp = 0
            act.wait(b1_ready)
            for m in range(KD):
                for c0, n in TOKEN_SPANS:
                    b, bank, free = banks.take()
                    pe.wait(free)
                    got = product(bank[:, 0:n], [(at(h, slice(None), k, slice(m * P, (m + 1) * P)), at(adj, slice(None), k, slice(c0, c0 + n)))
                                                 for k in range(TT)])
                    tmp = z_tmp[:, n_tmp % 2, 0:n]
                    s = a(lambda: nc.scalar.activation(tmp, bank[:, 0:n], ACT.Relu, bias=bcol[:, m:m + 1]), got, tmp_free[n_tmp % 2])
                    banks.release(b, s)
                    s = split(at(xT, slice(None), m, slice(c0, c0 + n)), tmp, s, hT_start)
                    tmp_free[n_tmp % 2] = s
                    n_tmp += 1
            act.wait(pe.last())
            dve.wait(pe.last())
            s = node_product("gnn0_w2", xT, (s,))
            for c in range(2):
                add_tokens(lambda k, t: at(adj, slice(None), k, tok(t)), TT,
                           at(h, slice(None), slice(None), slice(c * HALF, (c + 1) * HALF)), HALF, c * HALF, (s,))
            phase_end()
        gcn.close()

        iota8 = sb("expert_number", [P, TT, E])
        with ExitStack() as scope:
            iota8_i = sb("expert_number_int", [P, TT, E], I32, scope)
            s = g(lambda: nc.gpsimd.iota(iota8_i[:, :, :], [[0, TT], [1, E]], base=0, channel_multiplier=0))
            iota8_ready = g(lambda: nc.gpsimd.tensor_copy(iota8[:, :, :], iota8_i[:, :, :]), s)
            phase_end()
        over_e = lambda ap: ap.unsqueeze(2).broadcast_to([P, TT, E])

        def router_logits(name, logits, scope):
            gate = sb(name + "_gate", [P, KD, E], F32, scope)
            gp = (sb(name + "_gate_hi", [P, KD, E], F32R, scope), sb(name + "_gate_lo", [P, KD, E], F32R, scope))
            s = split(at(gp, slice(None), slice(None), slice(None)), gate[:, :, :], load(name, gate[:, :, :], ins[name]))
            pe.wait(s, *xT_ready)
            for t in range(TT):
                b, bank, free = banks.take()
                pe.wait(free)
                got = product(bank[:, 0:E], [(at(xT, slice(None), k, tok(t)), at(gp, slice(None), k, slice(None))) for k in range(KD)])
                s = a(lambda: nc.scalar.activation(logits[:, t, :], bank[:, 0:E], ACT.Copy), got)
                banks.release(b, s)
            return s

        def top_two(name, p, scope, after):
            best = sb(name + "_best", [P, 2, TT], F32, scope)
            number = sb(name + "_number", [P, TT], F32, scope)
            hot = sb(name + "_one_hot", [P, 2, TT, E], F32, scope)
            work = sb(name + "_work", [P, TT, E], F32, scope)
            rest = sb(name + "_rest", [P, TT, E], F32, scope)
            s = v(lambda: nc.vector.tensor_copy(rest[:, :, :], p), after, iota8_ready)
            for k in range(2):
                s = v(lambda: nc.vector.tensor_reduce(best[:, k, :], rest[:, :, :], AX_X, ALU.max), s)
                s = v(lambda: nc.vector.tensor_tensor(work[:, :, :], rest[:, :, :], over_e(best[:, k, :]), ALU.is_equal), s)
                s = v(lambda: nc.vector.scalar_tensor_tensor(work[:, :, :], work[:, :, :], -float(E), iota8[:, :, :], ALU.mult, ALU.add), s)
                s = v(lambda: nc.vector.tensor_reduce(number[:, :], work[:, :, :], AX_X, ALU.min), s)
                s = v(lambda: nc.vector.tensor_scalar(number[:, :], number[:, :], float(E), None, ALU.add), s)
                s = v(lambda: nc.vector.tensor_tensor(hot[:, k, :, :], iota8[:, :, :], over_e(number[:, :]), ALU.is_equal), s)
                s = v(lambda: nc.vector.scalar_tensor_tensor(rest[:, :, :], hot[:, k, :, :], NEG, rest[:, :, :], ALU.mult, ALU.add), s)
            return best, hot, s

        def gate_matrix(name, weights, hot, scope, after):
            gates = sb(name + "_gates", [P, 2, TT, E], F32, scope)
            gT = (sb(name + "_gatesT_hi", [E, TP], F32R, scope), sb(name + "_gatesT_lo", [E, TP], F32R, scope))
            for k in range(2):
                s = v(lambda: nc.vector.tensor_tensor(gates[:, k, :, :], hot[:, k, :, :], over_e(weights[:, k, :]), ALU.mult), after)
            s = v(lambda: nc.vector.tensor_tensor(gates[:, 0, :, :], gates[:, 0, :, :], gates[:, 1, :, :], ALU.add), s)
            pe.wait(s)
            for t in range(TT):
                b, bank, free = banks.take()
                pe.wait(free)
                moved = pe.done(nc.tensor.transpose(bank[0:E, 0:P], gates[:, 0, t, :], ident[:, :]))
                s = split(at(gT, slice(None), tok(t)), bank[0:E, 0:P], moved)
                banks.release(b, s)
            return gT, s

        with ExitStack() as scope:
            xn = sb("xn1", [P, TT, D], F32, scope)
            xT_ready = transpose_in(xn, layer_norm(xn, dve.last()))
            phase_end()
        with ExitStack() as scope:
            p = sb("ffn0_p", [P, TT, E], F32, scope)
            m = sb("ffn0_m", [P, 2, TT], F32, scope)
            s = router_logits("ffn0_gate", p, scope)
            s = v(lambda: nc.vector.tensor_reduce(m[:, 0, :], p[:, :, :], AX_X, ALU.max), s)
            s = v(lambda: nc.vector.tensor_tensor(p[:, :, :], p[:, :, :], over_e(m[:, 0, :]), ALU.subtract), s)
            s = a(lambda: nc.scalar.activation(p[:, :, :], p[:, :, :], ACT.Exp), s)
            s = v(lambda: nc.vector.tensor_reduce(m[:, 1, :], p[:, :, :], AX_X, ALU.add), s)
            s = v(lambda: nc.vector.reciprocal(m[:, 1, :], m[:, 1, :]), s)
            s = v(lambda: nc.vector.tensor_tensor(p[:, :, :], p[:, :, :], over_e(m[:, 1, :]), ALU.mult), s)
            best, hot, s = top_two("ffn0", p[:, :, :], scope, s)
            s = v(lambda: nc.vector.tensor_tensor(m[:, 0, :], best[:, 0, :], best[:, 1, :], ALU.add), s)
            s = v(lambda: nc.vector.tensor_scalar(m[:, 0, :], m[:, 0, :], 1e-9, None, ALU.add), s)
            s = v(lambda: nc.vector.reciprocal(m[:, 0, :], m[:, 0, :]), s)
            for k in range(2):
                s = v(lambda: nc.vector.tensor_tensor(best[:, k, :], best[:, k, :], m[:, 0, :], ALU.mult), s)
            gT, gT_ready = gate_matrix("ffn0", best, hot, scope, s)
            sel_f = sb("expert_rows_f", [E, KH0, P], F32, scope)
            sel = sb("expert_rows_r", [E, KH0, P], F32R, scope)
            s = g(lambda: nc.gpsimd.memset(sel_f[:, :, :], 1.0))
            s = g(lambda: nc.gpsimd.affine_select(out=sel_f[:, :, :], in_=sel_f[:, :, :], compare_op=ALU.is_ge, fill=0.0,
                                                  base=0, pattern=[[P, KH0], [1, P]], channel_multiplier=-H0), s)
            s = g(lambda: nc.gpsimd.affine_select(out=sel_f[:, :, :], in_=sel_f[:, :, :], compare_op=ALU.is_ge, fill=0.0,
                                                  base=H0 - 1, pattern=[[-P, KH0], [-1, P]], channel_multiplier=H0), s)
            sel_ready = a(lambda: nc.scalar.activation(sel[:, :, :], sel_f[:, :, :], ACT.Copy), s)
            b1 = sb("ffn0_b1", [P, KH0], F32, scope)
            act.wait(load("ffn0_b1", b1[:, :], ins["ffn0_b1"]))
            b2 = sb("ffn0_b2", [E, D], F32, scope)
            b2p = (sb("ffn0_b2_hi", [E, D], F32R, scope), sb("ffn0_b2_lo", [E, D], F32R, scope))
            b2_ready = split(at(b2p, slice(None), slice(None)), b2[:, :], load("ffn0_b2", b2[:, :], ins["ffn0_b2"]))
            HALF_K = KH0 // 2
            hT = (sb("ffn0_hT_hi", [P, HALF_K, TP], F32R, scope), sb("ffn0_hT_lo", [P, HALF_K, TP], F32R, scope))
            tmp = sb("ffn0_tmp", [P, 2, 320], F32, scope)
            tmp_free, n_tmp = [None, None], 0
            s = v(lambda: nc.vector.memset(tmp[:, 0, :], 0.0))
            for k in range(HALF_K):
                s2 = split(at(hT, slice(None), k, slice(T + 1, TP)), tmp[:, 0, 0:TP - T - 1], s)
            tmp_free[0] = s2
            pe.wait(gT_ready, sel_ready)
            hT_read = None
            for kh in range(2):
                for c in range(2):
                    w, i, ready = take_weight("ffn0_w1", 2 * kh + c)
                    for mm in range(3):
                        hid = 6 * kh + 3 * c + mm
                        for c0, n in TOKEN_SPANS:
                            b, bank, free = banks.take()
                            pe.wait(free, ready)
                            got = product(bank[:, 0:n], [(at(w, slice(None), k, slice(mm * P, (mm + 1) * P)), at(xT, slice(None), k, slice(c0, c0 + n)))
                                                         for k in range(KD)])
                            bg, bankg, free = banks.take()
                            pe.wait(free)
                            gate_got = product_exact_a(bankg[:, 0:n], [(sel[:, hid, :], at(gT, slice(None), slice(c0, c0 + n)))])
                            part = tmp[:, n_tmp % 2, 0:n]
                            s = a(lambda: nc.scalar.activation(part, bank[:, 0:n], ACT.Gelu, bias=b1[:, hid:hid + 1]), got, tmp_free[n_tmp % 2])
                            banks.release(b, s)
                            s = v(lambda: nc.vector.tensor_tensor(part, part, bankg[:, 0:n], ALU.mult), s, gate_got)
                            banks.release(bg, s)
                            hT_ready = split(at(hT, slice(None), 3 * c + mm, slice(c0, c0 + n)), part, s, hT_read)
                            tmp_free[n_tmp % 2] = hT_ready
                            n_tmp += 1
                    drop_weight(i)
                for c in range(2):
                    w, i, ready = take_weight("ffn0_w2", 2 * kh + c)
                    pe.wait(ready, hT_ready, b2_ready)
                    cols = slice(c * HALF, (c + 1) * HALF)
                    for t in range(TT):
                        b, bank, free = banks.take()
                        pe.wait(free)
                        terms = [(at(hT, slice(None), k, tok(t)), at(w, slice(None), k, slice(None))) for k in range(HALF_K)]
                        if kh == 0:
                            terms.append((at(gT, slice(None), tok(t)), at(b2p, slice(None), cols)))
                        got = product(bank[:, 0:HALF], terms)
                        s = v(lambda: nc.vector.tensor_tensor(x[:, t, cols], x[:, t, cols], bank[:, 0:HALF], ALU.add), got)
                        banks.release(b, s)
                    drop_weight(i)
                hT_read = pe.last()
            phase_end()

        with ExitStack() as scope:
            xn = sb("xn2", [P, TT, D], F32, scope)
            xT_ready = transpose_in(xn, layer_norm(xn, dve.last()))
            phase_end()
        add_bias(("mix1_b", "gat_b2"))

        def kv1(which, kv, rows, after=None):
            if which is None:
                return sb("kv_exp", [P, TT, HALF], F32, rows)
            if which == 1:
                return after
            k, e = kv[:, :, 0, :], rows[:, :, :]
            s = v(lambda: nc.vector.tensor_scalar(e, k, 0.0, None, ALU.min), after, act.last())
            s = a(lambda: nc.scalar.activation(e, e, ACT.Exp), s)
            return v(lambda: nc.vector.scalar_tensor_tensor(k, k, 0.0, e, ALU.max, ALU.add), s)

        def q1(q, tmp, bank, got, b):
            s = v(lambda: nc.vector.tensor_scalar(tmp, bank, 0.0, None, ALU.min), got, act.last(), dve.last())
            s = a(lambda: nc.scalar.activation(tmp, tmp, ACT.Exp), s)
            s = v(lambda: nc.vector.scalar_tensor_tensor(q, bank, 0.0, tmp, ALU.max, ALU.add), s)
            banks.release(b, s)
            return s

        linear_attention("mix1", kv1, q1, True)

        gat = ExitStack()
        sel4_f = bias0[0:4, 0:4 * P].rearrange("p (a n) -> p a n", a=4)
        sel4 = sb("row_selector", [4, 4, P], F32R, gat)
        s = g(lambda: nc.gpsimd.memset(sel4_f[:, :, :], 0.0), dve.last())
        s = g(lambda: nc.gpsimd.affine_select(out=sel4_f[:, :, :], in_=sel4_f[:, :, :], compare_op=ALU.not_equal, fill=1.0,
                                              base=0, pattern=[[-1, 4], [0, P]], channel_multiplier=1), s)
        sel4_ready = a(lambda: nc.scalar.activation(sel4[:, :, :], sel4_f[:, :, :], ACT.Copy), s)
        no_edge = sb("no_edge", [P, TT, TP], mybir.dt.bfloat16, gat)
        with ExitStack() as scope:
            cf = sb("count_f", [P, TT, TP], F32, scope)
            s = v(lambda: nc.vector.tensor_copy(cf[:, :, :], count[:, :, :]))
            pe.wait(s)
            for t in range(TT):
                for k0, kn in ((0, 3), (3, 2)):
                    b, bank, free = banks.take()
                    pe.wait(free)
                    for k in range(kn):
                        end = nc.tensor.transpose(bank[:, k * P:(k + 1) * P], cf[:, k0 + k, tok(t)], ident[:, :])
                    s = v(lambda: nc.vector.tensor_scalar(no_edge[:, t, k0 * P:(k0 + kn) * P], bank[:, 0:kn * P], 0.0, NEG,
                                                          ALU.is_equal, ALU.mult), pe.done(end))
                    banks.release(b, s)
            phase_end()
        scores = sb("gat_scores", [P, TT, 4], F32, gat)
        peak = sb("gat_peak", [P, TT, 4], F32, gat)
        leak = sb("gat_leak", [P, TT, 4], F32, gat)
        rowT = (sb("gat_rowT_hi", [4, TP], F32R, gat), sb("gat_rowT_lo", [4, TP], F32R, gat))
        src_row = sb("gat_src_row", [P, TP], F32, gat)
        dst_row = sb("gat_dst_row", [P, TP], F32, gat)
        max_row = sb("gat_max_row", [P, TP], F32, gat)
        masked = sb("gat_masked", [P, TP], F32, gat)
        ESLOTS = 2
        edge_w = sb("gat_edge", [P, ESLOTS, TP], F32, gat)

        def rows_from_columns(cols, n, *after):
            pe.wait(*after)
            for t in range(TT):
                b, bank, free = banks.take()
                pe.wait(free)
                moved = pe.done(nc.tensor.transpose(bank[0:n, 0:P], cols[:, t, 0:n], ident[:, :]))
                s = split(at(rowT, slice(0, n), tok(t)), bank[0:n, 0:P], moved)
                banks.release(b, s)
            return s

        def spread_row(dst, n, j, *after):
            for c0 in (0, 320):
                b, bank, free = banks.take()
                pe.wait(free, sel4_ready, *after)
                got = product_exact_a(bank[:, 0:320], [(sel4[0:n, j, :], at(rowT, slice(0, n), slice(c0, c0 + 320)))])
                s = a(lambda: nc.scalar.activation(dst[:, c0:c0 + 320], bank[:, 0:320], ACT.Copy), got, dve.last(), pool.last())
                banks.release(b, s)
            return s

        def segment_peaks(heads, s):
            rows_ready = rows_from_columns(scores, 2 * heads, s)
            for h in range(heads):
                s = spread_row(src_row, 2 * heads, h, rows_ready)
                for t in range(TT):
                    s = v(lambda: nc.vector.tensor_tensor(masked[:, :], no_edge[:, t, :], src_row[:, :], ALU.add), s, act.last())
                    s = v(lambda: nc.vector.tensor_reduce(peak[:, t, h:h + 1], masked[:, :], AX_X, ALU.max), s)
            pk, lk = peak[:, :, 0:heads], leak[:, :, 0:heads]
            s = v(lambda: nc.vector.tensor_tensor(pk, pk, scores[:, :, heads:2 * heads], ALU.add), s)
            s = v(lambda: nc.vector.tensor_scalar(lk, pk, SLOPE, None, ALU.mult), s)
            return rows_ready, v(lambda: nc.vector.tensor_tensor(pk, pk, lk, ALU.max), s)

        state = {"n": 0, "free": [None] * ESLOTS}

        def edge_tile(t, heads, h, pair, rows_ready, *after):
            r = state["n"] % ESLOTS
            state["n"] += 1
            e = edge_w[:, r, :]
            s = a(lambda: nc.scalar.activation(e, dst_row[:, :], ACT.Identity, bias=scores[:, t, h:h + 1]), state["free"][r], rows_ready)
            s = v(lambda: nc.vector.scalar_tensor_tensor(e, e, SLOPE, e, ALU.mult, ALU.max), s)
            s = g(lambda: nc.gpsimd.tensor_tensor(e, e, max_row[:, :], ALU.subtract), s)
            s = g(lambda: nc.gpsimd.tensor_scalar(e, e, 0.0, None, ALU.min), s)
            s = a(lambda: nc.scalar.activation(e, e, ACT.Exp), s)
            s = v(lambda: nc.vector.tensor_tensor(e, e, count[:, t, :], ALU.mult), s)
            s = split(pair, e, s, *after)
            state["free"][r] = s
            return s

        h2 = sb("gat_h2", [P, TT, D], F32, gat)
        with ExitStack() as scope:
            hg = (sb("gat_h_hi", [P, TT, 2 * P], F32R, scope), sb("gat_h_lo", [P, TT, 2 * P], F32R, scope))
            att = sb("gat_att_rows", [P, 2, 2 * P], F32, scope)
            prod = sb("gat_prod", [P, 2, 2 * P], F32, scope)
            EX = 2
            ex = (sb("gat_ex_hi", [P, EX, TP], F32R, scope), sb("gat_ex_lo", [P, EX, TP], F32R, scope))
            ex_free = [None] * EX
            n_ex = 0
            zT = (sb("gat_zT_hi", [P, 2, TP], F32R, scope), sb("gat_zT_lo", [P, 2, TP], F32R, scope))
            zt = masked
            b1 = sb("gat_b1", [P, G1], F32, scope)
            act.wait(load("gat_b1", b1[:, :], ins["gat_b1"]))
            s = v(lambda: nc.vector.memset(zt[:, :], 0.0), dve.last())
            for j in range(2):
                s = split(at(zT, slice(None), j, slice(None)), zt[:, :], s)
            zT_read = None
            for grp in range(4):
                cols = slice(grp * 2 * P, (grp + 1) * 2 * P)
                att_free = dve.last()
                for n, name in enumerate(("gat_as1", "gat_ad1")):
                    att_ready = load(f"{name}_{grp}", att[:, n, :], ins[name][cols].rearrange("(a n) -> a n", a=1).broadcast_to([P, 2 * P]), att_free)
                    dve.wait(att_ready)
                w, i, ready = take_weight("gat_w1", grp)
                for t in range(TT):
                    b, bank, free = banks.take()
                    pe.wait(free, ready, *xT_ready)
                    got = product(bank[:, 0:2 * P], [(at(xT, slice(None), k, tok(t)), at(w, slice(None), k, slice(None))) for k in range(KD)])
                    split(at(hg, slice(None), t, slice(None)), bank[:, 0:2 * P], got)
                    for n in range(2):
                        s = v(lambda: nc.vector.tensor_tensor(prod[:, n, :], bank[:, 0:2 * P], att[:, n, :], ALU.mult), dve.last())
                    banks.release(b, s)
                    s = v(lambda: nc.vector.tensor_reduce(scores[:, t, :], prod[:, :, :].rearrange("p a (h c) -> p (a h) c", c=P), AX_X, ALU.add), s)
                drop_weight(i)
                rows_ready, s = segment_peaks(2, s)
                for h in range(2):
                    row = spread_row(dst_row, 4, 2 + h, rows_ready)
                    if h == 0:
                        keep = spread_row(src_row, 4, 3, rows_ready)
                        act.wait(pe.last())
                        dve.wait(pe.last())
                        peaks_ready = rows_from_columns(peak, 2, s)
                    else:
                        row = a(lambda: nc.scalar.activation(dst_row[:, :], src_row[:, :], ACT.Copy), act.last())
                    row = spread_row(max_row, 2, h, peaks_ready)
                    pool.wait(row)
                    open_banks = [banks.take() for _ in range(4)]
                    for t in range(TT):
                        r = n_ex % EX
                        n_ex += 1
                        pair = at(ex, slice(None), r, slice(None))
                        s = edge_tile(t, 2, h, pair, row, ex_free[r])
                        pe.wait(s)
                        for q, (c0, n) in enumerate(TOKEN_SPANS):
                            part = at(ex, slice(None), r, slice(c0, c0 + n))
                            if t == 0:
                                pe.wait(open_banks[q][2], open_banks[2 + q][2])
                            mm3(open_banks[q][1][:, 0:n], at(hg, slice(None), t, slice(h * P, (h + 1) * P)), part, t == 0, t == TT - 1)
                            nc.tensor.matmul(open_banks[2 + q][1][:, 0:n], ones[:, :], part[0], start=(t == 0), stop=False)
                            end = nc.tensor.matmul(open_banks[2 + q][1][:, 0:n], ones[:, :], part[1], start=False, stop=(t == TT - 1))
                        ex_free[r] = pe.done(end)
                    for q, (c0, n) in enumerate(TOKEN_SPANS):
                        z = zt[:, c0:c0 + n]
                        s = v(lambda: nc.vector.tensor_scalar(z, open_banks[2 + q][1][:, 0:n], 1e-16, None, ALU.add), ex_free[r], act.last(), dve.last())
                        banks.release(open_banks[2 + q][0], s)
                        s = v(lambda: nc.vector.reciprocal(z, z), s)
                        s = v(lambda: nc.vector.tensor_tensor(z, z, open_banks[q][1][:, 0:n], ALU.mult), s)
                        banks.release(open_banks[q][0], s)
                        s = a(lambda: nc.scalar.activation(z, z, ACT.Relu, bias=b1[:, 2 * grp + h:2 * grp + h + 1]), s)
                        s = split(at(zT, slice(None), h, slice(c0, c0 + n)), z, s, zT_read)
                w, i, ready = take_weight("gat_w2", grp)
                for c in range(2):
                    for t in range(TT):
                        b, bank, free = banks.take()
                        pe.wait(free, ready, s)
                        got = product(bank[:, 0:HALF], [(at(zT, slice(None), k, tok(t)), at(w, slice(None), k, slice(c * HALF, (c + 1) * HALF))) for k in range(2)])
                        o = h2[:, t, c * HALF:(c + 1) * HALF]
                        if grp == 0:
                            s2 = v(lambda: nc.vector.tensor_copy(o, bank[:, 0:HALF]), got)
                        else:
                            s2 = v(lambda: nc.vector.tensor_tensor(o, o, bank[:, 0:HALF], ALU.add), got, h2_done)
                        banks.release(b, s2)
                h2_done = s2
                zT_read = pe.last()
                drop_weight(i)
            phase_end()

        with ExitStack() as scope:
            hp = (sb("gat2_h_hi", [P, TT, D], F32R, scope), sb("gat2_h_lo", [P, TT, D], F32R, scope))
            att = bias0
            prod = sb("gat2_prod", [P, D], F32, scope)
            h_ready = split(at(hp, slice(None), slice(None), slice(None)), h2[:, :, :])
            for n, name in enumerate(("gat_as2", "gat_ad2")):
                dve.wait(row_load(name, att[:, :], ins[name], D, dve.last()))
                for t in range(TT):
                    s = v(lambda: nc.vector.tensor_tensor(prod[:, :], h2[:, t, :], att[:, :], ALU.mult), dve.last())
                    s = v(lambda: nc.vector.tensor_reduce(scores[:, t, n:n + 1], prod[:, :], AX_X, ALU.add), s)
            rows_ready, s = segment_peaks(1, s)
            row = spread_row(dst_row, 2, 1, rows_ready)
            act.wait(pe.last())
            dve.wait(pe.last())
            row = spread_row(max_row, 1, 0, rows_from_columns(peak, 1, s))
            pool.wait(row)
            for t in range(TT):
                s = edge_tile(t, 1, 0, at(xT, slice(None), t, slice(None)), row)
            inverse = sb("gat2_inverse", [P, TT], F32, scope)
            pe.wait(s, h_ready)
            for t in range(TT):
                b, bank, free = banks.take()
                pe.wait(free)
                for k in range(TT):
                    nc.tensor.matmul(bank[:, 0:2], xT[0][:, k, tok(t)], ones[:, 0:2], start=(k == 0), stop=False)
                    end = nc.tensor.matmul(bank[:, 0:2], xT[1][:, k, tok(t)], ones[:, 0:2], start=False, stop=(k == TT - 1))
                s = v(lambda: nc.vector.tensor_scalar(inverse[:, t:t + 1], bank[:, 0:1], 1e-16, None, ALU.add), pe.done(end))
                banks.release(b, s)
                s = v(lambda: nc.vector.reciprocal(inverse[:, t:t + 1], inverse[:, t:t + 1]), s)
                for c in range(2):
                    b, bank, free = banks.take()
                    pe.wait(free)
                    got = product(bank[:, 0:HALF], [(at(xT, slice(None), k, tok(t)), at(hp, slice(None), k, slice(c * HALF, (c + 1) * HALF)))
                                                    for k in range(TT)])
                    o = x[:, t, c * HALF:(c + 1) * HALF]
                    s = v(lambda: nc.vector.scalar_tensor_tensor(o, bank[:, 0:HALF], inverse[:, t:t + 1], o, ALU.mult, ALU.add), got, s)
                    banks.release(b, s)
            phase_end()
        gat.close()

        moe = ExitStack()
        slot_row = sb("slot_row", [P, 2, TT], U32, moe)
        slot_token = sb("slot_token", [P, E * MAIN], U32, moe)
        extra_token = sb("extra_token", [P, E * EXTRA], U32, moe)
        overflow = sb("overflow", [P, E * EXTRA], I32, moe)
        any_overflow = sb("any_overflow", [P, 1], I32, moe)
        weights2 = sb("gate_weights", [P, 2, TT], F32, moe)
        with ExitStack() as scope:
            xn = sb("xn3", [P, TT, D], F32, scope)
            xn_ready = layer_norm(xn, dve.last())
            xT_ready = transpose_in(xn, xn_ready)
            xn_stored = (sem("xn_stored"), 16)
            act.wait(xn_ready[-1])
            act.engine.dma_start(slots_dram.rearrange("(t p) d -> p t d", p=P), xn[:, :, :]).then_inc(xn_stored[0], 16)
            stores.append(xn_stored)
            logits = sb("ffn1_logits", [P, TT, E], F32, scope)
            s = router_logits("ffn1_gate", logits, scope)
            best, hot, s = top_two("ffn1", logits[:, :, :], scope, s)
            s = v(lambda: nc.vector.tensor_tensor(weights2[:, 1, :], best[:, 1, :], best[:, 0, :], ALU.subtract), s)
            s = a(lambda: nc.scalar.activation(weights2[:, 1, :], weights2[:, 1, :], ACT.Exp), s)
            s = v(lambda: nc.vector.tensor_scalar(weights2[:, 0, :], weights2[:, 1, :], 1.0, None, ALU.add), s)
            s = v(lambda: nc.vector.reciprocal(weights2[:, 0, :], weights2[:, 0, :]), s)
            s = v(lambda: nc.vector.tensor_tensor(weights2[:, 1, :], weights2[:, 1, :], weights2[:, 0, :], ALU.mult), s)
            gT, gT_ready = gate_matrix("ffn1", weights2, hot, scope, s)
            b2 = sb("ffn1_b2", [E, D], F32, scope)
            b2p = (sb("ffn1_b2_hi", [E, D], F32R, scope), sb("ffn1_b2_lo", [E, D], F32R, scope))
            b2_ready = split(at(b2p, slice(None), slice(None)), b2[:, :], load("ffn1_b2", b2[:, :], ins["ffn1_b2"]))
            pe.wait(b2_ready, gT_ready)
            add_bias(("shared_b2",), 0.1 * 2)
            for t in range(TT):
                for c in range(2):
                    cols = slice(c * HALF, (c + 1) * HALF)
                    b, bank, free = banks.take()
                    pe.wait(free)
                    got = product(bank[:, 0:HALF], [(at(gT, slice(None), tok(t)), at(b2p, slice(None), cols))])
                    s = v(lambda: nc.vector.tensor_tensor(x[:, t, cols], x[:, t, cols], bank[:, 0:HALF], ALU.add), got, dve.last())
                    banks.release(b, s)
            chosen_f = sb("chosen_f", [P, TT, E], F32, scope)
            chosen = sb("chosen", [P, TT, E], F32R, scope)
            before_f = sb("before_f", [P, P], F32, scope)
            before = sb("before", [P, P], F32R, scope)
            s = g(lambda: nc.gpsimd.affine_select(out=before_f[:, :], in_=ones_f[:, :], compare_op=ALU.is_ge, fill=0.0,
                                                  base=-1, pattern=[[1, P]], channel_multiplier=-1))
            before_ready = a(lambda: nc.scalar.activation(before[:, :], before_f[:, :], ACT.Copy), s)
            s = v(lambda: nc.vector.tensor_tensor(chosen_f[:, :, :], hot[:, 0, :, :], hot[:, 1, :, :], ALU.add), dve.last())
            s = g(lambda: nc.gpsimd.affine_select(out=chosen_f[:, TT - 1, :], in_=chosen_f[:, TT - 1, :], compare_op=ALU.is_ge,
                                                  fill=0.0, base=LAST - 1, pattern=[[0, E]], channel_multiplier=-1), s)
            chosen_ready = a(lambda: nc.scalar.activation(chosen[:, :, :], chosen_f[:, :, :], ACT.Copy), s)
            rank = sb("rank", [P, TT, E], F32, scope)
            pe.wait(before_ready, chosen_ready)
            for t in range(TT):
                b, bank, free = banks.take()
                pe.wait(free)
                for k in range(t):
                    nc.tensor.matmul(bank[:, 0:E], ones[:, :], chosen[:, k, :], start=(k == 0), stop=False)
                got = pe.done(nc.tensor.matmul(bank[:, 0:E], before[:, :], chosen[:, t, :], start=(t == 0), stop=True))
                rank_ready = v(lambda: nc.vector.tensor_copy(rank[:, t, :], bank[:, 0:E]), got)
                banks.release(b, rank_ready)
            b, bank, free = banks.take()
            pe.wait(free)
            for k in range(TT):
                end = nc.tensor.matmul(bank[:, 0:E], ones[:, :], chosen[:, k, :], start=(k == 0), stop=(k == TT - 1))
            total = sb("tokens_of_expert", [P, E], F32, scope)
            s = v(lambda: nc.vector.tensor_copy(total[:, :], bank[:, 0:E]), pe.done(end))
            banks.release(b, s)
            most = sb("most_tokens", [P, 1], F32, scope)
            tiles = overflow[:, :].rearrange("p (e n) -> p e n", n=EXTRA)
            for n in range(EXTRA):
                v(lambda: nc.vector.tensor_scalar(tiles[:, :, n], total[:, :], float(CAP + n * P), None, ALU.is_gt), s)
            s = v(lambda: nc.vector.tensor_reduce(most[:, :], total[:, :], AX_X, ALU.max), s)
            v(lambda: nc.vector.tensor_scalar(any_overflow[:, :], most[:, :], float(CAP), None, ALU.is_gt), s)
            row_e = sb("row_of_expert", [P, TT, E], F32, scope)
            picked = sb("picked_row", [P, 2, TT, E], F32, scope)
            row_f = sb("picked_row_f", [P, 2, TT], F32, scope)
            shift = sb("overflow_shift", [P, TT, E], F32, scope)
            over = sb("beyond_first_pass", [P, TT, E], F32, scope)
            v(lambda: nc.vector.scalar_tensor_tensor(row_e[:, :, :], iota8[:, :, :], float(CAP), rank[:, :, :], ALU.mult, ALU.add), rank_ready)
            v(lambda: nc.vector.tensor_scalar(shift[:, :, :], iota8[:, :, :], float(EXTRA * P - CAP), float((E - 1) * CAP), ALU.mult, ALU.add))
            s = v(lambda: nc.vector.tensor_scalar(over[:, :, :], rank[:, :, :], float(CAP), None, ALU.is_ge))
            s = v(lambda: nc.vector.tensor_tensor(shift[:, :, :], shift[:, :, :], over[:, :, :], ALU.mult), s)
            s = v(lambda: nc.vector.tensor_tensor(row_e[:, :, :], row_e[:, :, :], shift[:, :, :], ALU.add), s)
            for k in range(2):
                s = v(lambda: nc.vector.tensor_tensor(picked[:, k, :, :], hot[:, k, :, :], row_e[:, :, :], ALU.mult), s)
                s = v(lambda: nc.vector.tensor_reduce(row_f[:, k, :], picked[:, k, :, :], AX_X, ALU.add), s)
            rows_done = v(lambda: nc.vector.tensor_copy(slot_row[:, :, :], row_f[:, :, :]), s)
            here = sb("rank_or_none", [P, TT, E], F32, scope)
            s = v(lambda: nc.vector.tensor_scalar(here[:, :, :], rank[:, :, :], 1.0, None, ALU.add), rank_ready)
            s = v(lambda: nc.vector.tensor_tensor(here[:, :, :], here[:, :, :], chosen_f[:, :, :], ALU.mult), s, chosen_ready)
            s = v(lambda: nc.vector.tensor_scalar(here[:, :, :], here[:, :, :], -1.0, None, ALU.add), s)
            number_i = sb("token_number_int", [P, TT], I32, scope)
            number = sb("token_number", [P, TT], F16, scope)
            s2 = g(lambda: nc.gpsimd.iota(number_i[:, :], [[P, TT]], base=0, channel_multiplier=1))
            s2 = g(lambda: nc.gpsimd.tensor_copy(number[:, :], number_i[:, :]), s2)
            hot_slot = sb("one_hot_slot", [P, 2, TT, TP], F16, scope)
            hot_free = [None, None]
            dve.wait(s)
            pe.wait(s2)
            b, bank, free = banks.take()
            pe.wait(free)
            for e in range(E):
                dve.wait(hot_free[e % 2])
                for t in range(TT):
                    s = v(lambda: nc.vector.tensor_scalar(hot_slot[:, e % 2, t, :], iota_h[:, :], here[:, t, e:e + 1], None, ALU.is_equal))
                pe.wait(s)
                for st in range(TT):
                    for t in range(TT):
                        end = nc.tensor.matmul(bank[:, e * TT + st:e * TT + st + 1], hot_slot[:, e % 2, t, tok(st)], number[:, t:t + 1],
                                               start=(t == 0), stop=(t == TT - 1))
                hot_free[e % 2] = pe.done(end)
            by_tile = bank[:, 0:E * TT].rearrange("p (e n) -> p e n", n=TT)
            tokens_done = v(lambda: nc.vector.tensor_copy(slot_token[:, :].rearrange("p (e n) -> p e n", n=MAIN), by_tile[:, :, 0:MAIN]), hot_free[1])
            v(lambda: nc.vector.tensor_copy(extra_token[:, :].rearrange("p (e n) -> p e n", n=EXTRA), by_tile[:, :, MAIN:TT]))
            banks.release(b, tokens_done)
            phase_end()

        xg = sb("gathered", [P, 2, 2, D], F32, moe)
        xe = (sb("slots_T_hi", [P, 2, KD, 2 * P], F32R, moe), sb("slots_T_lo", [P, 2, KD, 2 * P], F32R, moe))
        hT = (sb("ffn1_hT_hi", [P, 2, 3, 2 * P], F32R, moe), sb("ffn1_hT_lo", [P, 2, 3, 2 * P], F32R, moe))
        ht = sb("ffn1_tmp", [P, 2, 2 * P], F32, moe)
        yt = sb("ffn1_y", [P, 2, 2, D], F32, moe)
        b1e = sb("ffn1_b1", [P, E, H1 // P], F32, moe)
        b1s = sb("shared_b1", [P, H1 // P], F32, moe)
        act.wait(load("ffn1_b1", b1e[:, :, :], ins["ffn1_b1"]), load("shared_b1", b1s[:, :], ins["shared_b1"]))
        y_banks = psum[4:8]
        y_free = None
        banks = Banks(psum[0:4])
        gather_sem = [sem(f"gathered{n}") for n in range(2)]
        store_sem = [sem(f"rows_stored{n}") for n in range(2)]
        gathers, row_stores = [0, 0], [0, 0]
        state = {"xg_free": [None, None], "xe_read": [None, None], "yt_free": [None, None], "h_read": [None, None], "tmp": [None, None], "n": 0}

        def tiles_of(who, grp):
            return [t for t in (2 * grp, 2 * grp + 1) if t < TT] if who == "shared" else list(range(MAIN))

        def gather(r, e, grp):
            pool.wait(xn_stored, tokens_done, state["xg_free"][r])
            for n, st in enumerate(tiles_of(e, grp)):
                j = e * MAIN + st
                nc.gpsimd.indirect_dma_start(xg[:, r, n, :], None, slots_dram[:, :],
                                             bass.IndirectOffsetOnAxis(ap=slot_token[:, j:j + 1], axis=0)).then_inc(gather_sem[r], 16)
                gathers[r] += 16
            return (gather_sem[r], gathers[r])

        def turn(r, grp, arrived):
            pe.wait(arrived)
            for n, st in enumerate(tiles_of(0, grp)):
                for c in range(2):
                    i, bank, free = banks.take()
                    pe.wait(free)
                    for k in range(3):
                        end = nc.tensor.transpose(bank[:, k * P:(k + 1) * P], xg[:, r, n, (3 * c + k) * P:(3 * c + k + 1) * P], ident[:, :])
                    moved = pe.done(end)
                    s = split(at(xe, slice(None), r, slice(3 * c, 3 * c + 3), slice(n * P, (n + 1) * P)),
                              bank[:, 0:3 * P].rearrange("p (k n) -> p k n", k=3), moved, state["xe_read"][r])
                    banks.release(i, s)
            state["xg_free"][r] = moved
            return s

        expert_passes = [p for p in passes if p[0] != "shared"]
        arrived, turned = {}, {}

        def prepare(n):
            if n < len(expert_passes):
                arrived[n] = gather(n % 2, *expert_passes[n])

        def run_pass(who, grp, source, ready, bias, after_first_chunk):
            nonlocal y_free
            st = tiles_of(who, grp)
            width = P * len(st)

            def hidden(c):
                w, i, w_ready = take_weight("ffn1_w1", who, c)
                pe.wait(w_ready, *ready)
                for m in range(3):
                    b, bank, free = banks.take()
                    pe.wait(free)
                    got = product(bank[:, 0:width], [(at(w, slice(None), k, slice(m * P, (m + 1) * P)), source(k, width)) for k in range(KD)])
                    n = state["n"]
                    state["n"] += 1
                    part = ht[:, n % 2, 0:width]
                    col = 3 * c + m
                    s = a(lambda: nc.scalar.activation(part, bank[:, 0:width], ACT.Relu, bias=bias(col)), got, state["tmp"][n % 2])
                    banks.release(b, s)
                    s = split(at(hT, slice(None), c % 2, m, slice(0, width)), part, s, state["h_read"][c % 2])
                    state["tmp"][n % 2] = s
                drop_weight(i)
                return s

            def output(c, h_ready):
                w, i, w_ready = take_weight("ffn1_w2", who, c)
                pe.wait(w_ready, h_ready)
                if c == 0:
                    pe.wait(y_free)
                for n in range(len(st)):
                    for half in range(2):
                        got = product(y_banks[2 * n + half][:, 0:HALF],
                                      [(at(hT, slice(None), c % 2, k, tok(n)), at(w, slice(None), k, slice(half * HALF, (half + 1) * HALF)))
                                       for k in range(3)], first=(c == 0), last=(c == NCH - 1))
                state["h_read"][c % 2] = got
                drop_weight(i)
                return got

            h_ready = {}
            for c in range(NCH + 1):
                if c < NCH:
                    h_ready[c] = hidden(c)
                if c == 1:
                    after_first_chunk()
                if c > 0:
                    y_done = output(c - 1, h_ready[c - 1])
            if who == "shared":
                for n, t in enumerate(st):
                    for half in range(2):
                        o = x[:, t, half * HALF:(half + 1) * HALF]
                        y_free = v(lambda: nc.vector.scalar_tensor_tensor(o, y_banks[2 * n + half][:, 0:HALF], 0.1 * 2, o, ALU.mult, ALU.add), y_done)
                return
            r = state["n_store"] % 2
            state["n_store"] += 1
            act.wait(y_done, state["yt_free"][r])
            for n, t in enumerate(st):
                for half in range(2):
                    y_free = a(lambda: nc.scalar.activation(yt[:, r, n, half * HALF:(half + 1) * HALF], y_banks[2 * n + half][:, 0:HALF], ACT.Copy))
            pool.wait(y_free)
            row0 = who * CAP
            nc.gpsimd.dma_start(result_dram[row0:row0 + width, :].rearrange("(t p) d -> p t d", p=P), yt[:, r, 0:len(st), :]).then_inc(store_sem[r], 16)
            row_stores[r] += 16
            state["yt_free"][r] = (store_sem[r], row_stores[r])

        state["n_store"] = 0
        n_expert = 0
        prepare(0)
        for n_pass, (who, grp) in enumerate(passes):
            def between():
                if n_expert_next in arrived:
                    expert, group = expert_passes[n_expert_next]
                    turned[n_expert_next] = turn(n_expert_next % 2, group, arrived[n_expert_next])
                    prepare(n_expert_next + 1)
            if who == "shared":
                n_expert_next = 0 if n_pass == 2 else -1
                cols = slice(2 * grp * P, None)
                run_pass(who, grp, lambda k, width: at(xT, slice(None), k, slice(2 * grp * P, 2 * grp * P + width)), tuple(xT_ready),
                         lambda col: b1s[:, col:col + 1], between)
            else:
                n_expert_next = n_expert + 1
                r = n_expert % 2
                run_pass(who, grp, lambda k, width: at(xe, slice(None), r, k, slice(0, width)), (turned[n_expert],),
                         lambda col: b1e[:, who, col:col + 1], between)
                state["xe_read"][r] = pe.last()
                n_expert += 1
        phase_end()
        stored = [(store_sem[r], row_stores[r]) for r in range(2)]

        spill_sems = [sem("spill_" + name) for name in ("pe", "act", "dve", "gather", "bias", "w0", "w1", "store")]
        numbers = [x_.num for x_ in spill_sems]
        assert numbers == list(range(numbers[0], numbers[0] + len(numbers)))
        (s_pe, s_act, s_dve, s_gather, s_bias, s_w0, s_w1, s_store) = spill_sems
        pool.wait(*stored)
        extra_rows = result_dram[E * CAP:E * TP, :].rearrange("(n p) d -> n p d", p=P)

        def overflow_tile(e, i):
            q_pe, q_act, q_dve = Queue(nc.tensor, s_pe), Queue(nc.scalar, s_act), Queue(nc.vector, s_dve)
            index = sb("spill_index", [P, 1], U32, spill)
            bias = sb("spill_b1", [P, H1 // P], F32, spill)
            nc.sync.dma_start(bias[:, :].unsqueeze(1), ins["ffn1_b1"][:, bass.ds(e, 1), :]).then_inc(s_bias, 16)
            index_ready = q_dve.done(nc.vector.tensor_copy(index[:, :], extra_token[:, bass.ds(i, 1)]))
            nc.gpsimd.wait_ge(*index_ready)
            nc.gpsimd.indirect_dma_start(xg[:, 0, 0, :], None, slots_dram[:, :],
                                         bass.IndirectOffsetOnAxis(ap=index[:, :], axis=0)).then_inc(s_gather, 16)
            q_pe.wait((s_gather, 16))
            for c in range(2):
                for k in range(3):
                    end = nc.tensor.transpose(psum[c][:, k * P:(k + 1) * P], xg[:, 0, 0, (3 * c + k) * P:(3 * c + k + 1) * P], ident[:, :])
                turned_now = q_pe.done(end)
                q_act.wait(turned_now)
                src = psum[c][:, 0:3 * P].rearrange("p (k n) -> p k n", k=3)
                hi = q_act.done(nc.scalar.activation(xe[0][:, 0, 3 * c:3 * c + 3, 0:P], src, ACT.Copy))
                q_dve.wait(hi, turned_now)
                x_ready = q_dve.done(nc.vector.tensor_tensor(xe[1][:, 0, 3 * c:3 * c + 3, 0:P], src,
                                                             xe[0][:, 0, 3 * c:3 * c + 3, 0:P].bitcast(F32), ALU.subtract))
            q_act.wait((s_bias, 16))
            w_read = x_ready
            for c in range(NCH):
                for n, (name, sem_w) in enumerate((("ffn1_w1", s_w0), ("ffn1_w2", s_w1))):
                    nc.sync.wait_ge(*w_read)
                    nc.sync.dma_start(raw[:, n:n + 1, :],
                                      ins[name][bass.ds(e * NCH + c, 1), :, :].rearrange("a p n -> p a n")).then_inc(sem_w, 16)
                for n, sem_w in enumerate((s_w0, s_w1)):
                    q_act.wait((sem_w, 16 * (c + 1)), w_read)
                    hi = q_act.done(nc.scalar.activation(whi[:, n, :], raw[:, n, :], ACT.Copy))
                    q_dve.wait(hi, (sem_w, 16 * (c + 1)), w_read)
                    split_done = q_dve.done(nc.vector.tensor_tensor(wlo[:, n, :], raw[:, n, :], whi[:, n, :].bitcast(F32), ALU.subtract))
                w1 = [w_[:, 0, :].rearrange("p (k n) -> p k n", k=KD) for w_ in (whi, wlo)]
                w2 = [w_[:, 1, :].rearrange("p (k n) -> p k n", k=3) for w_ in (whi, wlo)]
                q_pe.wait(split_done, x_ready)
                for m in range(3):
                    for k in range(KD):
                        end = mm3(psum[m][:, 0:P], at(w1, slice(None), k, slice(m * P, (m + 1) * P)), at(xe, slice(None), 0, k, slice(0, P)),
                                  k == 0, k == KD - 1)
                    got = q_pe.done(end)
                    q_act.wait(got, q_dve.last())
                    s_ = q_act.done(nc.scalar.activation(ht[:, 0, 0:P], psum[m][:, 0:P], ACT.Relu, bias=bias[:, 3 * c + m:3 * c + m + 1]))
                    q_act.wait(s_)
                    hi = q_act.done(nc.scalar.activation(hT[0][:, 0, m, 0:P], ht[:, 0, 0:P], ACT.Copy))
                    q_dve.wait(hi)
                    h_ready = q_dve.done(nc.vector.tensor_tensor(hT[1][:, 0, m, 0:P], ht[:, 0, 0:P], hT[0][:, 0, m, 0:P].bitcast(F32), ALU.subtract))
                q_pe.wait(h_ready)
                for half in range(2):
                    for k in range(3):
                        end = mm3(y_banks[half][:, 0:HALF], at(hT, slice(None), 0, k, slice(0, P)),
                                  at(w2, slice(None), k, slice(half * HALF, (half + 1) * HALF)),
                                  c == 0 and k == 0, c == NCH - 1 and k == 2)
                w_read = q_pe.done(end)
            q_act.wait(w_read)
            for half in range(2):
                y_kept = q_act.done(nc.scalar.activation(yt[:, 0, 0, half * HALF:(half + 1) * HALF], y_banks[half][:, 0:HALF], ACT.Copy))
            nc.sync.wait_ge(*y_kept)
            nc.sync.dma_start(extra_rows[bass.ds(i, 1), :, :].rearrange("a p d -> p a d"), yt[:, 0, 0:1, :]).then_inc(s_store, 16)
            nc.sync.wait_ge(s_store, 16)
            nc.gpsimd.wait_ge(s_gather, 16)
            nc.gpsimd.dma_reset(range(s_gather.num, s_gather.num + 1))
            nc.all_engine_barrier(sems_to_clear=range(numbers[0], numbers[0] + len(numbers)))

        with ExitStack() as spill:
            some = nc.values_load(any_overflow[0:1, 0:1], min_val=0, max_val=1)
            with nc.If(some > 0):
                with nc.Fori(0, E) as expert:
                    with nc.Fori(0, EXTRA) as extra:
                        number_ = nc.snap(expert * EXTRA + extra, min_val=0, max_val=E * EXTRA - 1)
                        used = nc.values_load(overflow[0:1, bass.ds(number_, 1)], min_val=0, max_val=1)
                        with nc.If(used > 0):
                            overflow_tile(expert, number_)
        moe_rows = xg[:, :, :, :].rearrange("p a b d -> p (a b) d")

        o_sem = sem("out_stored")
        pool.wait(rows_done, *stored)
        row_sem = [sem(f"row_back{n}") for n in range(4)]
        out_free = [None] * 4
        for t in range(TT):
            n = P if t < TT - 1 else LAST
            for k in range(2):
                i = 2 * t + k
                r = i % 4
                pool.wait(out_free[r])
                nc.gpsimd.indirect_dma_start(moe_rows[0:n, r, :], None, result_dram[:, :],
                                             bass.IndirectOffsetOnAxis(ap=slot_row[0:n, k, t:t + 1], axis=0)).then_inc(row_sem[r], 16)
                s = v(lambda: nc.vector.scalar_tensor_tensor(x[0:n, t, :], moe_rows[0:n, r, :], weights2[0:n, k, t:t + 1], x[0:n, t, :],
                                                             ALU.mult, ALU.add), (row_sem[r], 16 * (i // 4 + 1)), dve.last())
                out_free[r] = s
            sp.wait(s)
            sp.engine.dma_start(out[t * P:t * P + n, :], x[0:n, t, :]).then_inc(o_sem, 16)
        stores.append((o_sem, 16 * TT))
        sp.wait(*stores, *stored)
        moe.close()


def _columns(w, n, k=KD):
    c = w.shape[1] // n
    return w.reshape(k, P, n, c).transpose(2, 1, 0, 3).reshape(n, P, k * c)


def _rows(w, k):
    return w.reshape(-1, k, P, w.shape[1]).transpose(0, 2, 1, 3).reshape(-1, P, k * w.shape[1])


def kernel(**inputs):
    import numpy as np
    import concourse.bacc as bacc
    from concourse.bass_utils import run_bass_kernel_spmd

    i = {name: np.asarray(value) for name, value in inputs.items()}
    w_map = i["L0_mix_w_map"].T
    qkv = i["L1_mix_w_qkv"]

    def kv_chunks(w):
        k, v = _columns(w[:, D:2 * D], 2), _columns(w[:, 2 * D:], 2)
        return np.stack([k, v], 1).reshape(4, P, WC)

    arrays = {
        "x": i["x"], "src": i["src"].reshape(EP, EC), "dst": i["dst"].reshape(EP, EC),
        "gnn0_w1": _columns(i["L0_gnn_W1"], 2), "gnn0_w2": _columns(i["L0_gnn_W2"], 2),
        "gnn0_b1": i["L0_gnn_b1"].reshape(KD, P).T, "gnn0_b2": i["L0_gnn_b2"],
        "mix0_q": _columns(w_map[:, 0:D], 2), "mix0_kv": kv_chunks(w_map), "mix0_out": _rows(i["L0_mix_w_out"].T, 3),
        "mix0_gk": i["L0_mix_g_k"], "mix0_bk": i["L0_mix_b_k"], "mix0_gv": i["L0_mix_g_v"], "mix0_bv": i["L0_mix_b_v"],
        "mix0_b": i["L0_mix_b_out"],
        "ffn0_gate": i["L0_ffn_gate_w"].reshape(E, KD, P).transpose(2, 1, 0),
        "ffn0_w1": _columns(i["L0_ffn_w1"].transpose(1, 0, 2).reshape(D, E * H0), 4),
        "ffn0_b1": i["L0_ffn_b1"].reshape(KH0, P).T,
        "ffn0_w2": np.concatenate([_columns(w, 2) for w in i["L0_ffn_w2"].reshape(2, D, D)]), "ffn0_b2": i["L0_ffn_b2"],
        "gat_w1": _columns(i["L1_gnn_W1"].T, 4), "gat_as1": i["L1_gnn_att_src1"].reshape(-1),
        "gat_ad1": i["L1_gnn_att_dst1"].reshape(-1), "gat_b1": i["L1_gnn_b1"].reshape(G1, P).T,
        "gat_w2": _rows(i["L1_gnn_W2"].T, 2), "gat_as2": i["L1_gnn_att_src2"].reshape(-1),
        "gat_ad2": i["L1_gnn_att_dst2"].reshape(-1), "gat_b2": i["L1_gnn_b2"],
        "mix1_q": _columns(qkv[:, 0:D], 2), "mix1_kv": kv_chunks(qkv), "mix1_out": _rows(i["L1_mix_w_proj"], 3),
        "mix1_b": i["L1_mix_b_proj"],
        "ffn1_gate": i["L1_ffn_Wr"].reshape(E, KD, P).transpose(2, 1, 0),
        "ffn1_w1": np.concatenate([_columns(w.T, NCH) for w in i["L1_ffn_W1"]]),
        "ffn1_w2": np.concatenate([_rows(w.T, 3) for w in i["L1_ffn_W2"]]),
        "ffn1_b1": i["L1_ffn_b1"].reshape(E, H1 // P, P).transpose(2, 0, 1), "ffn1_b2": i["L1_ffn_b2"],
        "shared_w1": _columns(i["L1_ffn_sW1"].T, NCH), "shared_w2": _rows(i["L1_ffn_sW2"].T, 3),
        "shared_b1": i["L1_ffn_sb1"].reshape(H1 // P, P).T, "shared_b2": i["L1_ffn_sb2"],
    }
    nc = bacc.Bacc("TRN2", target_bir_lowering=False, num_devices=1)
    arrays = {name: np.ascontiguousarray(value) for name, value in arrays.items()}
    aps = {name: nc.dram_tensor("in_" + name, value.shape, mybir.dt.from_np(value.dtype), kind="ExternalInput").ap()
           for name, value in arrays.items()}
    out = nc.dram_tensor("out", (T, D), F32, kind="ExternalOutput").ap()
    slots = nc.dram_tensor("tokens_normed", (TP, D), F32, kind="Internal").ap()
    result = nc.dram_tensor("expert_rows", (E * TP, D), F32, kind="Internal").ap()
    build(nc, aps, out, slots, result)
    run = run_bass_kernel_spmd(nc, [{"in_" + name: value for name, value in arrays.items()}], core_ids=[0])
    return run.results[0]["out"]
```

```python
from contextlib import ExitStack

import concourse.bass as bass
from concourse import mybir

F32 = mybir.dt.float32
F32R = mybir.dt.float32r
F16 = mybir.dt.float16
I32 = mybir.dt.int32
U32 = mybir.dt.uint32
ACT = mybir.ActivationFunctionType
ALU = mybir.AluOpType
AX_X = mybir.AxisListType.X

P = 128
T = 625
TT = (T + P - 1) // P
TP = TT * P
LAST = T - (TT - 1) * P
D = 768
KD = D // P
HALF = D // 2
NE = 20000
EP = 125
EC = NE // EP
TM = T // 2 + 1
PACK = 4096
CHUNK_E = 32
assert CHUNK_E * EP < PACK and EC % CHUNK_E == 0 and PACK * CHUNK_E * EP < 2 ** 24
HEADS = 12
DH = 64
PAIRS = HEADS // 2
E = 8
H0 = 192
KH0 = E * H0 // P
G1 = 8
C1 = G1 * P
H1 = 3072
WC = KD * HALF
NCH = H1 // HALF
MAIN = 2
CAP = MAIN * P
EXTRA = TT - MAIN
NEG = -1.0e30
LN_EPS = 1e-5
SLOPE = 0.2
TOKEN_SPANS = [(0, 320), (320, 306)]


class Queue:

    def __init__(self, engine, semaphore):
        self.engine, self.semaphore, self.count, self.seen = engine, semaphore, 0, {}

    def wait(self, *tokens):
        for token in tokens:
            if token is None:
                continue
            semaphore, value = token
            if self.seen.get(semaphore.name, 0) < value:
                self.engine.wait_ge(semaphore, value)
                self.seen[semaphore.name] = value

    def done(self, instruction):
        self.count += 1
        instruction.then_inc(self.semaphore, 1)
        return (self.semaphore, self.count)

    def last(self):
        return (self.semaphore, self.count) if self.count else None


class Banks:

    def __init__(self, banks):
        self.banks, self.free, self.at = banks, [None] * len(banks), 0

    def take(self):
        i = self.at % len(self.banks)
        self.at += 1
        return i, self.banks[i], self.free[i]

    def release(self, i, token):
        self.free[i] = token


def build(nc, ins, out, slots_dram, result_dram):
    with ExitStack() as ctx:
        def sb(name, shape, dt=F32, scope=None):
            return (scope or ctx).enter_context(nc.sbuf_tensor(name, shape, dt))

        def sem(name):
            return ctx.enter_context(nc.semaphore(name))

        pe = Queue(nc.tensor, sem("pe_done"))
        act = Queue(nc.scalar, sem("act_done"))
        dve = Queue(nc.vector, sem("dve_done"))
        pool = Queue(nc.gpsimd, sem("pool_done"))
        sp = Queue(nc.sync, sem("sp_done"))
        engines = (pe, act, dve, pool)
        stores = []

        def phase_end():
            ends = [q.last() for q in engines]
            for q in engines + (sp,):
                q.wait(*ends, *stores)

        def load(name, dst, src, *after, queue=sp):
            s = sem("in_" + name)
            queue.wait(*after)
            queue.engine.dma_start(dst, src).then_inc(s, 16)
            return (s, 16)

        psum = [ctx.enter_context(nc.psum_tensor(f"bank{i}", [P, 512], F32)) for i in range(8)]
        banks = Banks(psum)

        order = []
        for name, n in (("mix0_kv", 4), ("mix0_q", 2), ("mix0_out", 2), ("gnn0_w1", 2), ("gnn0_w2", 2)):
            if name == "mix0_q":
                for g in range(2):
                    order += [("mix0_q", g), ("mix0_out", g)]
            elif name != "mix0_out":
                order += [(name, i) for i in range(n)]
        for half in range(2):
            order += [(f"ffn0_w{n}", 2 * half + i) for n in (1, 2) for i in range(2)]
        order += [("mix1_kv", i) for i in range(4)]
        for g in range(2):
            order += [("mix1_q", g), ("mix1_out", g)]
        for g in range(4):
            order += [("gat_w1", g), ("gat_w2", g)]
        passes = [("shared", g) for g in range(3)] + [(e, 0) for e in range(E)]
        for who, g in passes:
            for c in range(NCH + 1):
                if c < NCH:
                    order.append(("ffn1_w1", who, c))
                if c > 0:
                    order.append(("ffn1_w2", who, c - 1))

        def weight_source(key):
            if key[0] in ("ffn1_w1", "ffn1_w2"):
                if key[1] == "shared":
                    return ins["shared" + key[0][4:]][key[2]]
                return ins[key[0]][key[1] * NCH + key[2]]
            return ins[key[0]][key[1]]

        RAW, PAIR = 2, 3
        raw = sb("weight_raw", [P, RAW, WC])
        whi = sb("weight_hi", [P, PAIR, WC], F32R)
        wlo = sb("weight_lo", [P, PAIR, WC], F32R)
        raw_sem = [sem(f"weight_landed{i}") for i in range(RAW)]
        stream = {"loaded": 0, "split": 0, "used": 0}
        raw_free, pair_free, landed, pair_ready = {}, {}, {}, {}

        def stream_load():
            i = stream["loaded"]
            if i >= len(order):
                return
            src = weight_source(order[i])
            sp.wait(raw_free.get(i - RAW))
            sp.engine.dma_start(raw[:, i % RAW, 0:src.shape[1]], src).then_inc(raw_sem[i % RAW], 16)
            landed[i] = (raw_sem[i % RAW], 16 * (i // RAW + 1))
            stream["loaded"] += 1

        def stream_split():
            while stream["split"] < len(order):
                i = stream["split"]
                if i >= PAIR and i - PAIR not in pair_free:
                    return
                w = weight_source(order[i]).shape[1]
                r, h = i % RAW, i % PAIR
                act.wait(landed[i], pair_free.get(i - PAIR))
                hi_done = act.done(nc.scalar.activation(whi[:, h, 0:w], raw[:, r, 0:w], ACT.Copy))
                dve.wait(landed[i], hi_done, pair_free.get(i - PAIR))
                lo_done = dve.done(nc.vector.tensor_tensor(wlo[:, h, 0:w], raw[:, r, 0:w],
                                                           whi[:, h, 0:w].bitcast(F32), ALU.subtract))
                pair_ready[i] = lo_done
                raw_free[i] = lo_done
                stream["split"] += 1
                stream_load()

        def take_weight(*key):
            i = stream["used"]
            assert order[i] == key, (order[i], key)
            stream["used"] += 1
            stream_split()
            w = weight_source(key).shape[1]
            kt = {"mix0_out": 3, "mix1_out": 3, "ffn1_w2": 3, "gat_w2": 2}.get(key[0], KD)
            hi = whi[:, i % PAIR, 0:w].rearrange("p (k n) -> p k n", k=kt)
            lo = wlo[:, i % PAIR, 0:w].rearrange("p (k n) -> p k n", k=kt)
            return (hi, lo), i, pair_ready[i]

        def drop_weight(i):
            pair_free[i] = pe.last()
            stream_split()

        stream_load()
        stream_load()

        def mm3(dst, a, b, first, last):
            nc.tensor.matmul(dst, a[0], b[0], start=first, stop=False)
            nc.tensor.matmul(dst, a[0], b[1], start=False, stop=False)
            return nc.tensor.matmul(dst, a[1], b[0], start=False, stop=last)

        def product(dst, terms, first=True, last=True):
            terms = list(terms)
            for n, (a, b) in enumerate(terms):
                end = mm3(dst, a, b, first and n == 0, last and n == len(terms) - 1)
            return pe.done(end)

        def product_exact_a(dst, terms):
            terms = list(terms)
            for n, (a, b) in enumerate(terms):
                nc.tensor.matmul(dst, a, b[0], start=(n == 0), stop=False)
                end = nc.tensor.matmul(dst, a, b[1], start=False, stop=(n == len(terms) - 1))
            return pe.done(end)

        def split(pair, src, *after):
            act.wait(*after)
            hi_done = act.done(nc.scalar.activation(pair[0], src, ACT.Copy))
            dve.wait(hi_done, *after)
            return dve.done(nc.vector.tensor_tensor(pair[1], src, pair[0].bitcast(F32), ALU.subtract))

        def at(pair, *index):
            return (pair[0].__getitem__(index), pair[1].__getitem__(index))

        def v(instruction, *after):
            dve.wait(*after)
            return dve.done(instruction())

        def a(instruction, *after):
            act.wait(*after)
            return act.done(instruction())

        def g(instruction, *after):
            pool.wait(*after)
            return pool.done(instruction())

        ident = sb("identity", [P, P])
        ones = sb("ones", [P, P], F32R)
        iota_h = sb("iota_half", [P, TP], F16)
        ones_f = sb("ones_f", [P, P])
        c1 = g(lambda: nc.gpsimd.memset(ident[:, :], 0.0))
        c2 = g(lambda: nc.gpsimd.affine_select(out=ident[:, :], in_=ident[:, :], compare_op=ALU.not_equal, fill=1.0,
                                               base=0, pattern=[[-1, P]], channel_multiplier=1), c1)
        c3 = g(lambda: nc.gpsimd.memset(ones_f[:, :], 1.0))
        ones_ready = a(lambda: nc.scalar.activation(ones[:, :], ones_f[:, :], ACT.Copy), c3)

        x = sb("x", [P, TT, D])
        xT = (sb("xT_hi", [P, KD, TP], F32R), sb("xT_lo", [P, KD, TP], F32R))
        count = sb("edge_count", [P, TT, TP], mybir.dt.uint16)
        bias0 = sb("bias_row", [P, D])
        stats = sb("ln_stats", [P, TT, 2, 6])
        moments = sb("ln_moments", [P, TT, 2])
        rstd = sb("ln_rstd", [P, TT])
        start = ExitStack()
        iota_i = sb("iota_int", [P, TP], I32, start)
        edges_i = sb("edges_int", [EP, 2, EC], I32, start)
        c4 = g(lambda: nc.gpsimd.iota(iota_i[:, :], [[1, TP]], base=0, channel_multiplier=0))
        c5 = g(lambda: nc.gpsimd.tensor_copy(iota_h[:, :], iota_i[:, :]), c4)
        const_ready = c5
        zero_x = v(lambda: nc.vector.memset(x[96:P, TT - 1, :], 0.0))
        x_sem = sem("in_x")
        sp.wait(zero_x)
        sp.engine.dma_start(x[:, 0:TT - 1, :], ins["x"][0:(TT - 1) * P, :].rearrange("(t p) d -> p t d", p=P)).then_inc(x_sem, 16)
        sp.engine.dma_start(x[0:LAST, TT - 1, :], ins["x"][(TT - 1) * P:T, :]).then_inc(x_sem, 16)
        x_ready = (x_sem, 32)
        edge_sem = sem("in_edges")
        sp.engine.dma_start(edges_i[:, 0, :], ins["src"]).then_inc(edge_sem, 16)
        sp.engine.dma_start(edges_i[:, 1, :], ins["dst"]).then_inc(edge_sem, 16)
        edges_ready = (edge_sem, 32)
        zeros = v(lambda: nc.vector.memset(bias0[:, :], 0.0))
        zeroed = (sem("overflow_zeroed"), 16)
        act.wait(zeros, x_ready, edges_ready)
        act.engine.dma_start(result_dram[E * CAP:E * TP, :].rearrange("(n p) d -> p n d", p=P),
                             bias0[:, :].unsqueeze(1).broadcast_to([P, E * EXTRA, D])).then_inc(zeroed[0], 16)
        stores.append(zeroed)


        def layer_norm(xn, *after):
            for t in range(TT):
                for h in range(2):
                    s = v(lambda: nc.vector.bn_stats(stats[:, t, h, :], x[:, t, h * HALF:(h + 1) * HALF]), *after)
            dve.wait(s)
            for t in range(TT):
                s = v(lambda: nc.vector.bn_aggr(moments[:, t, :], stats[:, t, :, :].rearrange("p a b -> p (a b)")))
            s = v(lambda: nc.vector.tensor_scalar(rstd[:, :], moments[:, :, 1], LN_EPS, None, ALU.add), s)
            s = a(lambda: nc.scalar.activation(rstd[:, :], rstd[:, :], ACT.Sqrt), s)
            s = v(lambda: nc.vector.reciprocal(rstd[:, :], rstd[:, :]), s)
            dve.wait(s)
            return [v(lambda: nc.vector.tensor_scalar(xn[:, t, :], x[:, t, :], moments[:, t, 0:1], rstd[:, t:t + 1],
                                                      ALU.subtract, ALU.mult)) for t in range(TT)]

        def transpose_in(xn, ready, *after):
            done = []
            for t in range(TT):
                for c in range(2):
                    i, bank, free = banks.take()
                    pe.wait(ready[t], free, *after)
                    for k in range(3):
                        end = nc.tensor.transpose(bank[:, k * P:(k + 1) * P],
                                                  xn[:, t, (3 * c + k) * P:(3 * c + k + 1) * P], ident[:, :])
                    moved = pe.done(end)
                    part = at(xT, slice(None), slice(3 * c, 3 * c + 3), slice(t * P, (t + 1) * P))
                    s = split(part, bank[:, 0:3 * P].rearrange("p (k n) -> p k n", k=3), moved)
                    banks.release(i, s)
                done.append(s)
            return done

        def tok(t):
            return slice(t * P, (t + 1) * P)


        def row_load(name, dst, src, n, *after):
            return load(name, dst, src.rearrange("(a n) -> a n", a=1).broadcast_to([P, n]), *after)

        with ExitStack() as scope:
            xn = sb("xn0", [P, TT, D], scope=scope)
            pe.wait(c2)
            xT_ready = transpose_in(xn, layer_norm(xn, x_ready))

            edge = sb("edges", [EP, 4, EC], scope=scope)
            s = v(lambda: nc.vector.tensor_copy(edge[:, 0:2, :], edges_i[:, :, :]), edges_ready)
            s = v(lambda: nc.vector.tensor_scalar(edge[:, 3, :], edge[:, 1, :], float(TM), None, ALU.is_ge), s)
            s = v(lambda: nc.vector.tensor_scalar(edge[:, 2, :], edge[:, 3, :], float(PACK - 1), 1.0, ALU.mult, ALU.add), s)
            s = v(lambda: nc.vector.scalar_tensor_tensor(edge[:, 1, :], edge[:, 3, :], -float(TM), edge[:, 1, :],
                                                         ALU.mult, ALU.add), s)
            fold_ready = s
            RING = 4
            hot_src = sb("one_hot_src", [EP, RING, TP], F16, scope)
            hot_dst = sb("one_hot_dst", [EP, RING, 320], F16, scope)
            whole = sb("packed_counts", [P, TT, TM], I32, scope)
            low = sb("low_counts", [P, TT, TM], I32, scope)
            high = sb("high_counts", [P, TT, TM], I32, scope)
            cnt = sb("counts", [P, TT, TP], I32, scope)
            counted = g(lambda: nc.gpsimd.memset(cnt[:, :, :], 0))
            hot_free = [None] * RING
            dve.wait(const_ready, fold_ready)
            unpacked = None
            whole_free = None
            for chunk in range(EC // CHUNK_E):
                taken = [banks.take() for _ in range(TT)]
                for n in range(CHUNK_E):
                    j = chunk * CHUNK_E + n
                    r = j % RING
                    dve.wait(hot_free[r])
                    v(lambda: nc.vector.tensor_scalar(hot_src[:, r, :], iota_h[0:EP, :], edge[:, 0, j:j + 1], None, ALU.is_equal))
                    hot = v(lambda: nc.vector.tensor_scalar(hot_dst[:, r, :], iota_h[0:EP, 0:320], edge[:, 1, j:j + 1],
                                                            edge[:, 2, j:j + 1], ALU.is_equal, ALU.mult))
                    pe.wait(hot)
                    for t in range(TT):
                        if n == 0:
                            pe.wait(taken[t][2])
                        end = nc.tensor.matmul(taken[t][1][:, 0:TM], hot_src[:, r, tok(t)], hot_dst[:, r, 0:TM],
                                               start=(n == 0), stop=(n == CHUNK_E - 1))
                    hot_free[r] = pe.done(end)
                for t in range(TT):
                    got = a(lambda: nc.scalar.activation(whole[:, t, :], taken[t][1][:, 0:TM], ACT.Copy),
                            hot_free[r], whole_free)
                    banks.release(taken[t][0], got)
                v(lambda: nc.vector.tensor_scalar(low[:, :, :], whole[:, :, :], PACK - 1, None, ALU.bitwise_and), got, unpacked)
                cut = v(lambda: nc.vector.tensor_scalar(high[:, :, :], whole[:, :, :], 12, None, ALU.logical_shift_right))
                whole_free = cut
                counted = g(lambda: nc.gpsimd.tensor_tensor(cnt[:, :, 0:TM], cnt[:, :, 0:TM], low[:, :, :], ALU.add), cut, counted)
                counted = g(lambda: nc.gpsimd.tensor_tensor(cnt[:, :, TM:T], cnt[:, :, TM:T], high[:, :, 0:T - TM], ALU.add), counted)
                unpacked = counted
            counts_kept = v(lambda: nc.vector.tensor_copy(count[:, :, :], cnt[:, :, :]), counted)
            phase_end()
        start.close()

        def add_bias(names, scale=None):
            for name in names:
                s = row_load(name, bias0[:, :], ins[name], D, dve.last())
                if scale is not None:
                    s = v(lambda: nc.vector.tensor_scalar(bias0[:, :], bias0[:, :], scale, None, ALU.mult), s)
                dve.wait(s)
                for t in range(TT):
                    s = v(lambda: nc.vector.tensor_tensor(x[:, t, :], x[:, t, :], bias0[:, :], ALU.add), dve.last())
            return s

        def add_tokens(pairs_of, n_terms, weight, cols, c0, ready):
            for t in range(TT):
                i, bank, free = banks.take()
                pe.wait(free, *ready)
                got = product(bank[:, 0:cols], [(pairs_of(k, t), at(weight, slice(None), k, slice(0, cols))) for k in range(n_terms)])
                s = v(lambda: nc.vector.tensor_tensor(x[:, t, c0:c0 + cols], x[:, t, c0:c0 + cols], bank[:, 0:cols], ALU.add), got)
                banks.release(i, s)
            return s

        def linear_attention(kind, finish_kv, finish_q, normalised):
            with ExitStack() as scope:
                kv = sb(kind + "_kv", [P, 2, TT, HALF], F32, scope)
                KV = 3
                kvp = (sb(kind + "_kv_hi", [P, KV, TT, HALF], F32R, scope), sb(kind + "_kv_lo", [P, KV, TT, HALF], F32R, scope))
                att = (sb(kind + "_att_hi", [P, PAIRS, P], F32R, scope), sb(kind + "_att_lo", [P, PAIRS, P], F32R, scope))
                attf = sb(kind + "_att", [P, PAIRS, P], F32, scope)
                s0 = v(lambda: nc.vector.memset(attf[:, :, :], 0.0))
                if normalised:
                    den = (sb(kind + "_den_hi", [P, PAIRS, P], F32R, scope), sb(kind + "_den_lo", [P, PAIRS, P], F32R, scope))
                    denf = sb(kind + "_den", [P, PAIRS, P], F32, scope)
                    s0 = v(lambda: nc.vector.memset(denf[:, :, :], 0.0))
                rows = finish_kv(None, kv, scope)
                kv_free, pair_read = [None, None], [None] * KV
                sizes = [P] * (TT - 1) + [LAST]

                def keys_or_values(n):
                    r, which = n % 2, n % 2
                    w, i, ready = take_weight(kind + "_kv", n)
                    pe.wait(ready, *xT_ready)
                    for t in range(TT):
                        b, bank, free = banks.take()
                        pe.wait(free)
                        got = product(bank[:, 0:HALF], [(at(xT, slice(None), k, tok(t)), at(w, slice(None), k, slice(None))) for k in range(KD)])
                        s = a(lambda: nc.scalar.activation(kv[:, r, t, :], bank[:, 0:HALF], ACT.Copy), got, kv_free[r])
                        banks.release(b, s)
                    drop_weight(i)
                    s = finish_kv(which, kv, rows, s)
                    kv_free[r] = split(at(kvp, slice(None), n % KV, slice(None), slice(None)), kv[:, r, :, :], s, pair_read[n % KV])
                    return kv_free[r]

                def per_head_products(grp, ready):
                    pk, pv = (2 * grp) % KV, (2 * grp + 1) % KV
                    pe.wait(ready)
                    for pr in range(3):
                        b, bank, free = banks.take()
                        pe.wait(free)
                        cols = slice(pr * P, (pr + 1) * P)
                        kv_read = product(bank[:, 0:P], [(at(kvp, slice(0, n), pk, t, cols), at(kvp, slice(0, n), pv, t, cols))
                                                         for t, n in enumerate(sizes)])
                        for h in range(2):
                            blk = slice(h * DH, (h + 1) * DH)
                            s = v(lambda: nc.vector.tensor_scalar(attf[blk, 3 * grp + pr, blk], bank[blk, h * DH:(h + 1) * DH],
                                                                  1.0 if normalised else 1.0 / T, None, ALU.mult), kv_read, s0)
                        banks.release(b, s)
                        if normalised:
                            b, bank, free = banks.take()
                            pe.wait(free)
                            for t, n in enumerate(sizes):
                                nc.tensor.matmul(bank[:, 0:P], kvp[0][0:n, pk, t, cols], ones[0:n, :], start=(t == 0), stop=False)
                                end = nc.tensor.matmul(bank[:, 0:P], kvp[1][0:n, pk, t, cols], ones[0:n, :], start=False, stop=(t == TT - 1))
                            kv_read = pe.done(end)
                            for h in range(2):
                                blk = slice(h * DH, (h + 1) * DH)
                                s = v(lambda: nc.vector.tensor_copy(denf[blk, 3 * grp + pr, blk], bank[blk, h * DH:(h + 1) * DH]), kv_read)
                            banks.release(b, s)
                    pair_read[pk] = pair_read[pv] = pe.last()
                    return s

                keys_or_values(0)
                first_ready = keys_or_values(1)
                keys_or_values(2)
                per_head_products(0, first_ready)
                s = per_head_products(1, keys_or_values(3))
                att_ready = split(at(att, slice(None), slice(None), slice(None)), attf[:, :, :], s)
                if normalised:
                    att_ready = split(at(den, slice(None), slice(None), slice(None)), denf[:, :, :], s)
                phase_end()
                flat = [b[:, :, :, :].rearrange("p a b c -> p (a b c)") for b in kvp]
                qp = tuple(f[:, 0:TP].rearrange("p (a n) -> p a n", a=1) for f in flat)
                outT = tuple(f[:, TP:TP + 3 * TP].rearrange("p (a n) -> p a n", a=3) for f in flat)
                work = kv[:, :, :, :].rearrange("p a b c -> p (a b c)")
                q_tmp, q_tmp2, d_tmp = work[:, 0:TP], work[:, TP:2 * TP], work[:, 2 * TP:3 * TP]
                q_read = None
                out_read = None
                zero = v(lambda: nc.vector.memset(work[:, 0:4 * TP], 0.0))
                for part in (qp, outT):
                    zero = split(part, work[:, 0:part[0].shape[1] * TP].rearrange("p (a n) -> p a n", n=TP), zero)
                for grp in range(2):
                    w, i, ready = take_weight(kind + "_q", grp)
                    for pr in range(3):
                        got = {}
                        for c0, n in TOKEN_SPANS:
                            b, bank, free = banks.take()
                            pe.wait(free, ready)
                            tk = product(bank[:, 0:n], [(at(w, slice(None), k, slice(pr * P, (pr + 1) * P)),
                                                         at(xT, slice(None), k, slice(c0, c0 + n))) for k in range(KD)])
                            s = finish_q(q_tmp[:, c0:c0 + n], q_tmp2[:, c0:c0 + n], bank[:, 0:n], tk, b)
                        s = split(at(qp, slice(None), 0, slice(0, T + 1)), q_tmp[:, 0:T + 1], s, q_read)
                        pe.wait(s, att_ready)
                        for c0, n in TOKEN_SPANS:
                            b, bank, free = banks.take()
                            pe.wait(free)
                            q = at(qp, slice(None), 0, slice(c0, c0 + n))
                            tk = product(bank[:, 0:n], [(at(att, slice(None), 3 * grp + pr, slice(None)), q)])
                            o = at(outT, slice(None), pr, slice(c0, c0 + n))
                            if normalised:
                                b2, bank2, free = banks.take()
                                pe.wait(free)
                                tk2 = product(bank2[:, 0:n], [(at(den, slice(None), 3 * grp + pr, slice(None)), q)])
                                s = v(lambda: nc.vector.reciprocal(d_tmp[:, c0:c0 + n], bank2[:, 0:n]), tk2, dve.last())
                                banks.release(b2, s)
                                s = v(lambda: nc.vector.tensor_tensor(d_tmp[:, c0:c0 + n], bank[:, 0:n], d_tmp[:, c0:c0 + n], ALU.mult), tk, s)
                                banks.release(b, s)
                                s = split(o, d_tmp[:, c0:c0 + n], s, out_read)
                                tk = tk2
                            else:
                                s = split(o, bank[:, 0:n], tk, out_read)
                                banks.release(b, s)
                            q_read = tk
                    drop_weight(i)
                    w, i, ready = take_weight(kind + "_out", grp)
                    for c in range(2):
                        part = at(w, slice(None), slice(None), slice(c * HALF, (c + 1) * HALF))
                        add_tokens(lambda k, t: at(outT, slice(None), k, tok(t)), 3, part, HALF, c * HALF, (ready, s))
                    out_read = pe.last()
                    drop_weight(i)
                phase_end()

        x_based = add_bias(("gnn0_b2", "mix0_b"))

        def kv0(which, kv, rows, after=None):
            if which is None:
                scope = rows
                gb = sb("gain_shift_rows", [P, 4, DH], F32, scope)
                for n, name in enumerate(("mix0_gk", "mix0_bk", "mix0_gv", "mix0_bv")):
                    got = row_load(name, gb[:, n, :], ins[name], DH)
                    dve.wait(got)
                return gb, sb("kv_square", [P, TT * 6, DH], F32, scope), sb("kv_stats", [P, 3, TT * 6], F32, scope)
            gb, sq, st = rows
            z = [kv[:, which, t, :].rearrange("p (h d) -> p h d", d=DH) for t in range(TT)]
            n6 = lambda i, t: st[:, i, 6 * t:6 * t + 6]
            wide = lambda ap: ap.unsqueeze(2).broadcast_to([P, 6, DH])
            gain = lambda i: gb[:, i, :].unsqueeze(1).broadcast_to([P, 6, DH])
            sqt = lambda t: sq[:, 6 * t:6 * t + 6, :]
            every = range(TT)
            for t in every:
                s = v(lambda: nc.vector.tensor_reduce(n6(0, t), z[t], AX_X, ALU.add), after)
            s = v(lambda: nc.vector.tensor_scalar(st[:, 0, :], st[:, 0, :], 1.0 / DH, None, ALU.mult), s)
            dve.wait(s)
            for t in every:
                s = v(lambda: nc.vector.tensor_tensor(z[t], z[t], wide(n6(0, t)), ALU.subtract))
            act.wait(s)
            for t in every:
                s = a(lambda: nc.scalar.activation(sqt(t), z[t], ACT.Square))
            s = v(lambda: nc.vector.tensor_reduce(st[:, 1, :], sq[:, :, :], AX_X, ALU.add), s)
            s = v(lambda: nc.vector.tensor_scalar(st[:, 1, :], st[:, 1, :], 1.0 / DH, LN_EPS, ALU.mult, ALU.add), s)
            s = a(lambda: nc.scalar.activation(st[:, 1, :], st[:, 1, :], ACT.Sqrt), s)
            s = v(lambda: nc.vector.reciprocal(st[:, 2, :], st[:, 1, :]), s)
            for step in range(3):
                dve.wait(s)
                for t in every:
                    o = (wide(n6(2, t)), gain(2 * which), gain(2 * which + 1))[step]
                    s = v(lambda: nc.vector.tensor_tensor(z[t], z[t], o, ALU.add if step == 2 else ALU.mult))
            return s

        def q0(q, tmp, bank, got, b):
            s = a(lambda: nc.scalar.activation(q, bank, ACT.Copy), got, dve.last())
            banks.release(b, s)
            return s

        linear_attention("mix0", kv0, q0, False)

        gcn = ExitStack()
        adj = (sb("adj_hi", [P, TT, TP], F32R, gcn), sb("adj_lo", [P, TT, TP], F32R, gcn))
        with ExitStack() as scope:
            loops = sb("counts_with_loops", [P, TT, TP], F32, scope)
            deg_row = sb("deg_row", [P, TP], F32, scope)
            deg_col = sb("deg_col", [P, TT], F32, scope)
            s = v(lambda: nc.vector.tensor_copy(loops[:, :, :], count[:, :, :]))
            dve.wait(s)
            for t in range(TT):
                s = v(lambda: nc.vector.tensor_tensor(loops[:, t, tok(t)], loops[:, t, tok(t)], ident[:, :], ALU.add))
            s = split(at(adj, slice(None), slice(None), slice(None)), loops[:, :, :], s)
            pe.wait(s, ones_ready)
            for c0, n in ((0, 320), (320, 320)):
                i, bank, free = banks.take()
                pe.wait(free)
                got = product_exact_a(bank[:, 0:n], [(ones[:, :], at(adj, slice(None), k, slice(c0, c0 + n))) for k in range(TT)])
                s = a(lambda: nc.scalar.activation(deg_row[:, c0:c0 + n], bank[:, 0:n], ACT.Sqrt), got)
                banks.release(i, s)
            row_done = v(lambda: nc.vector.reciprocal(deg_row[:, :], deg_row[:, :]), s)
            for t in range(TT):
                i, bank, free = banks.take()
                pe.wait(free)
                for k in range(TT):
                    nc.tensor.matmul(bank[:, 0:2], adj[0][:, k, tok(t)], ones[:, 0:2], start=(k == 0), stop=False)
                    end = nc.tensor.matmul(bank[:, 0:2], adj[1][:, k, tok(t)], ones[:, 0:2], start=False, stop=(k == TT - 1))
                s = a(lambda: nc.scalar.activation(deg_col[:, t:t + 1], bank[:, 0:1], ACT.Sqrt), pe.done(end))
                banks.release(i, s)
            s = v(lambda: nc.vector.reciprocal(deg_col[:, :], deg_col[:, :]), s)
            dve.wait(s, row_done)
            for t in range(TT):
                s = v(lambda: nc.vector.scalar_tensor_tensor(loops[:, t, :], loops[:, t, :], deg_col[:, t:t + 1],
                                                             deg_row[:, :], ALU.mult, ALU.mult))
            adj_ready = split(at(adj, slice(None), slice(None), slice(None)), loops[:, :, :], s)
            phase_end()

        with ExitStack() as scope:
            h = (sb("gcn_h_hi", [P, TT, D], F32R, scope), sb("gcn_h_lo", [P, TT, D], F32R, scope))
            bcol = sb("gcn_b1", [P, KD], F32, scope)
            b1_ready = load("gcn_b1", bcol[:, :], ins["gnn0_b1"])
            z_tmp = sb("gcn_tmp", [P, 2, 320], F32, scope)

            def node_product(key, src, ready):
                for c in range(2):
                    w, i, w_ready = take_weight(key, c)
                    for t in range(TT):
                        b, bank, free = banks.take()
                        pe.wait(free, w_ready, *ready)
                        got = product(bank[:, 0:HALF], [(at(src, slice(None), k, tok(t)), at(w, slice(None), k, slice(None))) for k in range(KD)])
                        s = split(at(h, slice(None), t, slice(c * HALF, (c + 1) * HALF)), bank[:, 0:HALF], got)
                        banks.release(b, s)
                    drop_weight(i)
                return s

            s = node_product("gnn0_w1", xT, xT_ready)
            pe.wait(s)
            hT_start = pe.last()
            tmp_free = [None, None]
            n_tmp = 0
            act.wait(b1_ready)
            for m in range(KD):
                for c0, n in TOKEN_SPANS:
                    b, bank, free = banks.take()
                    pe.wait(free)
                    got = product(bank[:, 0:n], [(at(h, slice(None), k, slice(m * P, (m + 1) * P)), at(adj, slice(None), k, slice(c0, c0 + n)))
                                                 for k in range(TT)])
                    tmp = z_tmp[:, n_tmp % 2, 0:n]
                    s = a(lambda: nc.scalar.activation(tmp, bank[:, 0:n], ACT.Relu, bias=bcol[:, m:m + 1]), got, tmp_free[n_tmp % 2])
                    banks.release(b, s)
                    s = split(at(xT, slice(None), m, slice(c0, c0 + n)), tmp, s, hT_start)
                    tmp_free[n_tmp % 2] = s
                    n_tmp += 1
            act.wait(pe.last())
            dve.wait(pe.last())
            s = node_product("gnn0_w2", xT, (s,))
            for c in range(2):
                add_tokens(lambda k, t: at(adj, slice(None), k, tok(t)), TT,
                           at(h, slice(None), slice(None), slice(c * HALF, (c + 1) * HALF)), HALF, c * HALF, (s,))
            phase_end()
        gcn.close()

        iota8 = sb("expert_number", [P, TT, E])
        with ExitStack() as scope:
            iota8_i = sb("expert_number_int", [P, TT, E], I32, scope)
            s = g(lambda: nc.gpsimd.iota(iota8_i[:, :, :], [[0, TT], [1, E]], base=0, channel_multiplier=0))
            iota8_ready = g(lambda: nc.gpsimd.tensor_copy(iota8[:, :, :], iota8_i[:, :, :]), s)
            phase_end()
        over_e = lambda ap: ap.unsqueeze(2).broadcast_to([P, TT, E])

        def router_logits(name, logits, scope):
            gate = sb(name + "_gate", [P, KD, E], F32, scope)
            gp = (sb(name + "_gate_hi", [P, KD, E], F32R, scope), sb(name + "_gate_lo", [P, KD, E], F32R, scope))
            s = split(at(gp, slice(None), slice(None), slice(None)), gate[:, :, :], load(name, gate[:, :, :], ins[name]))
            pe.wait(s, *xT_ready)
            for t in range(TT):
                b, bank, free = banks.take()
                pe.wait(free)
                got = product(bank[:, 0:E], [(at(xT, slice(None), k, tok(t)), at(gp, slice(None), k, slice(None))) for k in range(KD)])
                s = a(lambda: nc.scalar.activation(logits[:, t, :], bank[:, 0:E], ACT.Copy), got)
                banks.release(b, s)
            return s

        def top_two(name, p, scope, after):
            best = sb(name + "_best", [P, 2, TT], F32, scope)
            number = sb(name + "_number", [P, TT], F32, scope)
            hot = sb(name + "_one_hot", [P, 2, TT, E], F32, scope)
            work = sb(name + "_work", [P, TT, E], F32, scope)
            rest = sb(name + "_rest", [P, TT, E], F32, scope)
            s = v(lambda: nc.vector.tensor_copy(rest[:, :, :], p), after, iota8_ready)
            for k in range(2):
                s = v(lambda: nc.vector.tensor_reduce(best[:, k, :], rest[:, :, :], AX_X, ALU.max), s)
                s = v(lambda: nc.vector.tensor_tensor(work[:, :, :], rest[:, :, :], over_e(best[:, k, :]), ALU.is_equal), s)
                s = v(lambda: nc.vector.scalar_tensor_tensor(work[:, :, :], work[:, :, :], -float(E), iota8[:, :, :], ALU.mult, ALU.add), s)
                s = v(lambda: nc.vector.tensor_reduce(number[:, :], work[:, :, :], AX_X, ALU.min), s)
                s = v(lambda: nc.vector.tensor_scalar(number[:, :], number[:, :], float(E), None, ALU.add), s)
                s = v(lambda: nc.vector.tensor_tensor(hot[:, k, :, :], iota8[:, :, :], over_e(number[:, :]), ALU.is_equal), s)
                s = v(lambda: nc.vector.scalar_tensor_tensor(rest[:, :, :], hot[:, k, :, :], NEG, rest[:, :, :], ALU.mult, ALU.add), s)
            return best, hot, s

        def gate_matrix(name, weights, hot, scope, after):
            gates = sb(name + "_gates", [P, 2, TT, E], F32, scope)
            gT = (sb(name + "_gatesT_hi", [E, TP], F32R, scope), sb(name + "_gatesT_lo", [E, TP], F32R, scope))
            for k in range(2):
                s = v(lambda: nc.vector.tensor_tensor(gates[:, k, :, :], hot[:, k, :, :], over_e(weights[:, k, :]), ALU.mult), after)
            s = v(lambda: nc.vector.tensor_tensor(gates[:, 0, :, :], gates[:, 0, :, :], gates[:, 1, :, :], ALU.add), s)
            pe.wait(s)
            for t in range(TT):
                b, bank, free = banks.take()
                pe.wait(free)
                moved = pe.done(nc.tensor.transpose(bank[0:E, 0:P], gates[:, 0, t, :], ident[:, :]))
                s = split(at(gT, slice(None), tok(t)), bank[0:E, 0:P], moved)
                banks.release(b, s)
            return gT, s

        with ExitStack() as scope:
            xn = sb("xn1", [P, TT, D], F32, scope)
            xT_ready = transpose_in(xn, layer_norm(xn, dve.last()))
            phase_end()
        with ExitStack() as scope:
            p = sb("ffn0_p", [P, TT, E], F32, scope)
            m = sb("ffn0_m", [P, 2, TT], F32, scope)
            s = router_logits("ffn0_gate", p, scope)
            s = v(lambda: nc.vector.tensor_reduce(m[:, 0, :], p[:, :, :], AX_X, ALU.max), s)
            s = v(lambda: nc.vector.tensor_tensor(p[:, :, :], p[:, :, :], over_e(m[:, 0, :]), ALU.subtract), s)
            s = a(lambda: nc.scalar.activation(p[:, :, :], p[:, :, :], ACT.Exp), s)
            s = v(lambda: nc.vector.tensor_reduce(m[:, 1, :], p[:, :, :], AX_X, ALU.add), s)
            s = v(lambda: nc.vector.reciprocal(m[:, 1, :], m[:, 1, :]), s)
            s = v(lambda: nc.vector.tensor_tensor(p[:, :, :], p[:, :, :], over_e(m[:, 1, :]), ALU.mult), s)
            best, hot, s = top_two("ffn0", p[:, :, :], scope, s)
            s = v(lambda: nc.vector.tensor_tensor(m[:, 0, :], best[:, 0, :], best[:, 1, :], ALU.add), s)
            s = v(lambda: nc.vector.tensor_scalar(m[:, 0, :], m[:, 0, :], 1e-9, None, ALU.add), s)
            s = v(lambda: nc.vector.reciprocal(m[:, 0, :], m[:, 0, :]), s)
            for k in range(2):
                s = v(lambda: nc.vector.tensor_tensor(best[:, k, :], best[:, k, :], m[:, 0, :], ALU.mult), s)
            gT, gT_ready = gate_matrix("ffn0", best, hot, scope, s)
            sel_f = sb("expert_rows_f", [E, KH0, P], F32, scope)
            sel = sb("expert_rows_r", [E, KH0, P], F32R, scope)
            s = g(lambda: nc.gpsimd.memset(sel_f[:, :, :], 1.0))
            s = g(lambda: nc.gpsimd.affine_select(out=sel_f[:, :, :], in_=sel_f[:, :, :], compare_op=ALU.is_ge, fill=0.0,
                                                  base=0, pattern=[[P, KH0], [1, P]], channel_multiplier=-H0), s)
            s = g(lambda: nc.gpsimd.affine_select(out=sel_f[:, :, :], in_=sel_f[:, :, :], compare_op=ALU.is_ge, fill=0.0,
                                                  base=H0 - 1, pattern=[[-P, KH0], [-1, P]], channel_multiplier=H0), s)
            sel_ready = a(lambda: nc.scalar.activation(sel[:, :, :], sel_f[:, :, :], ACT.Copy), s)
            b1 = sb("ffn0_b1", [P, KH0], F32, scope)
            act.wait(load("ffn0_b1", b1[:, :], ins["ffn0_b1"]))
            b2 = sb("ffn0_b2", [E, D], F32, scope)
            b2p = (sb("ffn0_b2_hi", [E, D], F32R, scope), sb("ffn0_b2_lo", [E, D], F32R, scope))
            b2_ready = split(at(b2p, slice(None), slice(None)), b2[:, :], load("ffn0_b2", b2[:, :], ins["ffn0_b2"]))
            HALF_K = KH0 // 2
            hT = (sb("ffn0_hT_hi", [P, HALF_K, TP], F32R, scope), sb("ffn0_hT_lo", [P, HALF_K, TP], F32R, scope))
            tmp = sb("ffn0_tmp", [P, 2, 320], F32, scope)
            tmp_free, n_tmp = [None, None], 0
            s = v(lambda: nc.vector.memset(tmp[:, 0, :], 0.0))
            for k in range(HALF_K):
                s2 = split(at(hT, slice(None), k, slice(T + 1, TP)), tmp[:, 0, 0:TP - T - 1], s)
            tmp_free[0] = s2
            pe.wait(gT_ready, sel_ready)
            hT_read = None
            for kh in range(2):
                for c in range(2):
                    w, i, ready = take_weight("ffn0_w1", 2 * kh + c)
                    for mm in range(3):
                        hid = 6 * kh + 3 * c + mm
                        for c0, n in TOKEN_SPANS:
                            b, bank, free = banks.take()
                            pe.wait(free, ready)
                            got = product(bank[:, 0:n], [(at(w, slice(None), k, slice(mm * P, (mm + 1) * P)), at(xT, slice(None), k, slice(c0, c0 + n)))
                                                         for k in range(KD)])
                            bg, bankg, free = banks.take()
                            pe.wait(free)
                            gate_got = product_exact_a(bankg[:, 0:n], [(sel[:, hid, :], at(gT, slice(None), slice(c0, c0 + n)))])
                            part = tmp[:, n_tmp % 2, 0:n]
                            s = a(lambda: nc.scalar.activation(part, bank[:, 0:n], ACT.Gelu, bias=b1[:, hid:hid + 1]), got, tmp_free[n_tmp % 2])
                            banks.release(b, s)
                            s = v(lambda: nc.vector.tensor_tensor(part, part, bankg[:, 0:n], ALU.mult), s, gate_got)
                            banks.release(bg, s)
                            hT_ready = split(at(hT, slice(None), 3 * c + mm, slice(c0, c0 + n)), part, s, hT_read)
                            tmp_free[n_tmp % 2] = hT_ready
                            n_tmp += 1
                    drop_weight(i)
                for c in range(2):
                    w, i, ready = take_weight("ffn0_w2", 2 * kh + c)
                    pe.wait(ready, hT_ready, b2_ready)
                    cols = slice(c * HALF, (c + 1) * HALF)
                    for t in range(TT):
                        b, bank, free = banks.take()
                        pe.wait(free)
                        terms = [(at(hT, slice(None), k, tok(t)), at(w, slice(None), k, slice(None))) for k in range(HALF_K)]
                        if kh == 0:
                            terms.append((at(gT, slice(None), tok(t)), at(b2p, slice(None), cols)))
                        got = product(bank[:, 0:HALF], terms)
                        s = v(lambda: nc.vector.tensor_tensor(x[:, t, cols], x[:, t, cols], bank[:, 0:HALF], ALU.add), got)
                        banks.release(b, s)
                    drop_weight(i)
                hT_read = pe.last()
            phase_end()

        with ExitStack() as scope:
            xn = sb("xn2", [P, TT, D], F32, scope)
            xT_ready = transpose_in(xn, layer_norm(xn, dve.last()))
            phase_end()
        add_bias(("mix1_b", "gat_b2"))

        def kv1(which, kv, rows, after=None):
            if which is None:
                return [bias0[:, n * HALF:(n + 1) * HALF] for n in range(2)]
            if which == 1:
                return after
            dve.wait(dve.last())
            used = [after, after]
            for t in range(TT):
                k, e = kv[:, 0, t, :], rows[t % 2]
                s = v(lambda: nc.vector.tensor_scalar(e, k, 0.0, None, ALU.min), used[t % 2])
                s = a(lambda: nc.scalar.activation(e, e, ACT.Exp), s)
                used[t % 2] = v(lambda: nc.vector.scalar_tensor_tensor(k, k, 0.0, e, ALU.max, ALU.add), s)
            return used[(TT - 1) % 2]

        def q1(q, tmp, bank, got, b):
            s = v(lambda: nc.vector.tensor_scalar(tmp, bank, 0.0, None, ALU.min), got, act.last(), dve.last())
            s = a(lambda: nc.scalar.activation(tmp, tmp, ACT.Exp), s)
            s = v(lambda: nc.vector.scalar_tensor_tensor(q, bank, 0.0, tmp, ALU.max, ALU.add), s)
            banks.release(b, s)
            return s

        linear_attention("mix1", kv1, q1, True)

        gat = ExitStack()
        sel4_f = bias0[0:4, 0:4 * P].rearrange("p (a n) -> p a n", a=4)
        sel4 = sb("row_selector", [4, 4, P], F32R, gat)
        s = g(lambda: nc.gpsimd.memset(sel4_f[:, :, :], 0.0), dve.last())
        s = g(lambda: nc.gpsimd.affine_select(out=sel4_f[:, :, :], in_=sel4_f[:, :, :], compare_op=ALU.not_equal, fill=1.0,
                                              base=0, pattern=[[-1, 4], [0, P]], channel_multiplier=1), s)
        sel4_ready = a(lambda: nc.scalar.activation(sel4[:, :, :], sel4_f[:, :, :], ACT.Copy), s)
        edges_in = count
        no_edge = sb("no_edge", [P, TT, TP], mybir.dt.bfloat16, gat)
        with ExitStack() as scope:
            cf = sb("count_f", [P, TT, TP], F32, scope)
            s = v(lambda: nc.vector.tensor_copy(cf[:, :, :], count[:, :, :]))
            pe.wait(s)
            act.wait(s)
            for t in range(TT):
                for k0, kn in ((0, 3), (3, 2)):
                    b, bank, free = banks.take()
                    pe.wait(free)
                    for k in range(kn):
                        end = nc.tensor.transpose(bank[:, k * P:(k + 1) * P], cf[:, k0 + k, tok(t)], ident[:, :])
                    cols = slice(k0 * P, (k0 + kn) * P)
                    s = a(lambda: nc.scalar.activation(edges_in[:, t, cols], bank[:, 0:kn * P], ACT.Copy), pe.done(end))
                    s = v(lambda: nc.vector.tensor_scalar(no_edge[:, t, cols], bank[:, 0:kn * P], 0.0, NEG, ALU.is_equal, ALU.mult), s)
                    banks.release(b, s)
            phase_end()
        scores = sb("gat_scores", [P, TT, 4], F32, gat)
        peak_src = sb("gat_peak_src", [P, 2, TT], F32, gat)
        minus_peak = sb("gat_minus_peak", [P, 2, TT], F32, gat)
        total = sb("gat_total", [P, 2, TT], F32, gat)
        small = sb("gat_small", [P, 2, TT], F32, gat)
        rowT = (sb("gat_rowT_hi", [4, TP], F32R, gat), sb("gat_rowT_lo", [4, TP], F32R, gat))
        src_row = sb("gat_src_row", [P, 2, TP], F32, gat)
        ZS, XS = 5, 2
        edge_w = sb("gat_edge", [P, ZS, TP], F32, gat)
        exT = (sb("gat_exT_hi", [P, XS, TT, P], F32R, gat), sb("gat_exT_lo", [P, XS, TT, P], F32R, gat))
        z_free, x_free = [None] * ZS, [None] * XS
        units = {"n": 0}

        def source_rows(heads, s):
            pe.wait(s, sel4_ready)
            for t in range(TT):
                b, bank, free = banks.take()
                pe.wait(free)
                moved = pe.done(nc.tensor.transpose(bank[0:heads, 0:P], scores[:, t, 0:heads], ident[:, :]))
                s = split(at(rowT, slice(0, heads), tok(t)), bank[0:heads, 0:P], moved, pe.last())
                banks.release(b, s)
            pe.wait(s)
            for h in range(heads):
                for c0 in (0, 320):
                    b, bank, free = banks.take()
                    pe.wait(free)
                    got = product_exact_a(bank[:, 0:320], [(sel4[0:heads, h, :], at(rowT, slice(0, heads), slice(c0, c0 + 320)))])
                    s = a(lambda: nc.scalar.activation(src_row[:, h, c0:c0 + 320], bank[:, 0:320], ACT.Copy), got, dve.last())
                    banks.release(b, s)
            return s

        def segment_peaks(heads, row_ready):
            dve.wait(row_ready)
            for h in range(heads):
                for t in range(TT):
                    u = t % ZS
                    s = v(lambda: nc.vector.tensor_tensor_reduce(out=edge_w[:, u, :], in0=no_edge[:, t, :], in1=src_row[:, h, :],
                                                                 scale=1.0, scalar=2.0 * NEG, op0=ALU.add, op1=ALU.max,
                                                                 accum_out=peak_src[:, h, t:t + 1]), z_free[u])
                    z_free[u] = s
            a_dst = scores[:, :, heads:2 * heads].rearrange("p t h -> p h t")
            o = minus_peak[:, 0:heads, :]
            w_ = small[:, 0:heads, :]
            s = v(lambda: nc.vector.tensor_tensor(o, peak_src[:, 0:heads, :], a_dst, ALU.add), s)
            s = v(lambda: nc.vector.tensor_scalar(w_, o, SLOPE, None, ALU.mult), s)
            s = v(lambda: nc.vector.tensor_tensor(o, o, w_, ALU.max), s)
            return v(lambda: nc.vector.tensor_scalar(o, o, -1.0, None, ALU.mult), s)

        def exponentials(unit, scale_rows):
            h, t, heads, u = unit["h"], unit["t"], unit["heads"], unit["u"]
            e = edge_w[:, u % ZS, :]
            s = v(lambda: nc.vector.tensor_scalar(e, src_row[:, h, :], peak_src[:, h, t:t + 1], scores[:, t, heads + h:heads + h + 1],
                                                  ALU.min, ALU.add), z_free[u % ZS])
            s = v(lambda: nc.vector.scalar_tensor_tensor(e, e, SLOPE, e, ALU.mult, ALU.max), s)
            yield
            unit["s"] = a(lambda: nc.scalar.activation(e, e, ACT.Exp, bias=minus_peak[:, h, t:t + 1]), s)
            yield
            tot = total[:, h, t:t + 1]
            s = v(lambda: nc.vector.scalar_tensor_tensor(e, e, 1.0, edges_in[:, t, :], ALU.mult, ALU.mult, accum_out=tot), unit["s"])
            s = v(lambda: nc.vector.tensor_scalar(tot, tot, 1e-16, None, ALU.add), s)
            s = v(lambda: nc.vector.reciprocal(tot, tot), s)
            if scale_rows:
                yield
                s = g(lambda: nc.gpsimd.tensor_scalar(e, e, tot, None, ALU.mult), s)
            unit["s"] = s
            yield
            x_ = u % XS
            pe.wait(unit["s"])
            turned_ = []
            for k0, kn in ((0, 3), (3, 2)):
                b, bank, free = banks.take()
                pe.wait(free)
                for k in range(kn):
                    end = nc.tensor.transpose(bank[:, k * P:(k + 1) * P], e[:, tok(k0 + k)], ident[:, :])
                turned_.append((k0, kn, b, bank, pe.done(end)))
            z_free[u % ZS] = pe.last()
            yield
            for k0, kn, b, bank, moved in turned_:
                s = split(at(exT, slice(None), x_, slice(k0, k0 + kn), slice(None)),
                          bank[:, 0:kn * P].rearrange("p (k n) -> p k n", n=P), moved, x_free[x_])
                banks.release(b, s)
            unit["s"] = s
            yield
            x_free[x_], finish = unit["aggregate"](h, t, lambda k: at(exT, slice(None), x_, k, slice(None)), s)
            yield
            finish()
            yield

        def run_units(tiles, scale_rows, aggregate):
            live = []
            tiles = list(tiles)
            while tiles or live:
                if tiles:
                    h, t, heads = tiles.pop(0)
                    unit = {"h": h, "t": t, "heads": heads, "u": units["n"]}
                    units["n"] += 1
                    unit["aggregate"] = aggregate
                    unit["steps"] = exponentials(unit, scale_rows)
                    live.append(unit)
                live = [unit for unit in live if next(unit["steps"], "end") != "end"]

        h2 = sb("gat_h2", [P, TT, D], F32, gat)
        with ExitStack() as scope:
            hg = (sb("gat_h_hi", [P, TT, 2 * P], F32R, scope), sb("gat_h_lo", [P, TT, 2 * P], F32R, scope))
            att = bias0[:, 0:4 * P].rearrange("p (a n) -> p a n", a=2)
            zT = (sb("gat_zT_hi", [P, 2, TP], F32R, scope), sb("gat_zT_lo", [P, 2, TP], F32R, scope))
            zt = sb("gat_z", [P, 2, P], F32, scope)
            zt_free = [None, None]
            b1 = sb("gat_b1", [P, G1], F32, scope)
            act.wait(load("gat_b1", b1[:, :], ins["gat_b1"]))
            zT_read = None
            hg_read = None
            for grp in range(4):
                cols = slice(grp * 2 * P, (grp + 1) * 2 * P)
                att_free = dve.last()
                for n, name in enumerate(("gat_as1", "gat_ad1")):
                    att_ready = load(f"{name}_{grp}", att[:, n, :], ins[name][cols].rearrange("(a n) -> a n", a=1).broadcast_to([P, 2 * P]), att_free)
                    dve.wait(att_ready)
                w, i, ready = take_weight("gat_w1", grp)
                for t in range(TT):
                    b, bank, free = banks.take()
                    pe.wait(free, ready, *xT_ready)
                    got = product(bank[:, 0:2 * P], [(at(xT, slice(None), k, tok(t)), at(w, slice(None), k, slice(None))) for k in range(KD)])
                    split(at(hg, slice(None), t, slice(None)), bank[:, 0:2 * P], got, hg_read)
                    u = t % ZS
                    prod = edge_w[:, u, 0:4 * P].rearrange("p (a n) -> p a n", a=2)
                    for n in range(2):
                        s = v(lambda: nc.vector.tensor_tensor(prod[:, n, :], bank[:, 0:2 * P], att[:, n, :], ALU.mult), z_free[u])
                    banks.release(b, s)
                    s = v(lambda: nc.vector.tensor_reduce(scores[:, t, :], prod.rearrange("p a (h c) -> p (a h) c", c=P), AX_X, ALU.add), s)
                    z_free[u] = s
                hg_ready = dve.last()
                drop_weight(i)
                s = segment_peaks(2, source_rows(2, s))
                act.wait(s)
                dve.wait(s)
                pe.wait(hg_ready)
                n_z = 0

                def aggregate(h, t, ex, ready):
                    nonlocal n_z
                    b, bank, free = banks.take()
                    pe.wait(free, ready)
                    got = product(bank[:, 0:P], [(at(hg, slice(None), k, slice(h * P, (h + 1) * P)), ex(k)) for k in range(TT)])
                    slot = n_z % 2
                    n_z += 1

                    def finish():
                        z = zt[:, slot, :]
                        s = a(lambda: nc.scalar.activation(z, bank[:, 0:P], ACT.Relu, bias=b1[:, 2 * grp + h:2 * grp + h + 1]), got, zt_free[slot])
                        banks.release(b, s)
                        zt_free[slot] = split(at(zT, slice(None), h, tok(t)), z, s, zT_read)
                    return got, finish

                run_units([(h, t, 2) for h in range(2) for t in range(TT)], True, aggregate)
                hg_read = pe.last()
                s = dve.last()
                w, i, ready = take_weight("gat_w2", grp)
                for c in range(2):
                    for t in range(TT):
                        b, bank, free = banks.take()
                        pe.wait(free, ready, s)
                        got = product(bank[:, 0:HALF], [(at(zT, slice(None), k, tok(t)), at(w, slice(None), k, slice(c * HALF, (c + 1) * HALF))) for k in range(2)])
                        o = h2[:, t, c * HALF:(c + 1) * HALF]
                        if grp == 0:
                            s2 = v(lambda: nc.vector.tensor_copy(o, bank[:, 0:HALF]), got)
                        else:
                            s2 = v(lambda: nc.vector.tensor_tensor(o, o, bank[:, 0:HALF], ALU.add), got, h2_done)
                        banks.release(b, s2)
                h2_done = s2
                zT_read = pe.last()
                drop_weight(i)
            phase_end()

        with ExitStack() as scope:
            hp = tuple(half[:, :, :].rearrange("p k n -> p (k n)").rearrange("p (t d) -> p t d", t=TT) for half in xT)
            att = bias0
            prod = sb("gat2_prod", [P, D], F32, scope)
            for n, name in enumerate(("gat_as2", "gat_ad2")):
                dve.wait(row_load(name, att[:, :], ins[name], D, dve.last()))
                for t in range(TT):
                    s = v(lambda: nc.vector.tensor_tensor(prod[:, :], h2[:, t, :], att[:, :], ALU.mult), dve.last())
                    s = v(lambda: nc.vector.tensor_reduce(scores[:, t, n:n + 1], prod[:, :], AX_X, ALU.add), s)
            row_ready = source_rows(1, s)
            h_ready = split(at(hp, slice(None), slice(None), slice(None)), h2[:, :, :])
            s = segment_peaks(1, row_ready)
            act.wait(s)
            dve.wait(s)
            pe.wait(h_ready)

            def aggregate2(h, t, ex, ready):
                kept = []
                for c in range(2):
                    b, bank, free = banks.take()
                    pe.wait(free, ready)
                    got = product(bank[:, 0:HALF], [(ex(k), at(hp, slice(None), k, slice(c * HALF, (c + 1) * HALF))) for k in range(TT)])
                    kept.append((c, b, bank, got))

                def finish():
                    for c, b, bank, got in kept:
                        o = x[:, t, c * HALF:(c + 1) * HALF]
                        s = v(lambda: nc.vector.scalar_tensor_tensor(o, bank[:, 0:HALF], total[:, 0, t:t + 1], o, ALU.mult, ALU.add), got)
                        banks.release(b, s)
                return got, finish

            run_units([(0, t, 1) for t in range(TT)], False, aggregate2)
            phase_end()
        gat.close()

        moe = ExitStack()
        slot_row = sb("slot_row", [P, 2, TT], U32, moe)
        slot_token = sb("slot_token", [P, E * MAIN], U32, moe)
        extra_token = sb("extra_token", [P, E * EXTRA], U32, moe)
        overflow = sb("overflow", [P, E * EXTRA], I32, moe)
        any_overflow = sb("any_overflow", [P, 1], I32, moe)
        weights2 = sb("gate_weights", [P, 2, TT], F32, moe)
        with ExitStack() as scope:
            xn = sb("xn3", [P, TT, D], F32, scope)
            xn_ready = layer_norm(xn, dve.last())
            xT_ready = transpose_in(xn, xn_ready)
            xn_stored = (sem("xn_stored"), 16)
            act.wait(xn_ready[-1])
            act.engine.dma_start(slots_dram.rearrange("(t p) d -> p t d", p=P), xn[:, :, :]).then_inc(xn_stored[0], 16)
            stores.append(xn_stored)
            logits = sb("ffn1_logits", [P, TT, E], F32, scope)
            s = router_logits("ffn1_gate", logits, scope)
            best, hot, s = top_two("ffn1", logits[:, :, :], scope, s)
            s = v(lambda: nc.vector.tensor_tensor(weights2[:, 1, :], best[:, 1, :], best[:, 0, :], ALU.subtract), s)
            s = a(lambda: nc.scalar.activation(weights2[:, 1, :], weights2[:, 1, :], ACT.Exp), s)
            s = v(lambda: nc.vector.tensor_scalar(weights2[:, 0, :], weights2[:, 1, :], 1.0, None, ALU.add), s)
            s = v(lambda: nc.vector.reciprocal(weights2[:, 0, :], weights2[:, 0, :]), s)
            s = v(lambda: nc.vector.tensor_tensor(weights2[:, 1, :], weights2[:, 1, :], weights2[:, 0, :], ALU.mult), s)
            gT, gT_ready = gate_matrix("ffn1", weights2, hot, scope, s)
            b2 = sb("ffn1_b2", [E, D], F32, scope)
            b2p = (sb("ffn1_b2_hi", [E, D], F32R, scope), sb("ffn1_b2_lo", [E, D], F32R, scope))
            b2_ready = split(at(b2p, slice(None), slice(None)), b2[:, :], load("ffn1_b2", b2[:, :], ins["ffn1_b2"]))
            pe.wait(b2_ready, gT_ready)
            add_bias(("shared_b2",), 0.1 * 2)
            for t in range(TT):
                for c in range(2):
                    cols = slice(c * HALF, (c + 1) * HALF)
                    b, bank, free = banks.take()
                    pe.wait(free)
                    got = product(bank[:, 0:HALF], [(at(gT, slice(None), tok(t)), at(b2p, slice(None), cols))])
                    s = v(lambda: nc.vector.tensor_tensor(x[:, t, cols], x[:, t, cols], bank[:, 0:HALF], ALU.add), got, dve.last())
                    banks.release(b, s)
            chosen_f = sb("chosen_f", [P, TT, E], F32, scope)
            chosen = sb("chosen", [P, TT, E], F32R, scope)
            before_f = sb("before_f", [P, P], F32, scope)
            before = sb("before", [P, P], F32R, scope)
            s = g(lambda: nc.gpsimd.affine_select(out=before_f[:, :], in_=ones_f[:, :], compare_op=ALU.is_ge, fill=0.0,
                                                  base=-1, pattern=[[1, P]], channel_multiplier=-1))
            before_ready = a(lambda: nc.scalar.activation(before[:, :], before_f[:, :], ACT.Copy), s)
            s = v(lambda: nc.vector.tensor_tensor(chosen_f[:, :, :], hot[:, 0, :, :], hot[:, 1, :, :], ALU.add), dve.last())
            s = g(lambda: nc.gpsimd.affine_select(out=chosen_f[:, TT - 1, :], in_=chosen_f[:, TT - 1, :], compare_op=ALU.is_ge,
                                                  fill=0.0, base=LAST - 1, pattern=[[0, E]], channel_multiplier=-1), s)
            chosen_ready = a(lambda: nc.scalar.activation(chosen[:, :, :], chosen_f[:, :, :], ACT.Copy), s)
            rank = sb("rank", [P, TT, E], F32, scope)
            pe.wait(before_ready, chosen_ready)
            for t in range(TT):
                b, bank, free = banks.take()
                pe.wait(free)
                for k in range(t):
                    nc.tensor.matmul(bank[:, 0:E], ones[:, :], chosen[:, k, :], start=(k == 0), stop=False)
                got = pe.done(nc.tensor.matmul(bank[:, 0:E], before[:, :], chosen[:, t, :], start=(t == 0), stop=True))
                rank_ready = v(lambda: nc.vector.tensor_copy(rank[:, t, :], bank[:, 0:E]), got)
                banks.release(b, rank_ready)
            b, bank, free = banks.take()
            pe.wait(free)
            for k in range(TT):
                end = nc.tensor.matmul(bank[:, 0:E], ones[:, :], chosen[:, k, :], start=(k == 0), stop=(k == TT - 1))
            total = sb("tokens_of_expert", [P, E], F32, scope)
            s = v(lambda: nc.vector.tensor_copy(total[:, :], bank[:, 0:E]), pe.done(end))
            banks.release(b, s)
            most = sb("most_tokens", [P, 1], F32, scope)
            tiles = overflow[:, :].rearrange("p (e n) -> p e n", n=EXTRA)
            for n in range(EXTRA):
                v(lambda: nc.vector.tensor_scalar(tiles[:, :, n], total[:, :], float(CAP + n * P), None, ALU.is_gt), s)
            s = v(lambda: nc.vector.tensor_reduce(most[:, :], total[:, :], AX_X, ALU.max), s)
            v(lambda: nc.vector.tensor_scalar(any_overflow[:, :], most[:, :], float(CAP), None, ALU.is_gt), s)
            row_e = sb("row_of_expert", [P, TT, E], F32, scope)
            picked = sb("picked_row", [P, 2, TT, E], F32, scope)
            row_f = sb("picked_row_f", [P, 2, TT], F32, scope)
            shift = sb("overflow_shift", [P, TT, E], F32, scope)
            over = sb("beyond_first_pass", [P, TT, E], F32, scope)
            v(lambda: nc.vector.scalar_tensor_tensor(row_e[:, :, :], iota8[:, :, :], float(CAP), rank[:, :, :], ALU.mult, ALU.add), rank_ready)
            v(lambda: nc.vector.tensor_scalar(shift[:, :, :], iota8[:, :, :], float(EXTRA * P - CAP), float((E - 1) * CAP), ALU.mult, ALU.add))
            s = v(lambda: nc.vector.tensor_scalar(over[:, :, :], rank[:, :, :], float(CAP), None, ALU.is_ge))
            s = v(lambda: nc.vector.tensor_tensor(shift[:, :, :], shift[:, :, :], over[:, :, :], ALU.mult), s)
            s = v(lambda: nc.vector.tensor_tensor(row_e[:, :, :], row_e[:, :, :], shift[:, :, :], ALU.add), s)
            for k in range(2):
                s = v(lambda: nc.vector.tensor_tensor(picked[:, k, :, :], hot[:, k, :, :], row_e[:, :, :], ALU.mult), s)
                s = v(lambda: nc.vector.tensor_reduce(row_f[:, k, :], picked[:, k, :, :], AX_X, ALU.add), s)
            rows_done = v(lambda: nc.vector.tensor_copy(slot_row[:, :, :], row_f[:, :, :]), s)
            here = sb("rank_or_none", [P, TT, E], F32, scope)
            s = v(lambda: nc.vector.tensor_scalar(here[:, :, :], rank[:, :, :], 1.0, None, ALU.add), rank_ready)
            s = v(lambda: nc.vector.tensor_tensor(here[:, :, :], here[:, :, :], chosen_f[:, :, :], ALU.mult), s, chosen_ready)
            s = v(lambda: nc.vector.tensor_scalar(here[:, :, :], here[:, :, :], -1.0, None, ALU.add), s)
            number_i = sb("token_number_int", [P, TT], I32, scope)
            number = sb("token_number", [P, TT], F16, scope)
            s2 = g(lambda: nc.gpsimd.iota(number_i[:, :], [[P, TT]], base=0, channel_multiplier=1))
            s2 = g(lambda: nc.gpsimd.tensor_copy(number[:, :], number_i[:, :]), s2)
            hot_slot = sb("one_hot_slot", [P, 2, TT, TP], F16, scope)
            hot_free = [None, None]
            dve.wait(s)
            pe.wait(s2)
            b, bank, free = banks.take()
            pe.wait(free)
            for e in range(E):
                dve.wait(hot_free[e % 2])
                for t in range(TT):
                    s = v(lambda: nc.vector.tensor_scalar(hot_slot[:, e % 2, t, :], iota_h[:, :], here[:, t, e:e + 1], None, ALU.is_equal))
                pe.wait(s)
                for st in range(TT):
                    for t in range(TT):
                        end = nc.tensor.matmul(bank[:, e * TT + st:e * TT + st + 1], hot_slot[:, e % 2, t, tok(st)], number[:, t:t + 1],
                                               start=(t == 0), stop=(t == TT - 1))
                hot_free[e % 2] = pe.done(end)
            by_tile = bank[:, 0:E * TT].rearrange("p (e n) -> p e n", n=TT)
            tokens_done = v(lambda: nc.vector.tensor_copy(slot_token[:, :].rearrange("p (e n) -> p e n", n=MAIN), by_tile[:, :, 0:MAIN]), hot_free[1])
            v(lambda: nc.vector.tensor_copy(extra_token[:, :].rearrange("p (e n) -> p e n", n=EXTRA), by_tile[:, :, MAIN:TT]))
            banks.release(b, tokens_done)
            phase_end()

        xg = sb("gathered", [P, 2, 2, D], F32, moe)
        xe = (sb("slots_T_hi", [P, 2, KD, 2 * P], F32R, moe), sb("slots_T_lo", [P, 2, KD, 2 * P], F32R, moe))
        hT = (sb("ffn1_hT_hi", [P, 2, 3, 2 * P], F32R, moe), sb("ffn1_hT_lo", [P, 2, 3, 2 * P], F32R, moe))
        ht = sb("ffn1_tmp", [P, 2, 2 * P], F32, moe)
        yt = sb("ffn1_y", [P, 2, 2, D], F32, moe)
        b1e = sb("ffn1_b1", [P, E, H1 // P], F32, moe)
        b1s = sb("shared_b1", [P, H1 // P], F32, moe)
        act.wait(load("ffn1_b1", b1e[:, :, :], ins["ffn1_b1"]), load("shared_b1", b1s[:, :], ins["shared_b1"]))
        y_banks = psum[4:8]
        y_free = None
        banks = Banks(psum[0:4])
        gather_sem = [sem(f"gathered{n}") for n in range(2)]
        store_sem = [sem(f"rows_stored{n}") for n in range(2)]
        gathers, row_stores = [0, 0], [0, 0]
        state = {"xg_free": [None, None], "xe_read": [None, None], "yt_free": [None, None], "h_read": [None, None], "tmp": [None, None], "n": 0}

        def tiles_of(who, grp):
            return [t for t in (2 * grp, 2 * grp + 1) if t < TT] if who == "shared" else list(range(MAIN))

        def gather(r, e, grp):
            pool.wait(xn_stored, tokens_done, state["xg_free"][r])
            for n, st in enumerate(tiles_of(e, grp)):
                j = e * MAIN + st
                nc.gpsimd.indirect_dma_start(xg[:, r, n, :], None, slots_dram[:, :],
                                             bass.IndirectOffsetOnAxis(ap=slot_token[:, j:j + 1], axis=0)).then_inc(gather_sem[r], 16)
                gathers[r] += 16
            return (gather_sem[r], gathers[r])

        def turn(r, grp, arrived):
            pe.wait(arrived)
            for n, st in enumerate(tiles_of(0, grp)):
                for c in range(2):
                    i, bank, free = banks.take()
                    pe.wait(free)
                    for k in range(3):
                        end = nc.tensor.transpose(bank[:, k * P:(k + 1) * P], xg[:, r, n, (3 * c + k) * P:(3 * c + k + 1) * P], ident[:, :])
                    moved = pe.done(end)
                    s = split(at(xe, slice(None), r, slice(3 * c, 3 * c + 3), slice(n * P, (n + 1) * P)),
                              bank[:, 0:3 * P].rearrange("p (k n) -> p k n", k=3), moved, state["xe_read"][r])
                    banks.release(i, s)
            state["xg_free"][r] = moved
            return s

        expert_passes = [p for p in passes if p[0] != "shared"]
        arrived, turned = {}, {}

        def prepare(n):
            if n < len(expert_passes):
                arrived[n] = gather(n % 2, *expert_passes[n])

        def run_pass(who, grp, source, ready, bias, after_first_chunk):
            nonlocal y_free
            st = tiles_of(who, grp)
            width = P * len(st)

            def hidden(c):
                w, i, w_ready = take_weight("ffn1_w1", who, c)
                pe.wait(w_ready, *ready)
                for m in range(3):
                    b, bank, free = banks.take()
                    pe.wait(free)
                    got = product(bank[:, 0:width], [(at(w, slice(None), k, slice(m * P, (m + 1) * P)), source(k, width)) for k in range(KD)])
                    n = state["n"]
                    state["n"] += 1
                    part = ht[:, n % 2, 0:width]
                    col = 3 * c + m
                    s = a(lambda: nc.scalar.activation(part, bank[:, 0:width], ACT.Relu, bias=bias(col)), got, state["tmp"][n % 2])
                    banks.release(b, s)
                    s = split(at(hT, slice(None), c % 2, m, slice(0, width)), part, s, state["h_read"][c % 2])
                    state["tmp"][n % 2] = s
                drop_weight(i)
                return s

            def output(c, h_ready):
                w, i, w_ready = take_weight("ffn1_w2", who, c)
                pe.wait(w_ready, h_ready)
                if c == 0:
                    pe.wait(y_free)
                for n in range(len(st)):
                    for half in range(2):
                        got = product(y_banks[2 * n + half][:, 0:HALF],
                                      [(at(hT, slice(None), c % 2, k, tok(n)), at(w, slice(None), k, slice(half * HALF, (half + 1) * HALF)))
                                       for k in range(3)], first=(c == 0), last=(c == NCH - 1))
                state["h_read"][c % 2] = got
                drop_weight(i)
                return got

            h_ready = {}
            for c in range(NCH + 1):
                if c < NCH:
                    h_ready[c] = hidden(c)
                if c == 1:
                    after_first_chunk()
                if c > 0:
                    y_done = output(c - 1, h_ready[c - 1])
            if who == "shared":
                for n, t in enumerate(st):
                    for half in range(2):
                        o = x[:, t, half * HALF:(half + 1) * HALF]
                        y_free = v(lambda: nc.vector.scalar_tensor_tensor(o, y_banks[2 * n + half][:, 0:HALF], 0.1 * 2, o, ALU.mult, ALU.add), y_done)
                return
            r = state["n_store"] % 2
            state["n_store"] += 1
            act.wait(y_done, state["yt_free"][r])
            for n, t in enumerate(st):
                for half in range(2):
                    y_free = a(lambda: nc.scalar.activation(yt[:, r, n, half * HALF:(half + 1) * HALF], y_banks[2 * n + half][:, 0:HALF], ACT.Copy))
            pool.wait(y_free)
            row0 = who * CAP
            nc.gpsimd.dma_start(result_dram[row0:row0 + width, :].rearrange("(t p) d -> p t d", p=P), yt[:, r, 0:len(st), :]).then_inc(store_sem[r], 16)
            row_stores[r] += 16
            state["yt_free"][r] = (store_sem[r], row_stores[r])

        state["n_store"] = 0
        n_expert = 0
        prepare(0)
        for n_pass, (who, grp) in enumerate(passes):
            def between():
                if n_expert_next in arrived:
                    expert, group = expert_passes[n_expert_next]
                    turned[n_expert_next] = turn(n_expert_next % 2, group, arrived[n_expert_next])
                    prepare(n_expert_next + 1)
            if who == "shared":
                n_expert_next = 0 if n_pass == 2 else -1
                cols = slice(2 * grp * P, None)
                run_pass(who, grp, lambda k, width: at(xT, slice(None), k, slice(2 * grp * P, 2 * grp * P + width)), tuple(xT_ready),
                         lambda col: b1s[:, col:col + 1], between)
            else:
                n_expert_next = n_expert + 1
                r = n_expert % 2
                run_pass(who, grp, lambda k, width: at(xe, slice(None), r, k, slice(0, width)), (turned[n_expert],),
                         lambda col: b1e[:, who, col:col + 1], between)
                state["xe_read"][r] = pe.last()
                n_expert += 1
        phase_end()
        stored = [(store_sem[r], row_stores[r]) for r in range(2)]

        spill_sems = [sem("spill_" + name) for name in ("pe", "act", "dve", "gather", "bias", "w0", "w1", "store")]
        numbers = [x_.num for x_ in spill_sems]
        assert numbers == list(range(numbers[0], numbers[0] + len(numbers)))
        (s_pe, s_act, s_dve, s_gather, s_bias, s_w0, s_w1, s_store) = spill_sems
        pool.wait(*stored)
        extra_rows = result_dram[E * CAP:E * TP, :].rearrange("(n p) d -> n p d", p=P)

        def overflow_tile(e, i):
            q_pe, q_act, q_dve = Queue(nc.tensor, s_pe), Queue(nc.scalar, s_act), Queue(nc.vector, s_dve)
            index = sb("spill_index", [P, 1], U32, spill)
            bias = sb("spill_b1", [P, H1 // P], F32, spill)
            nc.sync.dma_start(bias[:, :].unsqueeze(1), ins["ffn1_b1"][:, bass.ds(e, 1), :]).then_inc(s_bias, 16)
            index_ready = q_dve.done(nc.vector.tensor_copy(index[:, :], extra_token[:, bass.ds(i, 1)]))
            nc.gpsimd.wait_ge(*index_ready)
            nc.gpsimd.indirect_dma_start(xg[:, 0, 0, :], None, slots_dram[:, :],
                                         bass.IndirectOffsetOnAxis(ap=index[:, :], axis=0)).then_inc(s_gather, 16)
            q_pe.wait((s_gather, 16))
            for c in range(2):
                for k in range(3):
                    end = nc.tensor.transpose(psum[c][:, k * P:(k + 1) * P], xg[:, 0, 0, (3 * c + k) * P:(3 * c + k + 1) * P], ident[:, :])
                turned_now = q_pe.done(end)
                q_act.wait(turned_now)
                src = psum[c][:, 0:3 * P].rearrange("p (k n) -> p k n", k=3)
                hi = q_act.done(nc.scalar.activation(xe[0][:, 0, 3 * c:3 * c + 3, 0:P], src, ACT.Copy))
                q_dve.wait(hi, turned_now)
                x_ready = q_dve.done(nc.vector.tensor_tensor(xe[1][:, 0, 3 * c:3 * c + 3, 0:P], src,
                                                             xe[0][:, 0, 3 * c:3 * c + 3, 0:P].bitcast(F32), ALU.subtract))
            q_act.wait((s_bias, 16))
            w_read = x_ready
            for c in range(NCH):
                for n, (name, sem_w) in enumerate((("ffn1_w1", s_w0), ("ffn1_w2", s_w1))):
                    nc.sync.wait_ge(*w_read)
                    nc.sync.dma_start(raw[:, n:n + 1, :],
                                      ins[name][bass.ds(e * NCH + c, 1), :, :].rearrange("a p n -> p a n")).then_inc(sem_w, 16)
                for n, sem_w in enumerate((s_w0, s_w1)):
                    q_act.wait((sem_w, 16 * (c + 1)), w_read)
                    hi = q_act.done(nc.scalar.activation(whi[:, n, :], raw[:, n, :], ACT.Copy))
                    q_dve.wait(hi, (sem_w, 16 * (c + 1)), w_read)
                    split_done = q_dve.done(nc.vector.tensor_tensor(wlo[:, n, :], raw[:, n, :], whi[:, n, :].bitcast(F32), ALU.subtract))
                w1 = [w_[:, 0, :].rearrange("p (k n) -> p k n", k=KD) for w_ in (whi, wlo)]
                w2 = [w_[:, 1, :].rearrange("p (k n) -> p k n", k=3) for w_ in (whi, wlo)]
                q_pe.wait(split_done, x_ready)
                for m in range(3):
                    for k in range(KD):
                        end = mm3(psum[m][:, 0:P], at(w1, slice(None), k, slice(m * P, (m + 1) * P)), at(xe, slice(None), 0, k, slice(0, P)),
                                  k == 0, k == KD - 1)
                    got = q_pe.done(end)
                    q_act.wait(got, q_dve.last())
                    s_ = q_act.done(nc.scalar.activation(ht[:, 0, 0:P], psum[m][:, 0:P], ACT.Relu, bias=bias[:, 3 * c + m:3 * c + m + 1]))
                    q_act.wait(s_)
                    hi = q_act.done(nc.scalar.activation(hT[0][:, 0, m, 0:P], ht[:, 0, 0:P], ACT.Copy))
                    q_dve.wait(hi)
                    h_ready = q_dve.done(nc.vector.tensor_tensor(hT[1][:, 0, m, 0:P], ht[:, 0, 0:P], hT[0][:, 0, m, 0:P].bitcast(F32), ALU.subtract))
                q_pe.wait(h_ready)
                for half in range(2):
                    for k in range(3):
                        end = mm3(y_banks[half][:, 0:HALF], at(hT, slice(None), 0, k, slice(0, P)),
                                  at(w2, slice(None), k, slice(half * HALF, (half + 1) * HALF)),
                                  c == 0 and k == 0, c == NCH - 1 and k == 2)
                w_read = q_pe.done(end)
            q_act.wait(w_read)
            for half in range(2):
                y_kept = q_act.done(nc.scalar.activation(yt[:, 0, 0, half * HALF:(half + 1) * HALF], y_banks[half][:, 0:HALF], ACT.Copy))
            nc.sync.wait_ge(*y_kept)
            nc.sync.dma_start(extra_rows[bass.ds(i, 1), :, :].rearrange("a p d -> p a d"), yt[:, 0, 0:1, :]).then_inc(s_store, 16)
            nc.sync.wait_ge(s_store, 16)
            nc.gpsimd.wait_ge(s_gather, 16)
            nc.gpsimd.dma_reset(range(s_gather.num, s_gather.num + 1))
            nc.all_engine_barrier(sems_to_clear=range(numbers[0], numbers[0] + len(numbers)))

        with ExitStack() as spill:
            some = nc.values_load(any_overflow[0:1, 0:1], min_val=0, max_val=1)
            with nc.If(some > 0):
                with nc.Fori(0, E) as expert:
                    with nc.Fori(0, EXTRA) as extra:
                        number_ = nc.snap(expert * EXTRA + extra, min_val=0, max_val=E * EXTRA - 1)
                        used = nc.values_load(overflow[0:1, bass.ds(number_, 1)], min_val=0, max_val=1)
                        with nc.If(used > 0):
                            overflow_tile(expert, number_)
        moe_rows = xg[:, :, :, :].rearrange("p a b d -> p (a b) d")

        o_sem = sem("out_stored")
        pool.wait(rows_done, *stored)
        row_sem = [sem(f"row_back{n}") for n in range(4)]
        out_free = [None] * 4
        for t in range(TT):
            n = P if t < TT - 1 else LAST
            for k in range(2):
                i = 2 * t + k
                r = i % 4
                pool.wait(out_free[r])
                nc.gpsimd.indirect_dma_start(moe_rows[0:n, r, :], None, result_dram[:, :],
                                             bass.IndirectOffsetOnAxis(ap=slot_row[0:n, k, t:t + 1], axis=0)).then_inc(row_sem[r], 16)
                s = v(lambda: nc.vector.scalar_tensor_tensor(x[0:n, t, :], moe_rows[0:n, r, :], weights2[0:n, k, t:t + 1], x[0:n, t, :],
                                                             ALU.mult, ALU.add), (row_sem[r], 16 * (i // 4 + 1)), dve.last())
                out_free[r] = s
            sp.wait(s)
            sp.engine.dma_start(out[t * P:t * P + n, :], x[0:n, t, :]).then_inc(o_sem, 16)
        stores.append((o_sem, 16 * TT))
        sp.wait(*stores, *stored)
        moe.close()


def _columns(w, n, k=KD):
    c = w.shape[1] // n
    return w.reshape(k, P, n, c).transpose(2, 1, 0, 3).reshape(n, P, k * c)


def _rows(w, k):
    return w.reshape(-1, k, P, w.shape[1]).transpose(0, 2, 1, 3).reshape(-1, P, k * w.shape[1])


def kernel(**inputs):
    import numpy as np
    import concourse.bacc as bacc
    from concourse.bass_utils import run_bass_kernel_spmd

    i = {name: np.asarray(value) for name, value in inputs.items()}
    w_map = i["L0_mix_w_map"].T
    qkv = i["L1_mix_w_qkv"]

    def kv_chunks(w):
        k, v = _columns(w[:, D:2 * D], 2), _columns(w[:, 2 * D:], 2)
        return np.stack([k, v], 1).reshape(4, P, WC)

    arrays = {
        "x": i["x"], "src": i["src"].reshape(EP, EC), "dst": i["dst"].reshape(EP, EC),
        "gnn0_w1": _columns(i["L0_gnn_W1"], 2), "gnn0_w2": _columns(i["L0_gnn_W2"], 2),
        "gnn0_b1": i["L0_gnn_b1"].reshape(KD, P).T, "gnn0_b2": i["L0_gnn_b2"],
        "mix0_q": _columns(w_map[:, 0:D], 2), "mix0_kv": kv_chunks(w_map), "mix0_out": _rows(i["L0_mix_w_out"].T, 3),
        "mix0_gk": i["L0_mix_g_k"], "mix0_bk": i["L0_mix_b_k"], "mix0_gv": i["L0_mix_g_v"], "mix0_bv": i["L0_mix_b_v"],
        "mix0_b": i["L0_mix_b_out"],
        "ffn0_gate": i["L0_ffn_gate_w"].reshape(E, KD, P).transpose(2, 1, 0),
        "ffn0_w1": _columns(i["L0_ffn_w1"].transpose(1, 0, 2).reshape(D, E * H0), 4),
        "ffn0_b1": i["L0_ffn_b1"].reshape(KH0, P).T,
        "ffn0_w2": np.concatenate([_columns(w, 2) for w in i["L0_ffn_w2"].reshape(2, D, D)]), "ffn0_b2": i["L0_ffn_b2"],
        "gat_w1": _columns(i["L1_gnn_W1"].T, 4), "gat_as1": i["L1_gnn_att_src1"].reshape(-1),
        "gat_ad1": i["L1_gnn_att_dst1"].reshape(-1), "gat_b1": i["L1_gnn_b1"].reshape(G1, P).T,
        "gat_w2": _rows(i["L1_gnn_W2"].T, 2), "gat_as2": i["L1_gnn_att_src2"].reshape(-1),
        "gat_ad2": i["L1_gnn_att_dst2"].reshape(-1), "gat_b2": i["L1_gnn_b2"],
        "mix1_q": _columns(qkv[:, 0:D], 2), "mix1_kv": kv_chunks(qkv), "mix1_out": _rows(i["L1_mix_w_proj"], 3),
        "mix1_b": i["L1_mix_b_proj"],
        "ffn1_gate": i["L1_ffn_Wr"].reshape(E, KD, P).transpose(2, 1, 0),
        "ffn1_w1": np.concatenate([_columns(w.T, NCH) for w in i["L1_ffn_W1"]]),
        "ffn1_w2": np.concatenate([_rows(w.T, 3) for w in i["L1_ffn_W2"]]),
        "ffn1_b1": i["L1_ffn_b1"].reshape(E, H1 // P, P).transpose(2, 0, 1), "ffn1_b2": i["L1_ffn_b2"],
        "shared_w1": _columns(i["L1_ffn_sW1"].T, NCH), "shared_w2": _rows(i["L1_ffn_sW2"].T, 3),
        "shared_b1": i["L1_ffn_sb1"].reshape(H1 // P, P).T, "shared_b2": i["L1_ffn_sb2"],
    }
    nc = bacc.Bacc("TRN2", target_bir_lowering=False, num_devices=1)
    arrays = {name: np.ascontiguousarray(value) for name, value in arrays.items()}
    aps = {name: nc.dram_tensor("in_" + name, value.shape, mybir.dt.from_np(value.dtype), kind="ExternalInput").ap()
           for name, value in arrays.items()}
    out = nc.dram_tensor("out", (T, D), F32, kind="ExternalOutput").ap()
    slots = nc.dram_tensor("tokens_normed", (TP, D), F32, kind="Internal").ap()
    result = nc.dram_tensor("expert_rows", (E * TP, D), F32, kind="Internal").ap()
    build(nc, aps, out, slots, result)
    run = run_bass_kernel_spmd(nc, [{"in_" + name: value for name, value in arrays.items()}], core_ids=[0])
    return run.results[0]["out"]
```

```python
from contextlib import ExitStack

import concourse.bass as bass
from concourse import mybir

F32 = mybir.dt.float32
F32R = mybir.dt.float32r
F16 = mybir.dt.float16
I32 = mybir.dt.int32
U32 = mybir.dt.uint32
ACT = mybir.ActivationFunctionType
ALU = mybir.AluOpType
AX_X = mybir.AxisListType.X

P = 128
T = 625
TT = (T + P - 1) // P
TP = TT * P
LAST = T - (TT - 1) * P
D = 768
KD = D // P
HALF = D // 2
NE = 20000
EP = 125
EC = NE // EP
TM = T // 2 + 1
PACK = 4096
CHUNK_E = 32
assert CHUNK_E * EP < PACK and EC % CHUNK_E == 0 and PACK * CHUNK_E * EP < 2 ** 24
HEADS = 12
DH = 64
PAIRS = HEADS // 2
E = 8
H0 = 192
KH0 = E * H0 // P
G1 = 8
C1 = G1 * P
H1 = 3072
WC = KD * HALF
NCH = H1 // HALF
MAIN = 2
CAP = MAIN * P
EXTRA = TT - MAIN
PREPARE_FROM = 4
NEG = -1.0e30
LN_EPS = 1e-5
SLOPE = 0.2
TOKEN_SPANS = [(0, 320), (320, 306)]


class Queue:

    def __init__(self, engine, semaphore):
        self.engine, self.semaphore, self.count, self.seen = engine, semaphore, 0, {}

    def wait(self, *tokens):
        for token in tokens:
            if token is None:
                continue
            semaphore, value = token
            if self.seen.get(semaphore.name, 0) < value:
                self.engine.wait_ge(semaphore, value)
                self.seen[semaphore.name] = value

    def done(self, instruction):
        self.count += 1
        instruction.then_inc(self.semaphore, 1)
        return (self.semaphore, self.count)

    def last(self):
        return (self.semaphore, self.count) if self.count else None


class Banks:

    def __init__(self, banks):
        self.banks, self.free, self.at, self.held = banks, [None] * len(banks), 0, set()

    def take(self):
        while self.at % len(self.banks) in self.held:
            self.at += 1
        i = self.at % len(self.banks)
        self.at += 1
        self.held.add(i)
        assert len(self.held) < len(self.banks)
        return i, self.banks[i], self.free[i]

    def release(self, i, token):
        self.free[i] = token
        self.held.discard(i)


def build(nc, ins, out, slots_dram, result_dram):
    with ExitStack() as ctx:
        def sb(name, shape, dt=F32, scope=None):
            return (scope or ctx).enter_context(nc.sbuf_tensor(name, shape, dt))

        def sem(name):
            return ctx.enter_context(nc.semaphore(name))

        pe = Queue(nc.tensor, sem("pe_done"))
        act = Queue(nc.scalar, sem("act_done"))
        dve = Queue(nc.vector, sem("dve_done"))
        pool = Queue(nc.gpsimd, sem("pool_done"))
        sp = Queue(nc.sync, sem("sp_done"))
        engines = (pe, act, dve, pool)
        stores = []

        def phase_end():
            ends = [q.last() for q in engines]
            for q in (act, dve, pool, sp):
                q.wait(*ends, *stores)

        def load(name, dst, src, *after, queue=sp):
            s = sem("in_" + name)
            queue.wait(*after)
            queue.engine.dma_start(dst, src).then_inc(s, 16)
            return (s, 16)

        psum = [ctx.enter_context(nc.psum_tensor(f"bank{i}", [P, 512], F32)) for i in range(8)]
        banks = Banks(psum)

        order = []
        def mix_order(kind):
            return ([(kind + "_kv", i) for i in range(4)] + [(kind + "_q", 0), (kind + "_q", 1)]
                    + [(kind + "_out", 0), (kind + "_out", 1)])

        order += mix_order("mix0") + [(f"gnn0_w{n}", i) for n in (1, 2) for i in range(2)]
        for half in range(2):
            order += [(f"ffn0_w{n}", 2 * half + i) for n in (1, 2) for i in range(2)]
        order += mix_order("mix1")
        order += [("gat_w1", 0)] + [key for g in range(3) for key in (("gat_w1", g + 1), ("gat_w2", g))] + [("gat_w2", 3)]
        for who in ["shared"] + list(range(E)):
            for c in range(NCH + 1):
                if c < NCH:
                    order.append(("ffn1_w1", who, c))
                if c > 0:
                    order.append(("ffn1_w2", who, c - 1))

        def weight_source(key):
            if key[0] in ("ffn1_w1", "ffn1_w2"):
                if key[1] == "shared":
                    return ins["shared" + key[0][4:]][key[2]]
                return ins[key[0]][key[1] * NCH + key[2]]
            return ins[key[0]][key[1]]

        RAW, PAIR = 2, 3
        raw = sb("weight_raw", [P, RAW, WC])
        whi = sb("weight_hi", [P, PAIR, WC], F32R)
        wlo = sb("weight_lo", [P, PAIR, WC], F32R)
        raw_sem = [sem(f"weight_landed{i}") for i in range(RAW)]
        stream = {"loaded": 0, "split": 0, "used": 0}
        raw_free, pair_free, landed, pair_ready = {}, {}, {}, {}

        def stream_load():
            i = stream["loaded"]
            if i >= len(order):
                return
            src = weight_source(order[i])
            sp.wait(raw_free.get(i - RAW))
            sp.engine.dma_start(raw[:, i % RAW, 0:src.shape[1]], src).then_inc(raw_sem[i % RAW], 16)
            landed[i] = (raw_sem[i % RAW], 16 * (i // RAW + 1))
            stream["loaded"] += 1

        def stream_split(limit=None):
            while stream["split"] < (len(order) if limit is None else limit):
                i = stream["split"]
                if i >= PAIR and i - PAIR not in pair_free:
                    return
                w = weight_source(order[i]).shape[1]
                r, h = i % RAW, i % PAIR
                act.wait(landed[i], pair_free.get(i - PAIR))
                hi_done = act.done(nc.scalar.activation(whi[:, h, 0:w], raw[:, r, 0:w], ACT.Copy))
                dve.wait(landed[i], hi_done, pair_free.get(i - PAIR))
                lo_done = dve.done(nc.vector.tensor_tensor(wlo[:, h, 0:w], raw[:, r, 0:w],
                                                           whi[:, h, 0:w].bitcast(F32), ALU.subtract))
                pair_ready[i] = lo_done
                raw_free[i] = lo_done
                stream["split"] += 1
                stream_load()

        def take_weight(*key):
            i = stream["used"]
            assert order[i] == key, (order[i], key)
            stream["used"] += 1
            stream_split()
            w = weight_source(key).shape[1]
            kt = {"mix0_out": 3, "mix1_out": 3, "ffn1_w2": 3, "gat_w2": 2}.get(key[0], KD)
            hi = whi[:, i % PAIR, 0:w].rearrange("p (k n) -> p k n", k=kt)
            lo = wlo[:, i % PAIR, 0:w].rearrange("p (k n) -> p k n", k=kt)
            return (hi, lo), i, pair_ready[i]

        def drop_weight(i):
            pair_free[i] = pe.last()
            stream_split()

        stream_load()
        stream_load()

        def mm3(dst, a, b, first, last):
            nc.tensor.matmul(dst, a[0], b[0], start=first, stop=False)
            nc.tensor.matmul(dst, a[0], b[1], start=False, stop=False)
            return nc.tensor.matmul(dst, a[1], b[0], start=False, stop=last)

        def product(dst, terms, first=True, last=True):
            terms = list(terms)
            for n, (a, b) in enumerate(terms):
                end = mm3(dst, a, b, first and n == 0, last and n == len(terms) - 1)
            return pe.done(end)

        def product_exact_a(dst, terms):
            terms = list(terms)
            for n, (a, b) in enumerate(terms):
                nc.tensor.matmul(dst, a, b[0], start=(n == 0), stop=False)
                end = nc.tensor.matmul(dst, a, b[1], start=False, stop=(n == len(terms) - 1))
            return pe.done(end)

        def split(pair, src, *after):
            act.wait(*after)
            hi_done = act.done(nc.scalar.activation(pair[0], src, ACT.Copy))
            dve.wait(hi_done, *after)
            return dve.done(nc.vector.tensor_tensor(pair[1], src, pair[0].bitcast(F32), ALU.subtract))

        def at(pair, *index):
            return (pair[0].__getitem__(index), pair[1].__getitem__(index))

        def v(instruction, *after):
            dve.wait(*after)
            return dve.done(instruction())

        def a(instruction, *after):
            act.wait(*after)
            return act.done(instruction())

        def g(instruction, *after):
            pool.wait(*after)
            return pool.done(instruction())

        ident = sb("identity", [P, P])
        ones = sb("ones", [P, P], F32R)
        iota_h = sb("iota_half", [P, TP], F16)
        ones_f = sb("ones_f", [P, P])
        c1 = g(lambda: nc.gpsimd.memset(ident[:, :], 0.0))
        c2 = g(lambda: nc.gpsimd.affine_select(out=ident[:, :], in_=ident[:, :], compare_op=ALU.not_equal, fill=1.0,
                                               base=0, pattern=[[-1, P]], channel_multiplier=1), c1)
        c3 = g(lambda: nc.gpsimd.memset(ones_f[:, :], 1.0))
        ones_ready = a(lambda: nc.scalar.activation(ones[:, :], ones_f[:, :], ACT.Copy), c3)

        x = sb("x", [P, TT, D])
        xT = (sb("xT_hi", [P, KD, TP], F32R), sb("xT_lo", [P, KD, TP], F32R))
        count = sb("edge_count", [P, TT, TP], mybir.dt.uint16)
        bias0 = sb("bias_row", [P, D])
        stats = sb("ln_stats", [P, TT, 2, 6])
        moments = sb("ln_moments", [P, TT, 2])
        rstd = sb("ln_rstd", [P, TT])
        start = ExitStack()
        iota_i = sb("iota_int", [P, TP], I32, start)
        edges_i = sb("edges_int", [EP, 2, EC], I32, start)
        c4 = g(lambda: nc.gpsimd.iota(iota_i[:, :], [[1, TP]], base=0, channel_multiplier=0))
        c5 = g(lambda: nc.gpsimd.tensor_copy(iota_h[:, :], iota_i[:, :]), c4)
        const_ready = c5
        zero_x = v(lambda: nc.vector.memset(x[96:P, TT - 1, :], 0.0))
        x_sem = sem("in_x")
        sp.wait(zero_x)
        sp.engine.dma_start(x[:, 0:TT - 1, :], ins["x"][0:(TT - 1) * P, :].rearrange("(t p) d -> p t d", p=P)).then_inc(x_sem, 16)
        sp.engine.dma_start(x[0:LAST, TT - 1, :], ins["x"][(TT - 1) * P:T, :]).then_inc(x_sem, 16)
        x_ready = (x_sem, 32)
        edge_sem = sem("in_edges")
        sp.engine.dma_start(edges_i[:, 0, :], ins["src"]).then_inc(edge_sem, 16)
        sp.engine.dma_start(edges_i[:, 1, :], ins["dst"]).then_inc(edge_sem, 16)
        edges_ready = (edge_sem, 32)
        zeros = v(lambda: nc.vector.memset(bias0[:, :], 0.0))
        zeroed = (sem("overflow_zeroed"), 16)
        act.wait(zeros, x_ready, edges_ready)
        act.engine.dma_start(result_dram[E * CAP:E * TP, :].rearrange("(n p) d -> p n d", p=P),
                             bias0[:, :].unsqueeze(1).broadcast_to([P, E * EXTRA, D])).then_inc(zeroed[0], 16)
        stores.append(zeroed)


        def layer_norm(xn, *after):
            for t in range(TT):
                for h in range(2):
                    s = v(lambda: nc.vector.bn_stats(stats[:, t, h, :], x[:, t, h * HALF:(h + 1) * HALF]), *after)
            dve.wait(s)
            for t in range(TT):
                s = v(lambda: nc.vector.bn_aggr(moments[:, t, :], stats[:, t, :, :].rearrange("p a b -> p (a b)")))
            s = v(lambda: nc.vector.tensor_scalar(rstd[:, :], moments[:, :, 1], LN_EPS, None, ALU.add), s)
            s = a(lambda: nc.scalar.activation(rstd[:, :], rstd[:, :], ACT.Sqrt), s)
            s = v(lambda: nc.vector.reciprocal(rstd[:, :], rstd[:, :]), s)
            dve.wait(s)
            return [v(lambda: nc.vector.tensor_scalar(xn[:, t, :], x[:, t, :], moments[:, t, 0:1], rstd[:, t:t + 1],
                                                      ALU.subtract, ALU.mult)) for t in range(TT)]

        def transpose_in(xn, ready, *after):
            done = []
            for t in range(TT):
                for c in range(2):
                    i, bank, free = banks.take()
                    pe.wait(ready[t], free, *after)
                    for k in range(3):
                        end = nc.tensor.transpose(bank[:, k * P:(k + 1) * P],
                                                  xn[:, t, (3 * c + k) * P:(3 * c + k + 1) * P], ident[:, :])
                    moved = pe.done(end)
                    part = at(xT, slice(None), slice(3 * c, 3 * c + 3), slice(t * P, (t + 1) * P))
                    s = split(part, bank[:, 0:3 * P].rearrange("p (k n) -> p k n", k=3), moved)
                    banks.release(i, s)
                done.append(s)
            return done

        def tok(t):
            return slice(t * P, (t + 1) * P)


        def row_load(name, dst, src, n, *after):
            return load(name, dst, src.rearrange("(a n) -> a n", a=1).broadcast_to([P, n]), *after)

        with ExitStack() as scope:
            xn = sb("xn0", [P, TT, D], scope=scope)
            pe.wait(c2)
            xT_ready = transpose_in(xn, layer_norm(xn, x_ready))

            edge = sb("edges", [EP, 4, EC], scope=scope)
            s = v(lambda: nc.vector.tensor_copy(edge[:, 0:2, :], edges_i[:, :, :]), edges_ready)
            s = v(lambda: nc.vector.tensor_scalar(edge[:, 3, :], edge[:, 1, :], float(TM), None, ALU.is_ge), s)
            s = v(lambda: nc.vector.tensor_scalar(edge[:, 2, :], edge[:, 3, :], float(PACK - 1), 1.0, ALU.mult, ALU.add), s)
            s = v(lambda: nc.vector.scalar_tensor_tensor(edge[:, 1, :], edge[:, 3, :], -float(TM), edge[:, 1, :],
                                                         ALU.mult, ALU.add), s)
            fold_ready = s
            RING = 4
            hot_src = sb("one_hot_src", [EP, RING, TP], F16, scope)
            hot_dst = sb("one_hot_dst", [EP, RING, 320], F16, scope)
            whole = sb("packed_counts", [P, TT, TM], I32, scope)
            low = sb("low_counts", [P, TT, TM], I32, scope)
            high = sb("high_counts", [P, TT, TM], I32, scope)
            cnt = sb("counts", [P, TT, TP], I32, scope)
            counted = g(lambda: nc.gpsimd.memset(cnt[:, :, :], 0))
            hot_free = [None] * RING
            dve.wait(const_ready, fold_ready)
            unpacked = None
            whole_free = None
            for chunk in range(EC // CHUNK_E):
                if chunk > 0:
                    stream_split(chunk)
                taken = [banks.take() for _ in range(TT)]
                for n in range(CHUNK_E):
                    j = chunk * CHUNK_E + n
                    r = j % RING
                    dve.wait(hot_free[r])
                    v(lambda: nc.vector.tensor_scalar(hot_src[:, r, :], iota_h[0:EP, :], edge[:, 0, j:j + 1], None, ALU.is_equal))
                    hot = v(lambda: nc.vector.tensor_scalar(hot_dst[:, r, :], iota_h[0:EP, 0:320], edge[:, 1, j:j + 1],
                                                            edge[:, 2, j:j + 1], ALU.is_equal, ALU.mult))
                    pe.wait(hot)
                    for t in range(TT):
                        if n == 0:
                            pe.wait(taken[t][2])
                        end = nc.tensor.matmul(taken[t][1][:, 0:TM], hot_src[:, r, tok(t)], hot_dst[:, r, 0:TM],
                                               start=(n == 0), stop=(n == CHUNK_E - 1))
                    hot_free[r] = pe.done(end)
                for t in range(TT):
                    got = a(lambda: nc.scalar.activation(whole[:, t, :], taken[t][1][:, 0:TM], ACT.Copy),
                            hot_free[r], whole_free)
                    banks.release(taken[t][0], got)
                v(lambda: nc.vector.tensor_scalar(low[:, :, :], whole[:, :, :], PACK - 1, None, ALU.bitwise_and), got, unpacked)
                cut = v(lambda: nc.vector.tensor_scalar(high[:, :, :], whole[:, :, :], 12, None, ALU.logical_shift_right))
                whole_free = cut
                counted = g(lambda: nc.gpsimd.tensor_tensor(cnt[:, :, 0:TM], cnt[:, :, 0:TM], low[:, :, :], ALU.add), cut, counted)
                counted = g(lambda: nc.gpsimd.tensor_tensor(cnt[:, :, TM:T], cnt[:, :, TM:T], high[:, :, 0:T - TM], ALU.add), counted)
                unpacked = counted
            counts_kept = v(lambda: nc.vector.tensor_copy(count[:, :, :], cnt[:, :, :]), counted)
            phase_end()
        start.close()

        def add_bias(names, scale=None):
            for name in names:
                s = row_load(name, bias0[:, :], ins[name], D, dve.last())
                if scale is not None:
                    s = v(lambda: nc.vector.tensor_scalar(bias0[:, :], bias0[:, :], scale, None, ALU.mult), s)
                dve.wait(s)
                for t in range(TT):
                    s = v(lambda: nc.vector.tensor_tensor(x[:, t, :], x[:, t, :], bias0[:, :], ALU.add), dve.last())
            return s

        def add_tokens(pairs_of, n_terms, weight, cols, c0, ready):
            for t in range(TT):
                i, bank, free = banks.take()
                pe.wait(free, *ready)
                got = product(bank[:, 0:cols], [(pairs_of(k, t), at(weight, slice(None), k, slice(0, cols))) for k in range(n_terms)])
                s = v(lambda: nc.vector.tensor_tensor(x[:, t, c0:c0 + cols], x[:, t, c0:c0 + cols], bank[:, 0:cols], ALU.add), got)
                banks.release(i, s)
            return s

        def linear_attention(kind, finish_kv, finish_q, normalised):
            with ExitStack() as scope:
                kv = sb(kind + "_kv", [P, 2, TT, HALF], F32, scope)
                KV = 3
                kvp = (sb(kind + "_kv_hi", [P, KV, TT, HALF], F32R, scope), sb(kind + "_kv_lo", [P, KV, TT, HALF], F32R, scope))
                att = (sb(kind + "_att_hi", [P, PAIRS, P], F32R, scope), sb(kind + "_att_lo", [P, PAIRS, P], F32R, scope))
                attf = sb(kind + "_att", [P, PAIRS, P], F32, scope)
                s0 = v(lambda: nc.vector.memset(attf[:, :, :], 0.0))
                if normalised:
                    den = (sb(kind + "_den_hi", [P, PAIRS, P], F32R, scope), sb(kind + "_den_lo", [P, PAIRS, P], F32R, scope))
                    denf = sb(kind + "_den", [P, PAIRS, P], F32, scope)
                    s0 = v(lambda: nc.vector.memset(denf[:, :, :], 0.0))
                rows = finish_kv(None, kv, scope)
                kv_free, pair_read = [None, None], [None] * KV
                sizes = [P] * (TT - 1) + [LAST]

                def keys_or_values(n):
                    r, which = n % 2, n % 2
                    w, i, ready = take_weight(kind + "_kv", n)
                    pe.wait(ready, *xT_ready)
                    for t in range(TT):
                        b, bank, free = banks.take()
                        pe.wait(free)
                        got = product(bank[:, 0:HALF], [(at(xT, slice(None), k, tok(t)), at(w, slice(None), k, slice(None))) for k in range(KD)])
                        s = a(lambda: nc.scalar.activation(kv[:, r, t, :], bank[:, 0:HALF], ACT.Copy), got, kv_free[r])
                        banks.release(b, s)
                    drop_weight(i)
                    s = finish_kv(which, kv, rows, s)
                    kv_free[r] = split(at(kvp, slice(None), n % KV, slice(None), slice(None)), kv[:, r, :, :], s, pair_read[n % KV])
                    return kv_free[r]

                def per_head_products(grp, ready):
                    pk, pv = (2 * grp) % KV, (2 * grp + 1) % KV
                    pe.wait(ready)
                    for pr in range(3):
                        b, bank, free = banks.take()
                        pe.wait(free)
                        cols = slice(pr * P, (pr + 1) * P)
                        kv_read = product(bank[:, 0:P], [(at(kvp, slice(0, n), pk, t, cols), at(kvp, slice(0, n), pv, t, cols))
                                                         for t, n in enumerate(sizes)])
                        for h in range(2):
                            blk = slice(h * DH, (h + 1) * DH)
                            s = v(lambda: nc.vector.tensor_scalar(attf[blk, 3 * grp + pr, blk], bank[blk, h * DH:(h + 1) * DH],
                                                                  1.0 if normalised else 1.0 / T, None, ALU.mult), kv_read, s0)
                        banks.release(b, s)
                        if normalised:
                            b, bank, free = banks.take()
                            pe.wait(free)
                            for t, n in enumerate(sizes):
                                nc.tensor.matmul(bank[:, 0:P], kvp[0][0:n, pk, t, cols], ones[0:n, :], start=(t == 0), stop=False)
                                end = nc.tensor.matmul(bank[:, 0:P], kvp[1][0:n, pk, t, cols], ones[0:n, :], start=False, stop=(t == TT - 1))
                            kv_read = pe.done(end)
                            for h in range(2):
                                blk = slice(h * DH, (h + 1) * DH)
                                s = v(lambda: nc.vector.tensor_copy(denf[blk, 3 * grp + pr, blk], bank[blk, h * DH:(h + 1) * DH]), kv_read)
                            banks.release(b, s)
                    pair_read[pk] = pair_read[pv] = pe.last()
                    return s

                keys_or_values(0)
                first_ready = keys_or_values(1)
                keys_or_values(2)
                per_head_products(0, first_ready)
                last_ready = keys_or_values(3)
                flat = [b[:, :, :, :].rearrange("p a b c -> p (a b c)").rearrange("p (r n) -> p r n", n=TP) for b in kvp]
                per_part = TT * HALF // TP
                qp = tuple(f[:, per_part:per_part + 2] for f in flat)
                outT = tuple(f[:, 2 * per_part:2 * per_part + 3] for f in flat)
                work = kv[:, :, :, :].rearrange("p a b c -> p (a b c)").rearrange("p (r n) -> p r n", n=TP)
                q_tmp, q_tmp2, d_tmp = work[:, 0:3:2], work[:, 1:4:2], work[:, 4:6]
                pads = slice(T + 1, TP)
                zeros = sb(kind + "_zeros", [P, 3, TP - T - 1], F32, scope)
                zero = v(lambda: nc.vector.memset(zeros[:, :, :], 0.0))
                q_read = [split(at(qp, slice(None), slice(None), pads), zeros[:, 0:2, :], zero, pair_read[1])] * 2
                tmp_free, d_free = [last_ready, last_ready], [last_ready, last_ready]

                def queries(n, w, ready):
                    r = n % 2
                    for c0, width in TOKEN_SPANS:
                        b, bank, free = banks.take()
                        pe.wait(free, ready)
                        tk = product(bank[:, 0:width], [(at(w, slice(None), k, slice((n % 3) * P, (n % 3 + 1) * P)),
                                                         at(xT, slice(None), k, slice(c0, c0 + width))) for k in range(KD)])
                        s = finish_q(q_tmp[:, r, c0:c0 + width], q_tmp2[:, r, c0:c0 + width], bank[:, 0:width], tk, b, tmp_free[r])
                        s = split(at(qp, slice(None), r, slice(c0, c0 + width)), q_tmp[:, r, c0:c0 + width], s, q_read[r])
                    tmp_free[r] = s
                    return s

                def attend(n, q_ready):
                    r = n % 2
                    pe.wait(q_ready, att_ready)
                    for c0, width in TOKEN_SPANS:
                        b, bank, free = banks.take()
                        pe.wait(free)
                        q = at(qp, slice(None), r, slice(c0, c0 + width))
                        tk = product(bank[:, 0:width], [(at(att, slice(None), n, slice(None)), q)])
                        o = at(outT, slice(None), n % 3, slice(c0, c0 + width))
                        if normalised:
                            b2, bank2, free = banks.take()
                            pe.wait(free)
                            tk2 = product(bank2[:, 0:width], [(at(den, slice(None), n, slice(None)), q)])
                            d = d_tmp[:, r, c0:c0 + width]
                            s = v(lambda: nc.vector.reciprocal(d, bank2[:, 0:width]), tk2, d_free[r])
                            banks.release(b2, s)
                            s = v(lambda: nc.vector.tensor_tensor(d, bank[:, 0:width], d, ALU.mult), tk, s)
                            banks.release(b, s)
                            s = split(o, d, s, out_read)
                        else:
                            s = split(o, bank[:, 0:width], tk, out_read)
                            banks.release(b, s)
                    d_free[r] = s
                    q_read[r] = pe.last()
                    return s

                w, held, ready = take_weight(kind + "_q", 0)
                q_ready = {n: queries(n, w, ready) for n in range(2)}
                s = per_head_products(1, last_ready)
                att_ready = split(at(att, slice(None), slice(None), slice(None)), attf[:, :, :], s)
                if normalised:
                    att_ready = split(at(den, slice(None), slice(None), slice(None)), denf[:, :, :], s)
                out_read = split(at(outT, slice(None), slice(None), pads), zeros[:, :, :], pair_read[2])
                for n in range(PAIRS):
                    s = attend(n, q_ready[n])
                    if n + 2 == 3:
                        drop_weight(held)
                        w, held, ready = take_weight(kind + "_q", 1)
                    if n + 2 < PAIRS:
                        q_ready[n + 2] = queries(n + 2, w, ready)
                    elif n + 2 == PAIRS:
                        drop_weight(held)
                    if n % 3 == 2:
                        wo, i, o_ready = take_weight(kind + "_out", n // 3)
                        for c in range(2):
                            part = at(wo, slice(None), slice(None), slice(c * HALF, (c + 1) * HALF))
                            add_tokens(lambda k, t: at(outT, slice(None), k, tok(t)), 3, part, HALF, c * HALF, (o_ready, s))
                        out_read = pe.last()
                        drop_weight(i)
                phase_end()

        def kv0(which, kv, rows, after=None):
            if which is None:
                scope = rows
                gb = sb("gain_shift_rows", [P, 4, DH], F32, scope)
                for n, name in enumerate(("mix0_gk", "mix0_bk", "mix0_gv", "mix0_bv")):
                    got = row_load(name, gb[:, n, :], ins[name], DH)
                    dve.wait(got)
                return gb, sb("kv_square", [P, TT * 6, DH], F32, scope), sb("kv_stats", [P, 3, TT * 6], F32, scope)
            gb, sq, st = rows
            z = [kv[:, which, t, :].rearrange("p (h d) -> p h d", d=DH) for t in range(TT)]
            n6 = lambda i, t: st[:, i, 6 * t:6 * t + 6]
            wide = lambda ap: ap.unsqueeze(2).broadcast_to([P, 6, DH])
            gain = lambda i: gb[:, i, :].unsqueeze(1).broadcast_to([P, 6, DH])
            sqt = lambda t: sq[:, 6 * t:6 * t + 6, :]
            every = range(TT)
            for t in every:
                s = v(lambda: nc.vector.tensor_reduce(n6(0, t), z[t], AX_X, ALU.add), after)
            s = v(lambda: nc.vector.tensor_scalar(st[:, 0, :], st[:, 0, :], 1.0 / DH, None, ALU.mult), s)
            dve.wait(s)
            for t in every:
                s = v(lambda: nc.vector.tensor_tensor(z[t], z[t], wide(n6(0, t)), ALU.subtract))
            act.wait(s)
            for t in every:
                s = a(lambda: nc.scalar.activation(sqt(t), z[t], ACT.Square))
            s = v(lambda: nc.vector.tensor_reduce(st[:, 1, :], sq[:, :, :], AX_X, ALU.add), s)
            s = v(lambda: nc.vector.tensor_scalar(st[:, 1, :], st[:, 1, :], 1.0 / DH, LN_EPS, ALU.mult, ALU.add), s)
            s = a(lambda: nc.scalar.activation(st[:, 1, :], st[:, 1, :], ACT.Sqrt), s)
            s = v(lambda: nc.vector.reciprocal(st[:, 2, :], st[:, 1, :]), s)
            for step in range(3):
                dve.wait(s)
                for t in every:
                    o = (wide(n6(2, t)), gain(2 * which), gain(2 * which + 1))[step]
                    s = v(lambda: nc.vector.tensor_tensor(z[t], z[t], o, ALU.add if step == 2 else ALU.mult))
            return s

        def q0(q, tmp, bank, got, b, free):
            s = a(lambda: nc.scalar.activation(q, bank, ACT.Copy), got, free)
            banks.release(b, s)
            return s

        linear_attention("mix0", kv0, q0, False)

        gcn = ExitStack()
        adj = (sb("adj_hi", [P, TT, TP], F32R, gcn), sb("adj_lo", [P, TT, TP], F32R, gcn))
        h = (sb("gcn_h_hi", [P, TT, D], F32R, gcn), sb("gcn_h_lo", [P, TT, D], F32R, gcn))
        bcol = sb("gcn_b1", [P, KD], F32, gcn)
        b1_ready = load("gcn_b1", bcol[:, :], ins["gnn0_b1"])
        z_tmp = sb("gcn_tmp", [P, 2, 320], F32, gcn)

        def node_product(key, src, ready):
            for c in range(2):
                w, i, w_ready = take_weight(key, c)
                for t in range(TT):
                    b, bank, free = banks.take()
                    pe.wait(free, w_ready, *ready)
                    got = product(bank[:, 0:HALF], [(at(src, slice(None), k, tok(t)), at(w, slice(None), k, slice(None))) for k in range(KD)])
                    s = split(at(h, slice(None), t, slice(c * HALF, (c + 1) * HALF)), bank[:, 0:HALF], got)
                    banks.release(b, s)
                    if t == TT - 1:
                        drop_weight(i)
                    yield s

        first = node_product("gnn0_w1", xT, xT_ready)
        with ExitStack() as scope:
            loops = sb("counts_with_loops", [P, TT, TP], F32, scope)
            deg_row = sb("deg_row", [P, TP], F32, scope)
            deg_col = sb("deg_col", [P, TT], F32, scope)
            s = v(lambda: nc.vector.tensor_copy(loops[:, :, :], count[:, :, :]))
            dve.wait(s)
            for t in range(TT):
                s = v(lambda: nc.vector.tensor_tensor(loops[:, t, tok(t)], loops[:, t, tok(t)], ident[:, :], ALU.add))
            s = split(at(adj, slice(None), slice(None), slice(None)), loops[:, :, :], s)
            for _ in range(4):
                h_ready = next(first)
            pe.wait(s, ones_ready)
            for c0, n in ((0, 320), (320, 320)):
                i, bank, free = banks.take()
                pe.wait(free)
                got = product_exact_a(bank[:, 0:n], [(ones[:, :], at(adj, slice(None), k, slice(c0, c0 + n))) for k in range(TT)])
                s = a(lambda: nc.scalar.activation(deg_row[:, c0:c0 + n], bank[:, 0:n], ACT.Sqrt), got)
                banks.release(i, s)
            row_sqrt = s
            for t in range(TT):
                i, bank, free = banks.take()
                pe.wait(free)
                for k in range(TT):
                    nc.tensor.matmul(bank[:, 0:2], adj[0][:, k, tok(t)], ones[:, 0:2], start=(k == 0), stop=False)
                    end = nc.tensor.matmul(bank[:, 0:2], adj[1][:, k, tok(t)], ones[:, 0:2], start=False, stop=(k == TT - 1))
                s = a(lambda: nc.scalar.activation(deg_col[:, t:t + 1], bank[:, 0:1], ACT.Sqrt), pe.done(end))
                banks.release(i, s)
            row_done = v(lambda: nc.vector.reciprocal(deg_row[:, :], deg_row[:, :]), row_sqrt)
            s = v(lambda: nc.vector.reciprocal(deg_col[:, :], deg_col[:, :]), s)
            dve.wait(s, row_done)
            for t in range(TT):
                s = v(lambda: nc.vector.scalar_tensor_tensor(loops[:, t, :], loops[:, t, :], deg_col[:, t:t + 1],
                                                             deg_row[:, :], ALU.mult, ALU.mult))
                adj_ready = split(at(adj, slice(None), t, slice(None)), loops[:, t, :], s, pe.last() if t == 0 else None)
                h_ready = next(first, h_ready)
            for h_ready in first:
                pass
            add_bias(("gnn0_b2", "mix0_b"))

            pe.wait(h_ready, adj_ready)
            hT_start = pe.last()
            tmp_free = [None, None]
            n_tmp = 0
            act.wait(b1_ready)
            for m in range(KD):
                for c0, n in TOKEN_SPANS:
                    b, bank, free = banks.take()
                    pe.wait(free)
                    got = product(bank[:, 0:n], [(at(h, slice(None), k, slice(m * P, (m + 1) * P)), at(adj, slice(None), k, slice(c0, c0 + n)))
                                                 for k in range(TT)])
                    tmp = z_tmp[:, n_tmp % 2, 0:n]
                    s = a(lambda: nc.scalar.activation(tmp, bank[:, 0:n], ACT.Relu, bias=bcol[:, m:m + 1]), got, tmp_free[n_tmp % 2])
                    banks.release(b, s)
                    s = split(at(xT, slice(None), m, slice(c0, c0 + n)), tmp, s, hT_start)
                    tmp_free[n_tmp % 2] = s
                    n_tmp += 1
            act.wait(pe.last())
            dve.wait(pe.last())
            for s in node_product("gnn0_w2", xT, (s,)):
                pass
            for c in range(2):
                add_tokens(lambda k, t: at(adj, slice(None), k, tok(t)), TT,
                           at(h, slice(None), slice(None), slice(c * HALF, (c + 1) * HALF)), HALF, c * HALF, (s,))
            phase_end()
        gcn.close()

        iota8 = sb("expert_number", [P, TT, E])
        with ExitStack() as scope:
            iota8_i = sb("expert_number_int", [P, TT, E], I32, scope)
            s = g(lambda: nc.gpsimd.iota(iota8_i[:, :, :], [[0, TT], [1, E]], base=0, channel_multiplier=0))
            iota8_ready = g(lambda: nc.gpsimd.tensor_copy(iota8[:, :, :], iota8_i[:, :, :]), s)
            phase_end()
        over_e = lambda ap: ap.unsqueeze(2).broadcast_to([P, TT, E])

        def router_gate(name, scope):
            gate = sb(name + "_gate", [P, KD, E], F32, scope)
            gp = (sb(name + "_gate_hi", [P, KD, E], F32R, scope), sb(name + "_gate_lo", [P, KD, E], F32R, scope))
            s = split(at(gp, slice(None), slice(None), slice(None)), gate[:, :, :], load(name, gate[:, :, :], ins[name]))
            return gp, s

        def router_logits(weight, logits):
            gp, gate_ready = weight
            pe.wait(gate_ready, *xT_ready)
            for t in range(TT):
                b, bank, free = banks.take()
                pe.wait(free)
                got = product(bank[:, 0:E], [(at(xT, slice(None), k, tok(t)), at(gp, slice(None), k, slice(None))) for k in range(KD)])
                s = a(lambda: nc.scalar.activation(logits[:, t, :], bank[:, 0:E], ACT.Copy), got)
                banks.release(b, s)
            return s

        def top_two(name, p, scope, after):
            best = sb(name + "_best", [P, 2, TT], F32, scope)
            number = sb(name + "_number", [P, TT], F32, scope)
            hot = sb(name + "_one_hot", [P, 2, TT, E], F32, scope)
            work = sb(name + "_work", [P, TT, E], F32, scope)
            rest = sb(name + "_rest", [P, TT, E], F32, scope)
            s = v(lambda: nc.vector.tensor_copy(rest[:, :, :], p), after, iota8_ready)
            for k in range(2):
                s = v(lambda: nc.vector.tensor_reduce(best[:, k, :], rest[:, :, :], AX_X, ALU.max), s)
                s = v(lambda: nc.vector.tensor_tensor(work[:, :, :], rest[:, :, :], over_e(best[:, k, :]), ALU.is_equal), s)
                s = v(lambda: nc.vector.scalar_tensor_tensor(work[:, :, :], work[:, :, :], -float(E), iota8[:, :, :], ALU.mult, ALU.add), s)
                s = v(lambda: nc.vector.tensor_reduce(number[:, :], work[:, :, :], AX_X, ALU.min), s)
                s = v(lambda: nc.vector.tensor_scalar(number[:, :], number[:, :], float(E), None, ALU.add), s)
                s = v(lambda: nc.vector.tensor_tensor(hot[:, k, :, :], iota8[:, :, :], over_e(number[:, :]), ALU.is_equal), s)
                s = v(lambda: nc.vector.scalar_tensor_tensor(rest[:, :, :], hot[:, k, :, :], NEG, rest[:, :, :], ALU.mult, ALU.add), s)
            return best, hot, s

        def gate_sums(name, weights, hot, gates, after):
            dve.wait(after)
            for k in range(2):
                s = v(lambda: nc.vector.tensor_tensor(gates[:, k, :, :], hot[:, k, :, :], over_e(weights[:, k, :]), ALU.mult))
            return v(lambda: nc.vector.tensor_tensor(gates[:, 0, :, :], gates[:, 0, :, :], gates[:, 1, :, :], ALU.add), s)

        def turn_gates(name, gates, scope, after):
            gT = (sb(name + "_gatesT_hi", [E, TP], F32R, scope), sb(name + "_gatesT_lo", [E, TP], F32R, scope))
            pe.wait(after)
            for t in range(TT):
                b, bank, free = banks.take()
                pe.wait(free)
                moved = pe.done(nc.tensor.transpose(bank[0:E, 0:P], gates[:, 0, t, :], ident[:, :]))
                s = split(at(gT, slice(None), tok(t)), bank[0:E, 0:P], moved)
                banks.release(b, s)
            return gT, s

        with ExitStack() as scope:
            xn = sb("xn1", [P, TT, D], F32, scope)
            xT_ready = transpose_in(xn, layer_norm(xn, dve.last()))
            phase_end()
        with ExitStack() as scope:
            p = sb("ffn0_p", [P, TT, E], F32, scope)
            m = sb("ffn0_m", [P, 2, TT], F32, scope)
            s = router_logits(router_gate("ffn0_gate", scope), p)
            s = v(lambda: nc.vector.tensor_reduce(m[:, 0, :], p[:, :, :], AX_X, ALU.max), s)
            s = v(lambda: nc.vector.tensor_tensor(p[:, :, :], p[:, :, :], over_e(m[:, 0, :]), ALU.subtract), s)
            s = a(lambda: nc.scalar.activation(p[:, :, :], p[:, :, :], ACT.Exp), s)
            s = v(lambda: nc.vector.tensor_reduce(m[:, 1, :], p[:, :, :], AX_X, ALU.add), s)
            s = v(lambda: nc.vector.reciprocal(m[:, 1, :], m[:, 1, :]), s)
            s = v(lambda: nc.vector.tensor_tensor(p[:, :, :], p[:, :, :], over_e(m[:, 1, :]), ALU.mult), s)
            best, hot, s = top_two("ffn0", p[:, :, :], scope, s)
            s = v(lambda: nc.vector.tensor_tensor(m[:, 0, :], best[:, 0, :], best[:, 1, :], ALU.add), s)
            s = v(lambda: nc.vector.tensor_scalar(m[:, 0, :], m[:, 0, :], 1e-9, None, ALU.add), s)
            s = v(lambda: nc.vector.reciprocal(m[:, 0, :], m[:, 0, :]), s)
            for k in range(2):
                s = v(lambda: nc.vector.tensor_tensor(best[:, k, :], best[:, k, :], m[:, 0, :], ALU.mult), s)
            gates = sb("ffn0_gates", [P, 2, TT, E], F32, scope)
            gT, gT_ready = turn_gates("ffn0", gates, scope, gate_sums("ffn0", best, hot, gates, s))
            sel_f = sb("expert_rows_f", [E, KH0, P], F32, scope)
            sel = sb("expert_rows_r", [E, KH0, P], F32R, scope)
            s = g(lambda: nc.gpsimd.memset(sel_f[:, :, :], 1.0))
            s = g(lambda: nc.gpsimd.affine_select(out=sel_f[:, :, :], in_=sel_f[:, :, :], compare_op=ALU.is_ge, fill=0.0,
                                                  base=0, pattern=[[P, KH0], [1, P]], channel_multiplier=-H0), s)
            s = g(lambda: nc.gpsimd.affine_select(out=sel_f[:, :, :], in_=sel_f[:, :, :], compare_op=ALU.is_ge, fill=0.0,
                                                  base=H0 - 1, pattern=[[-P, KH0], [-1, P]], channel_multiplier=H0), s)
            sel_ready = a(lambda: nc.scalar.activation(sel[:, :, :], sel_f[:, :, :], ACT.Copy), s)
            b1 = sb("ffn0_b1", [P, KH0], F32, scope)
            act.wait(load("ffn0_b1", b1[:, :], ins["ffn0_b1"]))
            b2 = sb("ffn0_b2", [E, D], F32, scope)
            b2p = (sb("ffn0_b2_hi", [E, D], F32R, scope), sb("ffn0_b2_lo", [E, D], F32R, scope))
            b2_ready = split(at(b2p, slice(None), slice(None)), b2[:, :], load("ffn0_b2", b2[:, :], ins["ffn0_b2"]))
            HALF_K = KH0 // 2
            hT = (sb("ffn0_hT_hi", [P, HALF_K, TP], F32R, scope), sb("ffn0_hT_lo", [P, HALF_K, TP], F32R, scope))
            tmp = sb("ffn0_tmp", [P, 2, 320], F32, scope)
            tmp_free, n_tmp = [None, None], 0
            s = v(lambda: nc.vector.memset(tmp[:, 0, :], 0.0))
            for k in range(HALF_K):
                s2 = split(at(hT, slice(None), k, slice(T + 1, TP)), tmp[:, 0, 0:TP - T - 1], s)
            tmp_free[0] = s2
            pe.wait(gT_ready, sel_ready)
            hT_read = None
            for kh in range(2):
                for c in range(2):
                    w, i, ready = take_weight("ffn0_w1", 2 * kh + c)
                    for mm in range(3):
                        hid = 6 * kh + 3 * c + mm
                        for c0, n in TOKEN_SPANS:
                            b, bank, free = banks.take()
                            pe.wait(free, ready)
                            got = product(bank[:, 0:n], [(at(w, slice(None), k, slice(mm * P, (mm + 1) * P)), at(xT, slice(None), k, slice(c0, c0 + n)))
                                                         for k in range(KD)])
                            bg, bankg, free = banks.take()
                            pe.wait(free)
                            gate_got = product_exact_a(bankg[:, 0:n], [(sel[:, hid, :], at(gT, slice(None), slice(c0, c0 + n)))])
                            part = tmp[:, n_tmp % 2, 0:n]
                            s = a(lambda: nc.scalar.activation(part, bank[:, 0:n], ACT.Gelu, bias=b1[:, hid:hid + 1]), got, tmp_free[n_tmp % 2])
                            banks.release(b, s)
                            s = v(lambda: nc.vector.tensor_tensor(part, part, bankg[:, 0:n], ALU.mult), s, gate_got)
                            banks.release(bg, s)
                            hT_ready = split(at(hT, slice(None), 3 * c + mm, slice(c0, c0 + n)), part, s, hT_read)
                            tmp_free[n_tmp % 2] = hT_ready
                            n_tmp += 1
                    drop_weight(i)
                for c in range(2):
                    w, i, ready = take_weight("ffn0_w2", 2 * kh + c)
                    pe.wait(ready, hT_ready, b2_ready)
                    cols = slice(c * HALF, (c + 1) * HALF)
                    for t in range(TT):
                        b, bank, free = banks.take()
                        pe.wait(free)
                        terms = [(at(hT, slice(None), k, tok(t)), at(w, slice(None), k, slice(None))) for k in range(HALF_K)]
                        if kh == 0:
                            terms.append((at(gT, slice(None), tok(t)), at(b2p, slice(None), cols)))
                        got = product(bank[:, 0:HALF], terms)
                        s = v(lambda: nc.vector.tensor_tensor(x[:, t, cols], x[:, t, cols], bank[:, 0:HALF], ALU.add), got)
                        banks.release(b, s)
                    drop_weight(i)
                hT_read = pe.last()
            phase_end()

        with ExitStack() as scope:
            xn = sb("xn2", [P, TT, D], F32, scope)
            xT_ready = transpose_in(xn, layer_norm(xn, dve.last()))
            phase_end()
        add_bias(("mix1_b", "gat_b2"))

        def kv1(which, kv, rows, after=None):
            if which is None:
                return [bias0[:, n * HALF:(n + 1) * HALF] for n in range(2)]
            if which == 1:
                return after
            dve.wait(dve.last())
            used = [after, after]
            for t in range(TT):
                k, e = kv[:, 0, t, :], rows[t % 2]
                s = v(lambda: nc.vector.tensor_scalar(e, k, 0.0, None, ALU.min), used[t % 2])
                s = a(lambda: nc.scalar.activation(e, e, ACT.Exp), s)
                used[t % 2] = v(lambda: nc.vector.scalar_tensor_tensor(k, k, 0.0, e, ALU.max, ALU.add), s)
            return used[(TT - 1) % 2]

        def q1(q, tmp, bank, got, b, free):
            s = v(lambda: nc.vector.tensor_scalar(tmp, bank, 0.0, None, ALU.min), got, free)
            s = a(lambda: nc.scalar.activation(tmp, tmp, ACT.Exp), s)
            s = v(lambda: nc.vector.scalar_tensor_tensor(q, bank, 0.0, tmp, ALU.max, ALU.add), s)
            banks.release(b, s)
            return s

        linear_attention("mix1", kv1, q1, True)

        gat = ExitStack()
        x_kept = (sem("x_kept"), 16)
        act.wait(dve.last())
        act.engine.dma_start(slots_dram.rearrange("(t p) d -> p t d", p=P), x[:, :, :]).then_inc(x_kept[0], 16)
        stores.append(x_kept)
        sel4_f = bias0[0:2, 0:2 * P].rearrange("p (a n) -> p a n", a=2)
        sel4 = sb("row_selector", [2, 2, P], F32R, gat)
        s = g(lambda: nc.gpsimd.memset(sel4_f[:, :, :], 0.0), dve.last())
        s = g(lambda: nc.gpsimd.affine_select(out=sel4_f[:, :, :], in_=sel4_f[:, :, :], compare_op=ALU.not_equal, fill=1.0,
                                              base=0, pattern=[[-1, 2], [0, P]], channel_multiplier=1), s)
        sel4_ready = a(lambda: nc.scalar.activation(sel4[:, :, :], sel4_f[:, :, :], ACT.Copy), s)
        edges_in = count
        no_edge = sb("no_edge", [P, TT, TP], mybir.dt.bfloat16, gat)
        scores = sb("gat_scores", [P, 2, TT, 4], F32, gat)
        peak_src = sb("gat_peak_src", [P, 2, 2, TT], F32, gat)
        minus_peak = sb("gat_minus_peak", [P, 2, 2, TT], F32, gat)
        total = sb("gat_total", [P, 2, 2, TT], F32, gat)
        small = sb("gat_small", [P, 2, TT], F32, gat)
        rowT = (sb("gat_rowT_hi", [2, TP], F32R, gat), sb("gat_rowT_lo", [2, TP], F32R, gat))
        GW = 2 * P
        hg = [(sb(f"gat_h{n}_hi", [P, TT, GW], F32R, gat), sb(f"gat_h{n}_lo", [P, TT, GW], F32R, gat)) for n in range(2)]
        src_row = [sb(f"gat_src_row{n}", [P, 2, TP], F32, gat) for n in range(2)]
        ZS, XS = 5, 2
        edge_w = sb("gat_edge", [P, ZS, TP], F32, gat)
        exT = (sb("gat_exT_hi", [P, XS, TT, P], F32R, gat), sb("gat_exT_lo", [P, XS, TT, P], F32R, gat))
        unread = sb("gat_unread", [P, 2, TP], F32, gat)
        unread_free, n_unread = [None, None], 0
        zT = (sb("gat_zT_hi", [P, 2, 2, P], F32R, gat), sb("gat_zT_lo", [P, 2, 2, P], F32R, gat))
        zt = sb("gat_z", [P, 2, P], F32, gat)
        h2 = x
        hp = tuple(half[:, :, :].rearrange("p k n -> p (k n)").rearrange("p (t d) -> p t d", t=TT) for half in xT)
        b1 = sb("gat_b1", [P, G1], F32, gat)
        act.wait(load("gat_b1", b1[:, :], ins["gat_b1"]))
        z_free, x_free = [None] * ZS, [None] * XS
        units = {"n": 0}

        s = v(lambda: nc.vector.tensor_copy(edge_w[:, :, :], count[:, :, :]))
        pe.wait(s)
        act.wait(s)
        for t in range(TT):
            for k0, kn in ((0, 3), (3, 2)):
                b, bank, free = banks.take()
                pe.wait(free)
                for k in range(kn):
                    end = nc.tensor.transpose(bank[:, k * P:(k + 1) * P], edge_w[:, k0 + k, tok(t)], ident[:, :])
                cols = slice(k0 * P, (k0 + kn) * P)
                s = a(lambda: nc.scalar.activation(edges_in[:, t, cols], bank[:, 0:kn * P], ACT.Copy), pe.done(end))
                edges_ready_ = s = v(lambda: nc.vector.tensor_scalar(no_edge[:, t, cols], bank[:, 0:kn * P], 0.0, NEG, ALU.is_equal, ALU.mult), s)
                banks.release(b, s)
        z_free = [pe.last()] * ZS
        dve.wait(edges_ready_)

        def source_rows(grp, heads, s, row_free):
            par = grp % 2
            pe.wait(s, sel4_ready)
            for k0, kn in ((0, 3), (3, 2)):
                b, bank, free = banks.take()
                pe.wait(free)
                for k in range(kn):
                    end = nc.tensor.transpose(bank[0:heads, k * P:(k + 1) * P], scores[:, par, k0 + k, 0:heads], ident[:, :])
                s = split(at(rowT, slice(0, heads), slice(k0 * P, (k0 + kn) * P)), bank[0:heads, 0:kn * P], pe.done(end))
                banks.release(b, s)
            yield
            pe.wait(s)
            for h in range(heads):
                for c0 in (0, 320):
                    b, bank, free = banks.take()
                    pe.wait(free)
                    got = product_exact_a(bank[:, 0:320], [(sel4[0:heads, h, :], at(rowT, slice(0, heads), slice(c0, c0 + 320)))])
                    s = a(lambda: nc.scalar.activation(src_row[par][:, h, c0:c0 + 320], bank[:, 0:320], ACT.Copy), got, row_free)
                    banks.release(b, s)
            group[grp]["rows"] = s

        def sum_or_max(in0, in1, op0, op1, start, result, *after):
            nonlocal n_unread
            r = n_unread % 2
            n_unread += 1
            n = in0.shape[1]
            unread_free[r] = v(lambda: nc.vector.tensor_tensor_reduce(out=unread[:, r, 0:n], in0=in0, in1=in1, scale=1.0, scalar=start,
                                                                      op0=op0, op1=op1, accum_out=result), unread_free[r], *after)
            return unread_free[r]

        def segment_peaks(grp, heads):
            par = grp % 2
            for h in range(heads):
                for t in range(TT):
                    s = sum_or_max(no_edge[:, t, :], src_row[par][:, h, :], ALU.add, ALU.max, 2.0 * NEG, peak_src[:, par, h, t:t + 1],
                                   group[grp]["rows"])
                if h + 1 < heads:
                    yield
            a_dst = scores[:, par, :, heads:2 * heads].rearrange("p t h -> p h t")
            o = minus_peak[:, par, 0:heads, :]
            w_ = small[:, 0:heads, :]
            s = v(lambda: nc.vector.tensor_tensor(o, peak_src[:, par, 0:heads, :], a_dst, ALU.add), s)
            s = v(lambda: nc.vector.tensor_scalar(w_, o, SLOPE, None, ALU.mult), s)
            s = v(lambda: nc.vector.tensor_tensor(o, o, w_, ALU.max), s)
            group[grp]["ready"] = v(lambda: nc.vector.tensor_scalar(o, o, -1.0, None, ALU.mult), s)

        def exponentials(grp, h, t, heads, u, scale_rows, aggregate):
            par = grp % 2
            e = edge_w[:, u % ZS, :]
            s = v(lambda: nc.vector.tensor_scalar(e, src_row[par][:, h, :], peak_src[:, par, h, t:t + 1],
                                                  scores[:, par, t, heads + h:heads + h + 1], ALU.min, ALU.add),
                  z_free[u % ZS], group[grp]["ready"])
            group[grp]["row_read"] = s
            s = v(lambda: nc.vector.scalar_tensor_tensor(e, e, SLOPE, e, ALU.mult, ALU.max), s)
            yield
            s = a(lambda: nc.scalar.activation(e, e, ACT.Exp, bias=minus_peak[:, par, h, t:t + 1]), s)
            yield
            tot = total[:, par, h, t:t + 1]
            s = v(lambda: nc.vector.scalar_tensor_tensor(e, e, 1.0, edges_in[:, t, :], ALU.mult, ALU.mult, accum_out=tot), s)
            s = v(lambda: nc.vector.tensor_scalar(tot, tot, 1e-16, None, ALU.add), s)
            s = v(lambda: nc.vector.reciprocal(tot, tot), s)
            if scale_rows:
                yield
                s = g(lambda: nc.gpsimd.tensor_scalar(e, e, tot, None, ALU.mult), s)
            yield
            x_ = u % XS
            pe.wait(s)
            turned_ = []
            for k0, kn in ((0, 3), (3, 2)):
                b, bank, free = banks.take()
                pe.wait(free)
                for k in range(kn):
                    end = nc.tensor.transpose(bank[:, k * P:(k + 1) * P], e[:, tok(k0 + k)], ident[:, :])
                turned_.append((k0, kn, b, bank, pe.done(end)))
            z_free[u % ZS] = pe.last()
            yield
            for k0, kn, b, bank, moved in turned_:
                s = split(at(exT, slice(None), x_, slice(k0, k0 + kn), slice(None)),
                          bank[:, 0:kn * P].rearrange("p (k n) -> p k n", n=P), moved, x_free[x_])
                banks.release(b, s)
            yield
            steps = aggregate(grp, h, t, lambda k: at(exT, slice(None), x_, k, slice(None)), s)
            x_free[x_] = next(steps)
            yield
            for _ in steps:
                yield

        live = []

        def advance():
            live[:] = [steps for steps in live if next(steps, "end") != "end"]

        def admit(*unit):
            u = units["n"]
            units["n"] += 1
            grp, h, t, heads, scale_rows, aggregate = unit
            live.append(exponentials(grp, h, t, heads, u, scale_rows, aggregate))
            advance()

        att = bias0[:, 0:2 * GW].rearrange("p (a n) -> p a n", a=2)
        group = [{"aggregated": 0} for _ in range(5)]

        def prepare_group(grp):
            par = grp % 2
            cols = slice(grp * GW, (grp + 1) * GW)
            att_free = group[grp - 1]["scored"] if grp else sel4_ready
            att_ready = [load(f"{name}_{grp}", att[:, n, :], ins[name][cols].rearrange("(a n) -> a n", a=1).broadcast_to([P, GW]), att_free)
                         for n, name in enumerate(("gat_as1", "gat_ad1"))]
            yield
            w, i, ready = take_weight("gat_w1", grp)
            h_free = row_free = None
            if grp > 1:
                assert group[grp - 2]["aggregated"] == 2 * TT
                h_free, row_free = group[grp - 2]["h_read"], group[grp - 2]["row_read"]
            pe.wait(ready, *xT_ready)
            for t in range(TT):
                b, bank, free = banks.take()
                pe.wait(free)
                got = product(bank[:, 0:GW], [(at(xT, slice(None), k, tok(t)), at(w, slice(None), k, slice(None))) for k in range(KD)])
                group[grp]["h"] = split((hg[par][0][:, t, :], hg[par][1][:, t, :]), bank[:, 0:GW], got, h_free)
                for n in range(2):
                    for h in range(2):
                        s = sum_or_max(bank[:, h * P:(h + 1) * P], att[:, n, h * P:(h + 1) * P], ALU.mult, ALU.add, 0.0,
                                       scores[:, par, t, 2 * n + h:2 * n + h + 1], got, *att_ready)
                banks.release(b, s)
                if t < TT - 1:
                    yield
            group[grp]["scored"] = s
            xT_read = pe.last()
            drop_weight(i)
            yield
            yield from source_rows(grp, 2, s, row_free)
            yield
            yield from segment_peaks(grp, 2)
            group[grp]["xT_read"] = xT_read

        zt_free, zT_free, n_z = [None, None], [None, None], 0
        h2_done, w2 = {}, {}
        z_ready = {}

        def aggregate(grp, h, t, ex, ready):
            nonlocal n_z
            b, bank, free = banks.take()
            pe.wait(free, ready, group[grp]["h"])
            mine = hg[grp % 2]
            got = product(bank[:, 0:P], [((mine[0][:, k, h * P:(h + 1) * P], mine[1][:, k, h * P:(h + 1) * P]), ex(k)) for k in range(TT)])
            group[grp]["aggregated"] += 1
            group[grp]["h_read"] = got
            yield got
            slot, z_slot = n_z % 2, (grp * TT + t) % 2
            n_z += 1
            z = zt[:, slot, :]
            s = a(lambda: nc.scalar.activation(z, bank[:, 0:P], ACT.Relu, bias=b1[:, 2 * grp + h:2 * grp + h + 1]), got, zt_free[slot])
            banks.release(b, s)
            zt_free[slot] = z_ready[h] = split(at(zT, slice(None), z_slot, h, slice(None)), z, s, zT_free[z_slot])
            if h == 0:
                return
            yield
            if t == 0:
                w2[grp] = take_weight("gat_w2", grp)
            w, i, w_ready = w2[grp]
            pe.wait(w_ready, z_ready[0], z_ready[1])
            for c in range(2):
                b, bank, free = banks.take()
                pe.wait(free)
                got = product(bank[:, 0:HALF], [(at(zT, slice(None), z_slot, k, slice(None)), at(w, slice(None), k, slice(c * HALF, (c + 1) * HALF)))
                                                for k in range(2)])
                o = h2[:, t, c * HALF:(c + 1) * HALF]
                if grp == 0:
                    s = v(lambda: nc.vector.tensor_copy(o, bank[:, 0:HALF]), got, x_kept)
                else:
                    s = v(lambda: nc.vector.tensor_tensor(o, o, bank[:, 0:HALF], ALU.add), got, h2_done[t, c])
                h2_done[t, c] = s
                banks.release(b, s)
            zT_free[z_slot] = pe.last()
            if t == TT - 1:
                drop_weight(i)
            if grp == 2 and t == TT - 1:
                att2["rows"] = (bias0[:, :], src_row[0][:, :, :].rearrange("p h n -> p (h n)")[:, 0:D])
                att2["ready"] = [row_load(name, att2["rows"][n], ins[name], D, group[3]["scored"], group[2]["row_read"])
                                 for n, name in enumerate(("gat_as2", "gat_ad2"))]
            if grp == 3:
                yield
                for n in range(2):
                    for c in range(2):
                        c_ = slice(c * HALF, (c + 1) * HALF)
                        s = sum_or_max(h2[:, t, c_], att2["rows"][n][:, c_], ALU.mult, ALU.add, 0.0, half_scores[:, t, n, c:c + 1],
                                       h2_done[t, 0], h2_done[t, 1], *att2["ready"])
                att2["s"] = s
                att2["h"] = split(at(hp, slice(None), t, slice(None)), h2[:, t, :], h2_done[t, 0], h2_done[t, 1], group[3]["xT_read"])

        att2 = {}
        half_scores = sb("gat2_half_scores", [P, TT, 2, 2], F32, gat)
        for _ in prepare_group(0):
            pass
        for grp in range(4):
            coming = prepare_group(grp + 1) if grp < 3 else iter(())
            for n in range(2 * TT):
                admit(grp, n % 2, n // 2, 2, True, aggregate)
                if n >= PREPARE_FROM:
                    next(coming, None)
            for _ in coming:
                advance()
        while live:
            advance()
        s = v(lambda: nc.vector.tensor_tensor(scores[:, 0, :, 0:2], half_scores[:, :, :, 0], half_scores[:, :, :, 1], ALU.add), att2["s"],
              group[2]["row_read"])
        x_back = load("x_back", x[:, :, :], slots_dram.rearrange("(t p) d -> p t d", p=P), s, att2["h"], x_kept)
        for _ in source_rows(4, 1, s, att2["s"]):
            pass
        for _ in segment_peaks(4, 1):
            pass
        pe.wait(att2["h"])

        def aggregate2(grp, h, t, ex, ready):
            kept = []
            for c in range(2):
                b, bank, free = banks.take()
                pe.wait(free, ready)
                got = product(bank[:, 0:HALF], [(ex(k), at(hp, slice(None), k, slice(c * HALF, (c + 1) * HALF))) for k in range(TT)])
                kept.append((c, b, bank, got))
            yield got
            for c, b, bank, got in kept:
                o = x[:, t, c * HALF:(c + 1) * HALF]
                s = v(lambda: nc.vector.scalar_tensor_tensor(o, bank[:, 0:HALF], total[:, 0, 0, t:t + 1], o, ALU.mult, ALU.add), got, x_back)
                banks.release(b, s)

        for t in range(TT):
            admit(4, 0, t, 1, False, aggregate2)
        while live:
            advance()
        phase_end()
        gat.close()

        moe = ExitStack()
        slot_row = sb("slot_row", [P, 2, TT], U32, moe)
        slot_token = sb("slot_token", [P, E * MAIN], U32, moe)
        extra_token = sb("extra_token", [P, E * EXTRA], U32, moe)
        overflow = sb("overflow", [P, E * EXTRA], I32, moe)
        any_overflow = sb("any_overflow", [P, 1], I32, moe)
        weights2 = sb("gate_weights", [P, 2, TT], F32, moe)
        token_rows = sb("token_rows", [P, TT, D], F32, moe)
        xg = token_rows[:, 0:2 * MAIN, :].rearrange("p (r n) d -> p r n d", r=2)
        hs = (sb("hidden_hi", [P, 2, 3, TP], F32R, moe), sb("hidden_lo", [P, 2, 3, TP], F32R, moe))
        hst = sb("hidden_tmp", [P, 2, 320], F32, moe)
        hT = tuple(part[:, :, :, 0:CAP] for part in hs)
        ht = hst[:, :, 0:CAP]
        xe = tuple(part[:, :, 0:2 * CAP].rearrange("p k (r n) -> p r k n", r=2) for part in xT)
        b1e = sb("ffn1_b1", [P, E, H1 // P], F32, moe)
        act.wait(load("ffn1_b1", b1e[:, :, :], ins["ffn1_b1"]))
        gather_sem = [sem(f"gathered{n}") for n in range(2)]
        gathers = [0, 0]
        banks = Banks(psum[0:7])
        slot_bank = psum[7]
        made = {}
        state = {"xg_free": [None, None], "xe_read": [None, None]}
        arrived = {}

        def gather(r, e):
            pool.wait(made["stored"], made["tokens"], xT_ready[-1], state["xg_free"][r])
            for n, st in enumerate(range(MAIN)):
                j = e * MAIN + st
                nc.gpsimd.indirect_dma_start(xg[:, r, n, :], None, slots_dram[:, :],
                                             bass.IndirectOffsetOnAxis(ap=slot_token[:, j:j + 1], axis=0)).then_inc(gather_sem[r], 16)
                gathers[r] += 16
            return (gather_sem[r], gathers[r])

        def prepare(e):
            if e < E:
                arrived[e] = gather(e % 2, e)

        def turn(r, arrived):
            pe.wait(arrived)
            for n, st in enumerate(range(MAIN)):
                for c in range(2):
                    i, bank, free = banks.take()
                    pe.wait(free)
                    for k in range(3):
                        end = nc.tensor.transpose(bank[:, k * P:(k + 1) * P], xg[:, r, n, (3 * c + k) * P:(3 * c + k + 1) * P], ident[:, :])
                    moved = pe.done(end)
                    s = split(at(xe, slice(None), r, slice(3 * c, 3 * c + 3), slice(n * P, (n + 1) * P)),
                              bank[:, 0:3 * P].rearrange("p (k n) -> p k n", k=3), moved, state["xe_read"][r])
                    banks.release(i, s)
            state["xg_free"][r] = moved
            return s

        with ExitStack() as scope:
            xn = token_rows
            xn_ready = layer_norm(xn, dve.last())
            xT_ready = transpose_in(xn, xn_ready)
            xn_stored = (sem("xn_stored"), 16)
            act.wait(xn_ready[-1])
            act.engine.dma_start(slots_dram.rearrange("(t p) d -> p t d", p=P), xn[:, :, :]).then_inc(xn_stored[0], 16)
            stores.append(xn_stored)
            made["stored"] = xn_stored
            logits = sb("ffn1_logits", [P, TT, E], F32, scope)
            b2p = (sb("ffn1_b2_hi", [E, D], F32R, scope), sb("ffn1_b2_lo", [E, D], F32R, scope))
            chosen_f = sb("chosen_f", [P, TT, E], F32, scope)
            chosen = sb("chosen", [P, TT, E], F32R, scope)
            before_f = sb("before_f", [P, P], F32, scope)
            before = sb("before", [P, P], F32R, scope)
            rank = sb("rank", [P, TT, E], F32, scope)
            total = sb("tokens_of_expert", [P, E], F32, scope)
            most = sb("most_tokens", [P, 1], F32, scope)
            row_e = sb("row_of_expert", [P, TT, E], F32, scope)
            picked = sb("picked_row", [P, 2, TT, E], F32, scope)
            row_f = sb("picked_row_f", [P, 2, TT], F32, scope)
            shift = sb("overflow_shift", [P, TT, E], F32, scope)
            over = sb("beyond_first_pass", [P, TT, E], F32, scope)
            here = sb("rank_or_none", [P, TT, E], F32, scope)
            number_i = sb("token_number_int", [P, TT], I32, scope)
            number = sb("token_number", [P, TT], F16, scope)
            gates = sb("ffn1_gates", [P, 2, TT, E], F32, scope)
            hot_slot = (count[:, :, :].bitcast(F16), sb("one_hot_slot", [P, TT, TP], F16, scope)[:, :, :])

            def routing():
                gate = router_gate("ffn1_gate", scope)
                g(lambda: nc.gpsimd.affine_select(out=before_f[:, :], in_=ones_f[:, :], compare_op=ALU.is_ge, fill=0.0,
                                                  base=-1, pattern=[[1, P]], channel_multiplier=-1))
                before_ready = a(lambda: nc.scalar.activation(before[:, :], before_f[:, :], ACT.Copy), pool.last())
                s = g(lambda: nc.gpsimd.iota(number_i[:, :], [[P, TT]], base=0, channel_multiplier=1))
                number_ready = g(lambda: nc.gpsimd.tensor_copy(number[:, :], number_i[:, :]), s)
                yield
                s = router_logits(gate, logits)
                yield
                best, hot, s = top_two("ffn1", logits[:, :, :], scope, s)
                s = v(lambda: nc.vector.tensor_tensor(weights2[:, 1, :], best[:, 1, :], best[:, 0, :], ALU.subtract), s)
                s = a(lambda: nc.scalar.activation(weights2[:, 1, :], weights2[:, 1, :], ACT.Exp), s)
                s = v(lambda: nc.vector.tensor_scalar(weights2[:, 0, :], weights2[:, 1, :], 1.0, None, ALU.add), s)
                s = v(lambda: nc.vector.reciprocal(weights2[:, 0, :], weights2[:, 0, :]), s)
                s = v(lambda: nc.vector.tensor_tensor(weights2[:, 1, :], weights2[:, 1, :], weights2[:, 0, :], ALU.mult), s)
                s = gates_ready = gate_sums("ffn1", weights2, hot, gates, s)
                s = v(lambda: nc.vector.tensor_tensor(chosen_f[:, :, :], hot[:, 0, :, :], hot[:, 1, :, :], ALU.add))
                s = g(lambda: nc.gpsimd.affine_select(out=chosen_f[:, TT - 1, :], in_=chosen_f[:, TT - 1, :], compare_op=ALU.is_ge,
                                                      fill=0.0, base=LAST - 1, pattern=[[0, E]], channel_multiplier=-1), s)
                chosen_ready = a(lambda: nc.scalar.activation(chosen[:, :, :], chosen_f[:, :, :], ACT.Copy), s)
                yield
                yield
                yield
                yield
                pe.wait(before_ready, chosen_ready)
                for t in range(TT):
                    b, bank, free = banks.take()
                    pe.wait(free)
                    for k in range(t):
                        nc.tensor.matmul(bank[:, 0:E], ones[:, :], chosen[:, k, :], start=(k == 0), stop=False)
                    got = pe.done(nc.tensor.matmul(bank[:, 0:E], before[:, :], chosen[:, t, :], start=(t == 0), stop=True))
                    rank_ready = v(lambda: nc.vector.tensor_copy(rank[:, t, :], bank[:, 0:E]), got)
                    banks.release(b, rank_ready)
                gT, gT_ready = turn_gates("ffn1", gates, scope, gates_ready)
                yield
                for t in range(TT):
                    dve.wait(made.get(("x", t, 1)))
                s = add_bias(("shared_b2",), 0.1 * 2)
                yield
                b2 = bias0[0:E, :]
                b2_ready = split(at(b2p, slice(None), slice(None)), b2, load("ffn1_b2", b2, ins["ffn1_b2"], dve.last()))
                yield
                yield
                pe.wait(b2_ready, gT_ready)
                for t in range(TT):
                    for c in range(2):
                        cols = slice(c * HALF, (c + 1) * HALF)
                        b, bank, free = banks.take()
                        pe.wait(free)
                        got = product(bank[:, 0:HALF], [(at(gT, slice(None), tok(t)), at(b2p, slice(None), cols))])
                        s = v(lambda: nc.vector.tensor_tensor(x[:, t, cols], x[:, t, cols], bank[:, 0:HALF], ALU.add), got, dve.last())
                        banks.release(b, s)
                        made["x", t, c] = s
                    yield
                b, bank, free = banks.take()
                pe.wait(free)
                for k in range(TT):
                    end = nc.tensor.matmul(bank[:, 0:E], ones[:, :], chosen[:, k, :], start=(k == 0), stop=(k == TT - 1))
                s = v(lambda: nc.vector.tensor_copy(total[:, :], bank[:, 0:E]), pe.done(end))
                banks.release(b, s)
                tiles = overflow[:, :].rearrange("p (e n) -> p e n", n=EXTRA)
                for n in range(EXTRA):
                    v(lambda: nc.vector.tensor_scalar(tiles[:, :, n], total[:, :], float(CAP + n * P), None, ALU.is_gt), s)
                s = v(lambda: nc.vector.tensor_reduce(most[:, :], total[:, :], AX_X, ALU.max), s)
                v(lambda: nc.vector.tensor_scalar(any_overflow[:, :], most[:, :], float(CAP), None, ALU.is_gt), s)
                v(lambda: nc.vector.scalar_tensor_tensor(row_e[:, :, :], iota8[:, :, :], float(CAP), rank[:, :, :], ALU.mult, ALU.add), rank_ready)
                v(lambda: nc.vector.tensor_scalar(shift[:, :, :], iota8[:, :, :], float(EXTRA * P - CAP), float((E - 1) * CAP), ALU.mult, ALU.add))
                s = v(lambda: nc.vector.tensor_scalar(over[:, :, :], rank[:, :, :], float(CAP), None, ALU.is_ge))
                s = v(lambda: nc.vector.tensor_tensor(shift[:, :, :], shift[:, :, :], over[:, :, :], ALU.mult), s)
                s = v(lambda: nc.vector.tensor_tensor(row_e[:, :, :], row_e[:, :, :], shift[:, :, :], ALU.add), s)
                for k in range(2):
                    s = v(lambda: nc.vector.tensor_tensor(picked[:, k, :, :], hot[:, k, :, :], row_e[:, :, :], ALU.mult), s)
                    s = v(lambda: nc.vector.tensor_reduce(row_f[:, k, :], picked[:, k, :, :], AX_X, ALU.add), s)
                rows_done = v(lambda: nc.vector.tensor_copy(slot_row[:, :, :], row_f[:, :, :]), s)
                yield
                s = v(lambda: nc.vector.tensor_scalar(here[:, :, :], rank[:, :, :], 1.0, None, ALU.add), rank_ready)
                s = v(lambda: nc.vector.tensor_tensor(here[:, :, :], here[:, :, :], chosen_f[:, :, :], ALU.mult), s, chosen_ready)
                s = v(lambda: nc.vector.tensor_scalar(here[:, :, :], here[:, :, :], -1.0, None, ALU.add), s)
                hot_free = [None, None]
                dve.wait(s)
                pe.wait(number_ready)
                bank = slot_bank
                made_hot = [None] * E
                for e in range(E + 1):
                    if e < E:
                        dve.wait(hot_free[e % 2])
                        for t in range(TT):
                            made_hot[e] = v(lambda: nc.vector.tensor_scalar(hot_slot[e % 2][:, t, :], iota_h[:, :], here[:, t, e:e + 1], None, ALU.is_equal))
                        yield
                    if e > 0:
                        pe.wait(made_hot[e - 1])
                        for st in range(TT):
                            for t in range(TT):
                                end = nc.tensor.matmul(bank[:, (e - 1) * TT + st:(e - 1) * TT + st + 1], hot_slot[(e - 1) % 2][:, t, tok(st)],
                                                       number[:, t:t + 1], start=(t == 0), stop=(t == TT - 1))
                        hot_free[(e - 1) % 2] = pe.done(end)
                by_tile = bank[:, 0:E * TT].rearrange("p (e n) -> p e n", n=TT)
                tokens_done = v(lambda: nc.vector.tensor_copy(slot_token[:, :].rearrange("p (e n) -> p e n", n=MAIN), by_tile[:, :, 0:MAIN]), hot_free[1])
                v(lambda: nc.vector.tensor_copy(extra_token[:, :].rearrange("p (e n) -> p e n", n=EXTRA), by_tile[:, :, MAIN:TT]))
                made.update(tokens=tokens_done, rows=rows_done)
                yield

            b1s = sb("shared_b1", [P, H1 // P], F32, scope)
            act.wait(load("shared_b1", b1s[:, :], ins["shared_b1"]))
            s = v(lambda: nc.vector.memset(hst[:, 0, :], 0.0))
            for r in range(2):
                s = split(at(hs, slice(None), r, slice(None), slice(T + 1, TP)),
                          hst[:, 0, 0:3 * (TP - T - 1)].rearrange("p (m n) -> p m n", m=3), s)
            tmp_free, n_tmp = [s, None], 0
            h_read, h_ready = [None, None], {}
            route = routing()
            for c in range(NCH + 1):
                if c < NCH:
                    w, i, w_ready = take_weight("ffn1_w1", "shared", c)
                    pe.wait(w_ready, *xT_ready)
                    for m in range(3):
                        for c0, n in TOKEN_SPANS:
                            b, bank, free = banks.take()
                            pe.wait(free)
                            got = product(bank[:, 0:n], [(at(w, slice(None), k, slice(m * P, (m + 1) * P)), at(xT, slice(None), k, slice(c0, c0 + n)))
                                                         for k in range(KD)])
                            part = hst[:, n_tmp % 2, 0:n]
                            col = 3 * c + m
                            s = a(lambda: nc.scalar.activation(part, bank[:, 0:n], ACT.Relu, bias=b1s[:, col:col + 1]), got, tmp_free[n_tmp % 2])
                            banks.release(b, s)
                            s = split(at(hs, slice(None), c % 2, m, slice(c0, c0 + n)), part, s, h_read[c % 2])
                            tmp_free[n_tmp % 2] = s
                            n_tmp += 1
                        next(route, None)
                    h_ready[c] = s
                    drop_weight(i)
                if c == NCH - 1:
                    for _ in route:
                        pass
                    state["xe_read"] = [pe.last(), pe.last()]
                    prepare(0)
                    prepare(1)
                if c == NCH:
                    turned = {0: turn(0, arrived[0])}
                if c > 0:
                    w, i, w_ready = take_weight("ffn1_w2", "shared", c - 1)
                    pe.wait(w_ready, h_ready[c - 1])
                    r = (c - 1) % 2
                    for t in range(TT):
                        for half in range(2):
                            cols = slice(half * HALF, (half + 1) * HALF)
                            b, bank, free = banks.take()
                            pe.wait(free)
                            got = product(bank[:, 0:HALF], [(at(hs, slice(None), r, k, tok(t)), at(w, slice(None), k, cols)) for k in range(3)])
                            s = v(lambda: nc.vector.scalar_tensor_tensor(x[:, t, cols], bank[:, 0:HALF], 0.1 * 2, x[:, t, cols], ALU.mult, ALU.add),
                                  got, made.get(("x", t, half)))
                            made["x", t, half] = s
                            banks.release(b, s)
                        next(route, None)
                    h_read[r] = pe.last()
                    drop_weight(i)

        y_banks = psum[4:8]
        y_free = [banks.free[4], banks.free[5], banks.free[6], made["tokens"]]
        was = banks.free
        banks = Banks(psum[0:4])
        banks.free = was[0:4]
        store_sem = [sem(f"rows_stored{n}") for n in range(2)]
        row_stores = [0, 0]
        state.update(yt_free=[None, None], h_read=h_read, tmp=tmp_free, n=0)
        act.wait(*[q.last() for q in (dve, pool)])
        yt = sb("ffn1_y", [P, 2, 2, D], F32, moe)

        def run_pass(who, source, ready, bias, after_first_chunk):
            nonlocal y_free
            st = list(range(MAIN))
            width = P * len(st)

            def hidden(c):
                w, i, w_ready = take_weight("ffn1_w1", who, c)
                pe.wait(w_ready, *ready)
                for m in range(3):
                    b, bank, free = banks.take()
                    pe.wait(free)
                    got = product(bank[:, 0:width], [(at(w, slice(None), k, slice(m * P, (m + 1) * P)), source(k, width)) for k in range(KD)])
                    n = state["n"]
                    state["n"] += 1
                    part = ht[:, n % 2, 0:width]
                    col = 3 * c + m
                    s = a(lambda: nc.scalar.activation(part, bank[:, 0:width], ACT.Relu, bias=bias(col)), got, state["tmp"][n % 2])
                    banks.release(b, s)
                    s = split(at(hT, slice(None), c % 2, m, slice(0, width)), part, s, state["h_read"][c % 2])
                    state["tmp"][n % 2] = s
                drop_weight(i)
                return s

            def output(c, h_ready):
                w, i, w_ready = take_weight("ffn1_w2", who, c)
                pe.wait(w_ready, h_ready)
                if c == 0:
                    pe.wait(*y_free)
                for n in range(len(st)):
                    for half in range(2):
                        got = product(y_banks[2 * n + half][:, 0:HALF],
                                      [(at(hT, slice(None), c % 2, k, tok(n)), at(w, slice(None), k, slice(half * HALF, (half + 1) * HALF)))
                                       for k in range(3)], first=(c == 0), last=(c == NCH - 1))
                state["h_read"][c % 2] = got
                drop_weight(i)
                return got

            h_ready = {}
            for c in range(NCH + 1):
                if c < NCH:
                    h_ready[c] = hidden(c)
                if c == 1:
                    after_first_chunk()
                if c > 0:
                    y_done = output(c - 1, h_ready[c - 1])
            r = state["n_store"] % 2
            state["n_store"] += 1
            act.wait(y_done, state["yt_free"][r])
            for n, t in enumerate(st):
                for half in range(2):
                    s = a(lambda: nc.scalar.activation(yt[:, r, n, half * HALF:(half + 1) * HALF], y_banks[2 * n + half][:, 0:HALF], ACT.Copy))
            y_free = [s]
            pool.wait(s)
            row0 = who * CAP
            nc.gpsimd.dma_start(result_dram[row0:row0 + width, :].rearrange("(t p) d -> p t d", p=P), yt[:, r, 0:len(st), :]).then_inc(store_sem[r], 16)
            row_stores[r] += 16
            state["yt_free"][r] = (store_sem[r], row_stores[r])

        state["n_store"] = 0
        for who in range(E):
            def between():
                if who + 1 in arrived:
                    turned[who + 1] = turn((who + 1) % 2, arrived[who + 1])
                    prepare(who + 2)
            r = who % 2
            run_pass(who, lambda k, width: at(xe, slice(None), r, k, slice(0, width)), (turned[who],),
                     lambda col: b1e[:, who, col:col + 1], between)
            state["xe_read"][r] = pe.last()
        phase_end()
        stored = [(store_sem[r], row_stores[r]) for r in range(2)]

        spill_sems = [sem("spill_" + name) for name in ("pe", "act", "dve", "gather", "bias", "w0", "w1", "store")]
        numbers = [x_.num for x_ in spill_sems]
        assert numbers == list(range(numbers[0], numbers[0] + len(numbers)))
        (s_pe, s_act, s_dve, s_gather, s_bias, s_w0, s_w1, s_store) = spill_sems
        pool.wait(*stored)
        extra_rows = result_dram[E * CAP:E * TP, :].rearrange("(n p) d -> n p d", p=P)

        def overflow_tile(e, i):
            q_pe, q_act, q_dve = Queue(nc.tensor, s_pe), Queue(nc.scalar, s_act), Queue(nc.vector, s_dve)
            index = sb("spill_index", [P, 1], U32, spill)
            bias = sb("spill_b1", [P, H1 // P], F32, spill)
            nc.sync.dma_start(bias[:, :].unsqueeze(1), ins["ffn1_b1"][:, bass.ds(e, 1), :]).then_inc(s_bias, 16)
            index_ready = q_dve.done(nc.vector.tensor_copy(index[:, :], extra_token[:, bass.ds(i, 1)]))
            nc.gpsimd.wait_ge(*index_ready)
            nc.gpsimd.indirect_dma_start(xg[:, 0, 0, :], None, slots_dram[:, :],
                                         bass.IndirectOffsetOnAxis(ap=index[:, :], axis=0)).then_inc(s_gather, 16)
            q_pe.wait((s_gather, 16))
            for c in range(2):
                for k in range(3):
                    end = nc.tensor.transpose(psum[c][:, k * P:(k + 1) * P], xg[:, 0, 0, (3 * c + k) * P:(3 * c + k + 1) * P], ident[:, :])
                turned_now = q_pe.done(end)
                q_act.wait(turned_now)
                src = psum[c][:, 0:3 * P].rearrange("p (k n) -> p k n", k=3)
                hi = q_act.done(nc.scalar.activation(xe[0][:, 0, 3 * c:3 * c + 3, 0:P], src, ACT.Copy))
                q_dve.wait(hi, turned_now)
                x_ready = q_dve.done(nc.vector.tensor_tensor(xe[1][:, 0, 3 * c:3 * c + 3, 0:P], src,
                                                             xe[0][:, 0, 3 * c:3 * c + 3, 0:P].bitcast(F32), ALU.subtract))
            q_act.wait((s_bias, 16))
            w_read = x_ready
            for c in range(NCH):
                for n, (name, sem_w) in enumerate((("ffn1_w1", s_w0), ("ffn1_w2", s_w1))):
                    nc.sync.wait_ge(*w_read)
                    nc.sync.dma_start(raw[:, n:n + 1, :],
                                      ins[name][bass.ds(e * NCH + c, 1), :, :].rearrange("a p n -> p a n")).then_inc(sem_w, 16)
                for n, sem_w in enumerate((s_w0, s_w1)):
                    q_act.wait((sem_w, 16 * (c + 1)), w_read)
                    hi = q_act.done(nc.scalar.activation(whi[:, n, :], raw[:, n, :], ACT.Copy))
                    q_dve.wait(hi, (sem_w, 16 * (c + 1)), w_read)
                    split_done = q_dve.done(nc.vector.tensor_tensor(wlo[:, n, :], raw[:, n, :], whi[:, n, :].bitcast(F32), ALU.subtract))
                w1 = [w_[:, 0, :].rearrange("p (k n) -> p k n", k=KD) for w_ in (whi, wlo)]
                w2 = [w_[:, 1, :].rearrange("p (k n) -> p k n", k=3) for w_ in (whi, wlo)]
                q_pe.wait(split_done, x_ready)
                for m in range(3):
                    for k in range(KD):
                        end = mm3(psum[m][:, 0:P], at(w1, slice(None), k, slice(m * P, (m + 1) * P)), at(xe, slice(None), 0, k, slice(0, P)),
                                  k == 0, k == KD - 1)
                    got = q_pe.done(end)
                    q_act.wait(got, q_dve.last())
                    s_ = q_act.done(nc.scalar.activation(ht[:, 0, 0:P], psum[m][:, 0:P], ACT.Relu, bias=bias[:, 3 * c + m:3 * c + m + 1]))
                    q_act.wait(s_)
                    hi = q_act.done(nc.scalar.activation(hT[0][:, 0, m, 0:P], ht[:, 0, 0:P], ACT.Copy))
                    q_dve.wait(hi)
                    h_ready = q_dve.done(nc.vector.tensor_tensor(hT[1][:, 0, m, 0:P], ht[:, 0, 0:P], hT[0][:, 0, m, 0:P].bitcast(F32), ALU.subtract))
                q_pe.wait(h_ready)
                for half in range(2):
                    for k in range(3):
                        end = mm3(y_banks[half][:, 0:HALF], at(hT, slice(None), 0, k, slice(0, P)),
                                  at(w2, slice(None), k, slice(half * HALF, (half + 1) * HALF)),
                                  c == 0 and k == 0, c == NCH - 1 and k == 2)
                w_read = q_pe.done(end)
            q_act.wait(w_read)
            for half in range(2):
                y_kept = q_act.done(nc.scalar.activation(yt[:, 0, 0, half * HALF:(half + 1) * HALF], y_banks[half][:, 0:HALF], ACT.Copy))
            nc.sync.wait_ge(*y_kept)
            nc.sync.dma_start(extra_rows[bass.ds(i, 1), :, :].rearrange("a p d -> p a d"), yt[:, 0, 0:1, :]).then_inc(s_store, 16)
            nc.sync.wait_ge(s_store, 16)
            nc.gpsimd.wait_ge(s_gather, 16)
            nc.gpsimd.dma_reset(range(s_gather.num, s_gather.num + 1))
            nc.all_engine_barrier(sems_to_clear=range(numbers[0], numbers[0] + len(numbers)))

        with ExitStack() as spill:
            some = nc.values_load(any_overflow[0:1, 0:1], min_val=0, max_val=1)
            with nc.If(some > 0):
                with nc.Fori(0, E) as expert:
                    with nc.Fori(0, EXTRA) as extra:
                        number_ = nc.snap(expert * EXTRA + extra, min_val=0, max_val=E * EXTRA - 1)
                        used = nc.values_load(overflow[0:1, bass.ds(number_, 1)], min_val=0, max_val=1)
                        with nc.If(used > 0):
                            overflow_tile(expert, number_)
        moe_rows = token_rows

        o_sem = sem("out_stored")
        pool.wait(made["rows"], *stored)
        row_sem = [sem(f"row_back{n}") for n in range(4)]
        out_free = [None] * 4
        for t in range(TT):
            n = P if t < TT - 1 else LAST
            for k in range(2):
                i = 2 * t + k
                r = i % 4
                pool.wait(out_free[r])
                nc.gpsimd.indirect_dma_start(moe_rows[0:n, r, :], None, result_dram[:, :],
                                             bass.IndirectOffsetOnAxis(ap=slot_row[0:n, k, t:t + 1], axis=0)).then_inc(row_sem[r], 16)
                s = v(lambda: nc.vector.scalar_tensor_tensor(x[0:n, t, :], moe_rows[0:n, r, :], weights2[0:n, k, t:t + 1], x[0:n, t, :],
                                                             ALU.mult, ALU.add), (row_sem[r], 16 * (i // 4 + 1)), dve.last())
                out_free[r] = s
            sp.wait(s)
            sp.engine.dma_start(out[t * P:t * P + n, :], x[0:n, t, :]).then_inc(o_sem, 16)
        stores.append((o_sem, 16 * TT))
        sp.wait(*stores, *stored)
        moe.close()


def _columns(w, n, k=KD):
    c = w.shape[1] // n
    return w.reshape(k, P, n, c).transpose(2, 1, 0, 3).reshape(n, P, k * c)


def _rows(w, k):
    return w.reshape(-1, k, P, w.shape[1]).transpose(0, 2, 1, 3).reshape(-1, P, k * w.shape[1])


def kernel(**inputs):
    import numpy as np
    import concourse.bacc as bacc
    from concourse.bass_utils import run_bass_kernel_spmd

    i = {name: np.asarray(value) for name, value in inputs.items()}
    w_map = i["L0_mix_w_map"].T
    qkv = i["L1_mix_w_qkv"]

    def kv_chunks(w):
        k, v = _columns(w[:, D:2 * D], 2), _columns(w[:, 2 * D:], 2)
        return np.stack([k, v], 1).reshape(4, P, WC)

    arrays = {
        "x": i["x"], "src": i["src"].reshape(EP, EC), "dst": i["dst"].reshape(EP, EC),
        "gnn0_w1": _columns(i["L0_gnn_W1"], 2), "gnn0_w2": _columns(i["L0_gnn_W2"], 2),
        "gnn0_b1": i["L0_gnn_b1"].reshape(KD, P).T, "gnn0_b2": i["L0_gnn_b2"],
        "mix0_q": _columns(w_map[:, 0:D], 2), "mix0_kv": kv_chunks(w_map), "mix0_out": _rows(i["L0_mix_w_out"].T, 3),
        "mix0_gk": i["L0_mix_g_k"], "mix0_bk": i["L0_mix_b_k"], "mix0_gv": i["L0_mix_g_v"], "mix0_bv": i["L0_mix_b_v"],
        "mix0_b": i["L0_mix_b_out"],
        "ffn0_gate": i["L0_ffn_gate_w"].reshape(E, KD, P).transpose(2, 1, 0),
        "ffn0_w1": _columns(i["L0_ffn_w1"].transpose(1, 0, 2).reshape(D, E * H0), 4),
        "ffn0_b1": i["L0_ffn_b1"].reshape(KH0, P).T,
        "ffn0_w2": np.concatenate([_columns(w, 2) for w in i["L0_ffn_w2"].reshape(2, D, D)]), "ffn0_b2": i["L0_ffn_b2"],
        "gat_w1": _columns(i["L1_gnn_W1"].T, 4), "gat_as1": i["L1_gnn_att_src1"].reshape(-1),
        "gat_ad1": i["L1_gnn_att_dst1"].reshape(-1), "gat_b1": i["L1_gnn_b1"].reshape(G1, P).T,
        "gat_w2": _rows(i["L1_gnn_W2"].T, 2), "gat_as2": i["L1_gnn_att_src2"].reshape(-1),
        "gat_ad2": i["L1_gnn_att_dst2"].reshape(-1), "gat_b2": i["L1_gnn_b2"],
        "mix1_q": _columns(qkv[:, 0:D], 2), "mix1_kv": kv_chunks(qkv), "mix1_out": _rows(i["L1_mix_w_proj"], 3),
        "mix1_b": i["L1_mix_b_proj"],
        "ffn1_gate": i["L1_ffn_Wr"].reshape(E, KD, P).transpose(2, 1, 0),
        "ffn1_w1": np.concatenate([_columns(w.T, NCH) for w in i["L1_ffn_W1"]]),
        "ffn1_w2": np.concatenate([_rows(w.T, 3) for w in i["L1_ffn_W2"]]),
        "ffn1_b1": i["L1_ffn_b1"].reshape(E, H1 // P, P).transpose(2, 0, 1), "ffn1_b2": i["L1_ffn_b2"],
        "shared_w1": _columns(i["L1_ffn_sW1"].T, NCH), "shared_w2": _rows(i["L1_ffn_sW2"].T, 3),
        "shared_b1": i["L1_ffn_sb1"].reshape(H1 // P, P).T, "shared_b2": i["L1_ffn_sb2"],
    }
    nc = bacc.Bacc("TRN2", target_bir_lowering=False, num_devices=1)
    arrays = {name: np.ascontiguousarray(value) for name, value in arrays.items()}
    aps = {name: nc.dram_tensor("in_" + name, value.shape, mybir.dt.from_np(value.dtype), kind="ExternalInput").ap()
           for name, value in arrays.items()}
    out = nc.dram_tensor("out", (T, D), F32, kind="ExternalOutput").ap()
    slots = nc.dram_tensor("tokens_normed", (TP, D), F32, kind="Internal").ap()
    result = nc.dram_tensor("expert_rows", (E * TP, D), F32, kind="Internal").ap()
    build(nc, aps, out, slots, result)
    run = run_bass_kernel_spmd(nc, [{"in_" + name: value for name, value in arrays.items()}], core_ids=[0])
    return run.results[0]["out"]
```
